# Optimizing a Trainium2 kernel written in Bass

```python
import numpy as np
import jax
import jax.numpy as jnp

def _softmax(x, axis=-1):
    return jax.nn.softmax(x, axis=axis)

def _gelu(x):
    return jax.nn.gelu(x, approximate=True)

def _silu(x):
    return jax.nn.silu(x)

def _sigmoid(x):
    return jax.nn.sigmoid(x)

def _layernorm(x, axis=-1, eps=1e-05):
    m = jnp.mean(x, axis=axis, keepdims=True)
    v = jnp.var(x, axis=axis, keepdims=True)
    return (x - m) / jnp.sqrt(v + eps)

def _scatter_add(tgt, idx, src, axis=0):
    return tgt.at[idx].add(src)

def _segment_sum(src, seg, n):
    return jax.ops.segment_sum(src, seg, n)
kernel_name = 'mk_cond_seq_d4_seqx_r8_e91cf3'

def setup_inputs(seed: int=0):
    np.random.seed(seed)
    _w = jnp.asarray

    def _rec_inputs():
        import jax
        import jax.numpy as jnp
        _rk = jax.random.key(seed)
        x = -0.0002928 + 1 * jax.random.normal(jax.random.fold_in(_rk, 1), (32, 128, 128), jnp.float32)
        _lenS = 128 - jax.random.randint(jax.random.fold_in(_rk, 7), (32,), 0, max(1, 128 // 4) + 1, jnp.int32)
        _lenS2 = 128 - jax.random.randint(jax.random.fold_in(_rk, 8), (32,), 0, max(1, 128 // 4) + 1, jnp.int32)
        itok_B_6_14 = jax.random.randint(jax.random.fold_in(_rk, 11), (32,), 6, 15, jnp.int32)
        condB_dt = jax.random.uniform(jax.random.fold_in(_rk, 12), (32,), jnp.float32, 0.0, 0.981965)
        itok_B_34_63 = jax.random.randint(jax.random.fold_in(_rk, 14), (32,), 34, 64, jnp.int32)
        fside_Bx16xSxS_0 = -1.47943e-05 + 1.00017 * jax.random.normal(jax.random.fold_in(_rk, 15), (32, 16, 128, 128), jnp.float32)
        itok_B_0_15 = jax.random.randint(jax.random.fold_in(_rk, 16), (32,), 0, 16, jnp.int32)
        _validS = jnp.arange(128)[None, :] < _lenS[:, None]
        _validS2 = jnp.arange(128)[None, :] < _lenS2[:, None]
        _causal = jnp.tril(jnp.ones((128, 128), dtype=bool))
        mask_Bx1xSxS_bk0 = jnp.logical_not(jnp.broadcast_to(_validS[:, None, None, :], (32, 1, 128, 128)))
        return (x, itok_B_6_14, condB_dt, itok_B_34_63, fside_Bx16xSxS_0, itok_B_0_15, mask_Bx1xSxS_bk0)
    x, itok_B_6_14, condB_dt, itok_B_34_63, fside_Bx16xSxS_0, itok_B_0_15, mask_Bx1xSxS_bk0 = _rec_inputs()

    def _L0_cond_setup():
        import jax, jax.numpy as jnp
        import numpy as np
        D = 128
        E = 8
        FF = 512
        TOPK = 2
        S = 32
        SE = 64
        SH = 128
        B, T = (2, 256)

        def _forward(x, subject_ids, ln_g, ln_b, subj_emb, hyp_w1, hyp_b1, hyp_w2, hyp_b2, sty_w1, sty_b1, sty_w2, sty_b2, router_w, exp_w1, exp_b1, exp_w2, exp_b2):
            mu = x.mean(-1, keepdims=True)
            var = x.var(-1, keepdims=True)
            h = (x - mu) * jax.lax.rsqrt(var + 1e-05) * ln_g + ln_b
            m_t = h.mean(1, keepdims=True)
            v_t = h.var(1, keepdims=True)
            h_norm = (h - m_t) * jax.lax.rsqrt(v_t + 1e-08)
            se = subj_emb[subject_ids]
            hyp = jax.nn.relu(se @ hyp_w1 + hyp_b1) @ hyp_w2 + hyp_b2
            sty = jax.nn.relu(hyp @ sty_w1 + sty_b1) @ sty_w2 + sty_b2
            gamma, beta = jnp.split(sty, 2, axis=-1)
            gamma = jax.nn.softplus(gamma) + 1e-08
            h = h_norm * gamma[:, None, :] + beta[:, None, :]
            h_flat = h.reshape(-1, D)
            probs = jax.nn.softmax(h_flat @ router_w, axis=-1)
            gates, idx = jax.lax.top_k(probs, TOPK)
            gates = gates / gates.sum(-1, keepdims=True)
            N = h_flat.shape[0]
            combine = jnp.zeros((N, E), h_flat.dtype).at[jnp.arange(N)[:, None], idx].add(gates)
            hid = jax.nn.relu(jnp.einsum('nd,edf->nef', h_flat, exp_w1) + exp_b1)
            eout = jnp.einsum('nef,efd->ned', hid, exp_w2) + exp_b2
            y = jnp.einsum('ned,ne->nd', eout, combine)
            return x + y.reshape(x.shape)
        key = jax.random.key(seed)
        ks = jax.random.split(key, 16)
        n = lambda k, sh, s=0.02: jax.random.normal(k, sh, dtype=jnp.float32) * s
        return {'x': jax.random.normal(ks[0], (B, T, D), dtype=jnp.float32), 'subject_ids': jax.random.randint(ks[1], (B,), 0, S), 'ln_g': jnp.ones((D,), jnp.float32), 'ln_b': jnp.zeros((D,), jnp.float32), 'subj_emb': n(ks[2], (S, SE)), 'hyp_w1': n(ks[3], (SE, SH), 1.0 / np.sqrt(SE)), 'hyp_b1': jnp.zeros((SH,), jnp.float32), 'hyp_w2': n(ks[4], (SH, SH), 1.0 / np.sqrt(SH)), 'hyp_b2': jnp.zeros((SH,), jnp.float32), 'sty_w1': n(ks[5], (SH, SH // 2), 1.0 / np.sqrt(SH)), 'sty_b1': jnp.zeros((SH // 2,), jnp.float32), 'sty_w2': n(ks[6], (SH // 2, 2 * D), 1.0 / np.sqrt(SH // 2)), 'sty_b2': jnp.zeros((2 * D,), jnp.float32), 'router_w': n(ks[7], (D, E), 1.0 / np.sqrt(D)), 'exp_w1': n(ks[8], (E, D, FF), 1.0 / np.sqrt(D)), 'exp_b1': jnp.zeros((E, FF), jnp.float32), 'exp_w2': n(ks[9], (E, FF, D), 1.0 / np.sqrt(FF)), 'exp_b2': jnp.zeros((E, D), jnp.float32)}
    _L0_cond_all = _L0_cond_setup()
    _L0_cond_in = {k: v for k, v in _L0_cond_all.items() if k in ('ln_g', 'ln_b', 'subj_emb', 'hyp_w1', 'hyp_b1', 'hyp_w2', 'hyp_b2', 'sty_w1', 'sty_b1', 'sty_w2', 'sty_b2', 'router_w', 'exp_w1', 'exp_b1', 'exp_w2', 'exp_b2')}
    del _L0_cond_all

    def _L1_cond_setup():
        import jax, jax.numpy as jnp
        import numpy as np
        B, NX, NY = (16, 128, 128)

        def _grad(f, axis):
            fm = jnp.moveaxis(f, axis, -1)
            g = (jnp.roll(fm, -1, -1) - jnp.roll(fm, 1, -1)) * 0.5
            g0 = (-3.0 * fm[..., 0] + 4.0 * fm[..., 1] - fm[..., 2]) * 0.5
            gN = (3.0 * fm[..., -1] - 4.0 * fm[..., -2] + fm[..., -3]) * 0.5
            g = g.at[..., 0].set(g0).at[..., -1].set(gN)
            return jnp.moveaxis(g, -1, axis)

        def _grad2(f, axis):
            fm = jnp.moveaxis(f, axis, -1)
            g = jnp.roll(fm, -1, -1) - 2.0 * fm + jnp.roll(fm, 1, -1)
            g0 = 2.0 * fm[..., 0] - 5.0 * fm[..., 1] + 4.0 * fm[..., 2] - fm[..., 3]
            gN = 2.0 * fm[..., -1] - 5.0 * fm[..., -2] + 4.0 * fm[..., -3] - fm[..., -4]
            g = g.at[..., 0].set(g0).at[..., -1].set(gN)
            return jnp.moveaxis(g, -1, axis)
        key = jax.random.key(seed)
        k1, k2, k3, k4 = jax.random.split(key, 4)
        f = jax.random.uniform(k1, (B, NX, NY), dtype=jnp.float32)
        A_grid = jax.random.normal(k2, (2, NX, NY), dtype=jnp.float32)
        B_grid = jax.random.uniform(k3, (3, NX, NY), dtype=jnp.float32)
        dt = jax.random.uniform(k4, (B,), dtype=jnp.float32)
        return {'f': f, 'A_grid': A_grid, 'B_grid': B_grid, 'dt': dt}
    _L1_cond_all = _L1_cond_setup()
    _L1_cond_in = {k: v for k, v in _L1_cond_all.items() if k in ('A_grid', 'B_grid')}
    del _L1_cond_all

    def _L2_cond_setup():
        import jax, jax.numpy as jnp
        import numpy as np
        import math
        D_MODEL = 128
        N_HEAD = 16
        HEAD_DIM = D_MODEL // N_HEAD
        D_FF = 512
        NUM_STEPS = 100.0
        RESCALE = 4000.0
        EPS = 1e-05

        def _sin_emb(t):
            half = D_MODEL // 2
            x = t.astype(jnp.float32) / NUM_STEPS * RESCALE
            freqs = jnp.exp(jnp.arange(half, dtype=jnp.float32) * (-math.log(10000.0) / (half - 1)))
            e = x[:, None] * freqs[None, :]
            return jnp.concatenate([jnp.sin(e), jnp.cos(e)], axis=-1)

        def _ln(x):
            m = jnp.mean(x, axis=-1, keepdims=True)
            v = jnp.var(x, axis=-1, keepdims=True)
            return (x - m) / jnp.sqrt(v + EPS)

        def _gelu2(x):
            return x * jax.nn.sigmoid(1.702 * x)
        key = jax.random.key(seed)
        ks = jax.random.split(key, 24)
        B, S, D, F = (4, 64, D_MODEL, D_FF)
        std = 0.02
        inp = {'src': jax.random.normal(ks[0], (B, S, D), dtype=jnp.float32), 'src_mask': jax.random.randint(ks[1], (B, 1, S, S), 0, 2).astype(bool), 'timestep': jax.random.randint(ks[2], (B,), 0, 100, dtype=jnp.int32), 'attention_bias': jax.random.normal(ks[3], (B, N_HEAD, S, S), dtype=jnp.float32), 'W_ada': jax.random.normal(ks[4], (D, 2 * D), dtype=jnp.float32) * std, 'b_ada': jnp.zeros((2 * D,), dtype=jnp.float32), 'Wq': jax.random.normal(ks[5], (D, D), dtype=jnp.float32) * std, 'bq': jnp.zeros((D,), dtype=jnp.float32), 'Wk': jax.random.normal(ks[6], (D, D), dtype=jnp.float32) * std, 'bk': jnp.zeros((D,), dtype=jnp.float32), 'Wv': jax.random.normal(ks[7], (D, D), dtype=jnp.float32) * std, 'bv': jnp.zeros((D,), dtype=jnp.float32), 'Wo': jax.random.normal(ks[8], (D, D), dtype=jnp.float32) * std, 'bo': jnp.zeros((D,), dtype=jnp.float32), 'W1': jax.random.normal(ks[9], (D, F), dtype=jnp.float32) * std, 'b1': jnp.zeros((F,), dtype=jnp.float32), 'W2': jax.random.normal(ks[10], (F, D), dtype=jnp.float32) * std, 'b2': jnp.zeros((D,), dtype=jnp.float32), 'g2': jnp.ones((D,), dtype=jnp.float32), 'beta2': jnp.zeros((D,), dtype=jnp.float32)}
        return inp
    _L2_cond_all = _L2_cond_setup()
    _L2_cond_in = {k: v for k, v in _L2_cond_all.items() if k in ('W_ada', 'b_ada', 'Wq', 'bq', 'Wk', 'bk', 'Wv', 'bv', 'Wo', 'bo', 'W1', 'b1', 'W2', 'b2', 'g2', 'beta2')}
    del _L2_cond_all

    def _L3_cond_setup():
        import jax, jax.numpy as jnp
        import numpy as np
        B, S, D = (32, 128, 128)
        A = 32
        E = 16
        LN_EPS = 1e-05
        key = jax.random.key(seed)
        ks = jax.random.split(key, 10)
        s = lambda fan_in: 1.0 / np.sqrt(fan_in)
        return {'hidden_states': jax.random.normal(ks[0], (B, S, D), dtype=jnp.float32), 'domain_id': jax.random.randint(ks[1], (B,), 0, E, dtype=jnp.int64), 'down_W': jax.random.uniform(ks[2], (A, D), jnp.float32, -s(D), s(D)), 'down_b': jax.random.uniform(ks[3], (A,), jnp.float32, -s(D), s(D)), 'up_W': jax.random.uniform(ks[4], (D, A), jnp.float32, -s(A), s(A)), 'up_b': jax.random.uniform(ks[5], (D,), jnp.float32, -s(A), s(A)), 'expert_W': jax.random.uniform(ks[6], (E, A, A), jnp.float32, -s(A), s(A)), 'expert_b': jax.random.uniform(ks[7], (E, A), jnp.float32, -s(A), s(A)), 'domain_emb': jax.random.normal(ks[8], (E, A), dtype=jnp.float32), 'ln_gamma': jnp.ones((D,), jnp.float32), 'ln_beta': jnp.zeros((D,), jnp.float32)}
    _L3_cond_all = _L3_cond_setup()
    _L3_cond_in = {k: v for k, v in _L3_cond_all.items() if k in ('down_W', 'down_b', 'up_W', 'up_b', 'expert_W', 'expert_b', 'domain_emb', 'ln_gamma', 'ln_beta')}
    del _L3_cond_all
    return {'x': x, 'itok_B_6_14': itok_B_6_14, 'condB_dt': condB_dt, 'itok_B_34_63': itok_B_34_63, 'fside_Bx16xSxS_0': fside_Bx16xSxS_0, 'itok_B_0_15': itok_B_0_15, 'mask_Bx1xSxS_bk0': mask_Bx1xSxS_bk0, 'L0_cond_ln_g': _L0_cond_in['ln_g'], 'L0_cond_ln_b': _L0_cond_in['ln_b'], 'L0_cond_subj_emb': _L0_cond_in['subj_emb'], 'L0_cond_hyp_w1': _L0_cond_in['hyp_w1'], 'L0_cond_hyp_b1': _L0_cond_in['hyp_b1'], 'L0_cond_hyp_w2': _L0_cond_in['hyp_w2'], 'L0_cond_hyp_b2': _L0_cond_in['hyp_b2'], 'L0_cond_sty_w1': _L0_cond_in['sty_w1'], 'L0_cond_sty_b1': _L0_cond_in['sty_b1'], 'L0_cond_sty_w2': _L0_cond_in['sty_w2'], 'L0_cond_sty_b2': _L0_cond_in['sty_b2'], 'L0_cond_router_w': _L0_cond_in['router_w'], 'L0_cond_exp_w1': _L0_cond_in['exp_w1'], 'L0_cond_exp_b1': _L0_cond_in['exp_b1'], 'L0_cond_exp_w2': _L0_cond_in['exp_w2'], 'L0_cond_exp_b2': _L0_cond_in['exp_b2'], 'L1_cond_A_grid': _L1_cond_in['A_grid'], 'L1_cond_B_grid': _L1_cond_in['B_grid'], 'L2_cond_W_ada': _L2_cond_in['W_ada'], 'L2_cond_b_ada': _L2_cond_in['b_ada'], 'L2_cond_Wq': _L2_cond_in['Wq'], 'L2_cond_bq': _L2_cond_in['bq'], 'L2_cond_Wk': _L2_cond_in['Wk'], 'L2_cond_bk': _L2_cond_in['bk'], 'L2_cond_Wv': _L2_cond_in['Wv'], 'L2_cond_bv': _L2_cond_in['bv'], 'L2_cond_Wo': _L2_cond_in['Wo'], 'L2_cond_bo': _L2_cond_in['bo'], 'L2_cond_W1': _L2_cond_in['W1'], 'L2_cond_b1': _L2_cond_in['b1'], 'L2_cond_W2': _L2_cond_in['W2'], 'L2_cond_b2': _L2_cond_in['b2'], 'L2_cond_g2': _L2_cond_in['g2'], 'L2_cond_beta2': _L2_cond_in['beta2'], 'L3_cond_down_W': _L3_cond_in['down_W'], 'L3_cond_down_b': _L3_cond_in['down_b'], 'L3_cond_up_W': _L3_cond_in['up_W'], 'L3_cond_up_b': _L3_cond_in['up_b'], 'L3_cond_expert_W': _L3_cond_in['expert_W'], 'L3_cond_expert_b': _L3_cond_in['expert_b'], 'L3_cond_domain_emb': _L3_cond_in['domain_emb'], 'L3_cond_ln_gamma': _L3_cond_in['ln_gamma'], 'L3_cond_ln_beta': _L3_cond_in['ln_beta']}

def reference(x, itok_B_6_14, condB_dt, itok_B_34_63, fside_Bx16xSxS_0, itok_B_0_15, mask_Bx1xSxS_bk0, L0_cond_ln_g, L0_cond_ln_b, L0_cond_subj_emb, L0_cond_hyp_w1, L0_cond_hyp_b1, L0_cond_hyp_w2, L0_cond_hyp_b2, L0_cond_sty_w1, L0_cond_sty_b1, L0_cond_sty_w2, L0_cond_sty_b2, L0_cond_router_w, L0_cond_exp_w1, L0_cond_exp_b1, L0_cond_exp_w2, L0_cond_exp_b2, L1_cond_A_grid, L1_cond_B_grid, L2_cond_W_ada, L2_cond_b_ada, L2_cond_Wq, L2_cond_bq, L2_cond_Wk, L2_cond_bk, L2_cond_Wv, L2_cond_bv, L2_cond_Wo, L2_cond_bo, L2_cond_W1, L2_cond_b1, L2_cond_W2, L2_cond_b2, L2_cond_g2, L2_cond_beta2, L3_cond_down_W, L3_cond_down_b, L3_cond_up_W, L3_cond_up_b, L3_cond_expert_W, L3_cond_expert_b, L3_cond_domain_emb, L3_cond_ln_gamma, L3_cond_ln_beta):
    import jax
    import jax.numpy as jnp

    def _L0_cond_ref(x, subject_ids, ln_g, ln_b, subj_emb, hyp_w1, hyp_b1, hyp_w2, hyp_b2, sty_w1, sty_b1, sty_w2, sty_b2, router_w, exp_w1, exp_b1, exp_w2, exp_b2):
        import jax, jax.numpy as jnp
        import numpy as np
        D = 128
        E = 8
        FF = 512
        TOPK = 2
        S = 32
        SE = 64
        SH = 128
        B, T = (2, 256)

        def _forward(x, subject_ids, ln_g, ln_b, subj_emb, hyp_w1, hyp_b1, hyp_w2, hyp_b2, sty_w1, sty_b1, sty_w2, sty_b2, router_w, exp_w1, exp_b1, exp_w2, exp_b2):
            mu = x.mean(-1, keepdims=True)
            var = x.var(-1, keepdims=True)
            h = (x - mu) * jax.lax.rsqrt(var + 1e-05) * ln_g + ln_b
            m_t = h.mean(1, keepdims=True)
            v_t = h.var(1, keepdims=True)
            h_norm = (h - m_t) * jax.lax.rsqrt(v_t + 1e-08)
            se = subj_emb[subject_ids]
            hyp = jax.nn.relu(se @ hyp_w1 + hyp_b1) @ hyp_w2 + hyp_b2
            sty = jax.nn.relu(hyp @ sty_w1 + sty_b1) @ sty_w2 + sty_b2
            gamma, beta = jnp.split(sty, 2, axis=-1)
            gamma = jax.nn.softplus(gamma) + 1e-08
            h = h_norm * gamma[:, None, :] + beta[:, None, :]
            h_flat = h.reshape(-1, D)
            probs = jax.nn.softmax(h_flat @ router_w, axis=-1)
            gates, idx = jax.lax.top_k(probs, TOPK)
            gates = gates / gates.sum(-1, keepdims=True)
            N = h_flat.shape[0]
            combine = jnp.zeros((N, E), h_flat.dtype).at[jnp.arange(N)[:, None], idx].add(gates)
            hid = jax.nn.relu(jnp.einsum('nd,edf->nef', h_flat, exp_w1) + exp_b1)
            eout = jnp.einsum('nef,efd->ned', hid, exp_w2) + exp_b2
            y = jnp.einsum('ned,ne->nd', eout, combine)
            return x + y.reshape(x.shape)
        return _forward(x, subject_ids, ln_g, ln_b, subj_emb, hyp_w1, hyp_b1, hyp_w2, hyp_b2, sty_w1, sty_b1, sty_w2, sty_b2, router_w, exp_w1, exp_b1, exp_w2, exp_b2)

    def _L1_cond_ref(f, A_grid, B_grid, dt):
        import jax, jax.numpy as jnp
        import numpy as np
        B, NX, NY = (16, 128, 128)

        def _grad(f, axis):
            fm = jnp.moveaxis(f, axis, -1)
            g = (jnp.roll(fm, -1, -1) - jnp.roll(fm, 1, -1)) * 0.5
            g0 = (-3.0 * fm[..., 0] + 4.0 * fm[..., 1] - fm[..., 2]) * 0.5
            gN = (3.0 * fm[..., -1] - 4.0 * fm[..., -2] + fm[..., -3]) * 0.5
            g = g.at[..., 0].set(g0).at[..., -1].set(gN)
            return jnp.moveaxis(g, -1, axis)

        def _grad2(f, axis):
            fm = jnp.moveaxis(f, axis, -1)
            g = jnp.roll(fm, -1, -1) - 2.0 * fm + jnp.roll(fm, 1, -1)
            g0 = 2.0 * fm[..., 0] - 5.0 * fm[..., 1] + 4.0 * fm[..., 2] - fm[..., 3]
            gN = 2.0 * fm[..., -1] - 5.0 * fm[..., -2] + 4.0 * fm[..., -3] - fm[..., -4]
            g = g.at[..., 0].set(g0).at[..., -1].set(gN)
            return jnp.moveaxis(g, -1, axis)
        Af = A_grid[None] * f[:, None]
        Bf = B_grid[None] * f[:, None]
        gradv_Af = _grad(Af[:, 0], 1) + _grad(Af[:, 1], 2)
        gradvv_Bf = _grad2(Bf[:, 0], 1) + _grad2(Bf[:, 1], 2) + _grad(_grad(Bf[:, 2], 2), 1) + _grad(_grad(Bf[:, 2], 1), 2)
        df = -gradv_Af + gradvv_Bf * 0.5
        f_new = f + df * dt[:, None, None]
        return jnp.maximum(f_new, 0.0)

    def _L2_cond_ref(src, src_mask, timestep, attention_bias, W_ada, b_ada, Wq, bq, Wk, bk, Wv, bv, Wo, bo, W1, b1, W2, b2, g2, beta2):
        import jax, jax.numpy as jnp
        import numpy as np
        import math
        D_MODEL = 128
        N_HEAD = 16
        HEAD_DIM = D_MODEL // N_HEAD
        D_FF = 512
        NUM_STEPS = 100.0
        RESCALE = 4000.0
        EPS = 1e-05

        def _sin_emb(t):
            half = D_MODEL // 2
            x = t.astype(jnp.float32) / NUM_STEPS * RESCALE
            freqs = jnp.exp(jnp.arange(half, dtype=jnp.float32) * (-math.log(10000.0) / (half - 1)))
            e = x[:, None] * freqs[None, :]
            return jnp.concatenate([jnp.sin(e), jnp.cos(e)], axis=-1)

        def _ln(x):
            m = jnp.mean(x, axis=-1, keepdims=True)
            v = jnp.var(x, axis=-1, keepdims=True)
            return (x - m) / jnp.sqrt(v + EPS)

        def _gelu2(x):
            return x * jax.nn.sigmoid(1.702 * x)
        B, S, D = src.shape
        emb = jax.nn.silu(_sin_emb(timestep)) @ W_ada + b_ada
        scale, shift = jnp.split(emb[:, None, :], 2, axis=-1)
        x = _ln(src) * (1.0 + scale) + shift
        q = (x @ Wq + bq).reshape(B, S, N_HEAD, HEAD_DIM).transpose(0, 2, 1, 3)
        k = (x @ Wk + bk).reshape(B, S, N_HEAD, HEAD_DIM).transpose(0, 2, 1, 3)
        v = (x @ Wv + bv).reshape(B, S, N_HEAD, HEAD_DIM).transpose(0, 2, 1, 3)
        scores = jnp.einsum('bhqd,bhkd->bhqk', q / math.sqrt(HEAD_DIM), k)
        scores = scores + attention_bias
        scores = jnp.where(src_mask, -jnp.inf, scores.astype(jnp.float32))
        probs = jax.nn.softmax(scores, axis=-1).astype(v.dtype)
        ctx = jnp.einsum('bhqk,bhkd->bhqd', probs, v)
        ctx = ctx.transpose(0, 2, 1, 3).reshape(B, S, D)
        x = x + (ctx @ Wo + bo)
        h = _ln(x) * g2 + beta2
        ff = _gelu2(h @ W1 + b1) @ W2 + b2
        return x + ff

    def _L3_cond_ref(hidden_states, domain_id, down_W, down_b, up_W, up_b, expert_W, expert_b, domain_emb, ln_gamma, ln_beta):
        import jax, jax.numpy as jnp
        import numpy as np
        B, S, D = (32, 128, 128)
        A = 32
        E = 16
        LN_EPS = 1e-05
        residual = hidden_states
        hidden = jnp.einsum('bsd,ad->bsa', hidden_states, down_W) + down_b
        hidden = jax.nn.gelu(hidden, approximate=False)
        valid = (domain_id >= 0) & (domain_id < E)
        idx = jnp.clip(domain_id, 0, E - 1)
        Wsel = expert_W[idx]
        bsel = expert_b[idx]
        expert_out = jnp.einsum('bsa,boa->bso', hidden, Wsel) + bsel[:, None, :]
        domain_output = jnp.where(valid[:, None, None], expert_out, hidden)
        hidden = domain_output + domain_emb[idx][:, None, :]
        hidden = jnp.einsum('bsa,da->bsd', hidden, up_W) + up_b
        x = hidden + residual
        mu = jnp.mean(x, axis=-1, keepdims=True)
        var = jnp.mean(jnp.square(x - mu), axis=-1, keepdims=True)
        return (x - mu) * jax.lax.rsqrt(var + LN_EPS) * ln_gamma + ln_beta
    x = _L0_cond_ref(x, itok_B_6_14, L0_cond_ln_g, L0_cond_ln_b, L0_cond_subj_emb, L0_cond_hyp_w1, L0_cond_hyp_b1, L0_cond_hyp_w2, L0_cond_hyp_b2, L0_cond_sty_w1, L0_cond_sty_b1, L0_cond_sty_w2, L0_cond_sty_b2, L0_cond_router_w, L0_cond_exp_w1, L0_cond_exp_b1, L0_cond_exp_w2, L0_cond_exp_b2)
    x = _L1_cond_ref(x, L1_cond_A_grid, L1_cond_B_grid, condB_dt)
    x = _L2_cond_ref(x, mask_Bx1xSxS_bk0, itok_B_34_63, fside_Bx16xSxS_0, L2_cond_W_ada, L2_cond_b_ada, L2_cond_Wq, L2_cond_bq, L2_cond_Wk, L2_cond_bk, L2_cond_Wv, L2_cond_bv, L2_cond_Wo, L2_cond_bo, L2_cond_W1, L2_cond_b1, L2_cond_W2, L2_cond_b2, L2_cond_g2, L2_cond_beta2)
    x = _L3_cond_ref(x, itok_B_0_15, L3_cond_down_W, L3_cond_down_b, L3_cond_up_W, L3_cond_up_b, L3_cond_expert_W, L3_cond_expert_b, L3_cond_domain_emb, L3_cond_ln_gamma, L3_cond_ln_beta)
    return x

_drawn_inputs = setup_inputs


def setup_inputs(seed=0):
    import zlib

    import numpy as np

    out = dict(_drawn_inputs(seed))
    spreads = {'L0_cond_ln_g': (1.0, 0.6),
     'L0_cond_ln_b': (0.0, 0.8),
     'L0_cond_hyp_b1': (0.0, 0.1),
     'L0_cond_hyp_b2': (0.0, 0.1),
     'L0_cond_sty_b1': (0.0, 0.1),
     'L0_cond_sty_b2': (0.0, 0.1),
     'L0_cond_exp_b1': (0.0, 0.1),
     'L0_cond_exp_b2': (0.0, 0.1),
     'L2_cond_b_ada': (0.0, 0.1),
     'L2_cond_bq': (0.0, 0.8),
     'L2_cond_bk': (0.0, 0.8),
     'L2_cond_bv': (0.0, 0.49),
     'L2_cond_bo': (0.0, 0.1),
     'L2_cond_b1': (0.0, 0.369),
     'L2_cond_b2': (0.0, 0.1),
     'L2_cond_g2': (1.0, 0.6),
     'L2_cond_beta2': (0.0, 0.8),
     'L3_cond_ln_gamma': (1.0, 0.2),
     'L3_cond_ln_beta': (0.0, 0.1)}
    factors = {'fside_Bx16xSxS_0': 8.0,
     'L2_cond_Wq': 8.0,
     'L2_cond_Wk': 8.0,
     'L2_cond_Wv': 5.653,
     'L2_cond_Wo': 3.099,
     'L3_cond_down_b': 5.79}
    for name, (base, spread) in spreads.items():
        noise = np.random.default_rng([zlib.crc32(name.encode()), seed]).standard_normal(out[name].shape)
        drawn = base * np.exp(spread * noise) if base else spread * noise
        out[name] = jnp.asarray(drawn.astype(out[name].dtype))
    for name, factor in factors.items():
        out[name] = (out[name] * factor).astype(out[name].dtype)
    return out
```

```python
import math
from contextlib import ExitStack

import numpy as np
import concourse.bass as bass
from concourse import mybir

ALU = mybir.AluOpType
ACT = mybir.ActivationFunctionType
F32 = mybir.dt.float32
BF16 = mybir.dt.bfloat16
I32 = mybir.dt.int32
U32 = mybir.dt.uint32
U8 = mybir.dt.uint8
AX_X = mybir.AxisListType.X

B, S, D = 32, 128, 128
G = 4
NG = B // G
N = G * S
E, FF = 8, 512
FC = FF // 128
H, HD = 16, 8
HQ = 4
A, ED = 32, 16
SE, SH = 64, 128
MASKED = -1e30
TWO_PI = 2.0 * math.pi
ROUND = 12582912.0
PI_HI = 6.28125
PI_MID = 0.0019340515136718750
PI_LO = TWO_PI - PI_HI - PI_MID

COLS = {}
for _name, _width in (("ln_g", 1), ("ln_b", 1), ("hyp_b1", 1), ("hyp_b2", 1), ("sty_b1", 1), ("gamma_b", 1),
                      ("beta_b", 1), ("scale_b", 1), ("shift_b", 1), ("bq", 1), ("bk", 1), ("bo", 1), ("g2", 1),
                      ("beta2", 1), ("down_b", 1), ("ff_b1", FC), ("exp_b1", E * FC), ("head", H), ("freq", 1),
                      ("turn", 1), ("row", 1), ("count", ED)):
    COLS[_name] = (sum(w for _, w in COLS.values()), _width)
NCOL = sum(w for _, w in COLS.values())

MATS = {}
for _name, _width in (("ident", 128), ("gradT", 128), ("ngradT", 128), ("hgrad2T", 128), ("A0", 128), ("B0", 128),
                      ("A1T", 128), ("B1T", 128), ("B2T", 128), ("subj", SE), ("hyp_w1", SH), ("hyp_w2", SH),
                      ("sty_w1", SH // 2), ("sty_w2", 2 * D), ("W_ada", 2 * D), ("router", E), ("Wq", D), ("Wk", D),
                      ("Wv", D), ("Wo", D), ("W1", FF), ("W2", FC * D), ("downT", A), ("upT", D), ("expert_b", A),
                      ("domain_emb", A), ("exp_b2", D)):
    MATS[_name] = (sum(w for _, w in MATS.values()), _width)
NMAT = sum(w for _, w in MATS.values())


VEC_A = 15
VEC_B = 11


class Signal:

    def __init__(self, sem, per, ahead=1):
        self.sem, self.per, self.ahead = sem, per, ahead

    def need(self, eng, g, k):
        eng.wait_ge(self.sem, g * self.per + (k + self.ahead))


def build(nc, t, out):
    with ExitStack() as ctx:
        def sb(name, shape, dt=F32):
            return ctx.enter_context(nc.sbuf_tensor(name, shape, dt))

        def sem(name):
            return ctx.enter_context(nc.semaphore(name))

        banks = [ctx.enter_context(nc.psum_tensor(f"bank{i}", [128, 512], F32)) for i in range(8)]

        def bank4(i):
            return banks[i][:, :].rearrange("p (b n) -> p b n", b=G)

        cols = sb("cols", [128, NCOL])
        mats = sb("mats", [128, NMAT])
        moe_w = sb("moe_w", [128, 2 * E * FF])
        w1 = moe_w[:, 0:E * FF].rearrange("p (e f) -> p e f", e=E)
        w2 = moe_w[:, E * FF:].rearrange("p (e c d) -> p e c d", e=E, c=FC)
        kh = moe_w[:, 0:H * N].rearrange("p (h b s) -> p h b s", h=H, b=G)
        xall = sb("xall", [128, B, D])
        rows = sb("rows", [128, 4, D])
        ids = sb("ids", [128, 3, B], I32)
        dt_row = sb("dt_row", [128, B])
        mask_u8 = sb("mask_u8", [128, B, S], U8)
        ident_bf = sb("ident_bf", [128, 128], BF16)
        minus_half = sb("minus_half", [128, G])
        expert_T = sb("expert_T", [A, ED, A])

        def col(name, k=0):
            c = COLS[name][0] + k
            return cols[:, c:c + 1]

        def mat(name, k=None, p=128):
            c, w = MATS[name]
            if k is not None:
                c, w = c + 128 * k, 128
            return mats[0:p, c:c + w]

        idf = sb("idf", [128, 3, B])
        onehot = sb("onehot", [128, 2, B])
        valid = sb("valid", [128, B])
        seT = sb("seT", [SE, B])
        hyp1T = sb("hyp1T", [SH, B])
        hyp2T = sb("hyp2T", [SH, B])
        sty1T = sb("sty1T", [SH // 2, B])
        gamT = sb("gamT", [128, B])
        betT = sb("betT", [128, B])
        sp = sb("sp", [128, 4, B])
        ang = sb("ang", [128, 6, B])
        scaleT = sb("scaleT", [128, B])
        shiftT = sb("shiftT", [128, B])
        onehot_ed = sb("onehot_ed", [A, ED, B])
        onehot_v = sb("onehot_v", [ED, B])
        invalid = sb("invalid", [A, B])
        wsel = sb("wsel", [A, B, A])
        wtmp = sb("wtmp", [A, B, A])
        esel = sb("esel", [A, B])

        st0 = sb("st0", [128, G, 6])
        mv0 = sb("mv0", [128, G, 2])
        ve0 = sb("ve0", [128, G])
        rs0 = sb("rs0", [128, G])
        xn0 = sb("xn0", [128, G, D])
        hT = sb("hT", [128, G, S])
        st1 = sb("st1", [128, G, 6])
        mv1 = sb("mv1", [128, G, 2])
        ve1 = sb("ve1", [128, G])
        rs1 = sb("rs1", [128, G])
        amp = sb("amp", [128, G])
        off = sb("off", [128, G])
        hs = sb("hs", [128, G, S])
        lg = sb("lg", [128, G, E])
        top = sb("top", [128, G, 8])
        topi = sb("topi", [128, G, 8], U32)
        topf = sb("topf", [128, G, 8])
        sel = sb("sel", [128, 2, G, E])
        lge = sb("lge", [128, G, E])
        gate = sb("gate", [128, G, E])
        gsum = sb("gsum", [128, G])
        grec = sb("grec", [128, G])
        gateT = sb("gateT", [E, G, S])
        hid = sb("hid", [128, 2, FC, N])
        hid2 = hid[:, 0, :, :]
        pT = hid[:, 1, :, :].rearrange("p c (h q) -> p (c h) q", q=S)

        f0 = sb("f0", [128, G, D])
        a0f = sb("a0f", [128, G, D])
        b0f = sb("b0f", [128, G, D])
        a1fT = sb("a1fT", [128, G, S])
        b1fT = sb("b1fT", [128, G, S])
        b2fT = sb("b2fT", [128, G, S])
        mix = sb("mix", [128, G, D])
        f1 = sb("f1", [128, G, D])
        dtc = sb("dtc", [128, G])
        adac = sb("adac", [128, 2, G])

        st2 = sb("st2", [128, G, 6])
        mv2 = sb("mv2", [128, G, 2])
        ve2 = sb("ve2", [128, G])
        rs2 = sb("rs2", [128, G])
        xn2 = sb("xn2", [128, G, D])
        xT = sb("xT", [128, G, S])
        xbT = sb("xbT", [128, G, S])
        qT = sb("qT", [128, G, S])
        kT = sb("kT", [128, G, S])
        vh = sb("vh", [128, G, H, HD + 1])
        bias = sb("bias", [128, 2, H, S])
        sc = sb("sc", [128, 2, H, S])
        mx = sb("mx", [128, 2, H])
        rec = sb("rec", [128, H])
        cx = sb("cx", [128, H, HD])
        cxT = sb("cxT", [128, G, S])
        x2 = sb("x2", [128, G, D])
        x2b = sb("x2b", [128, G, D])
        st3 = sb("st3", [128, G, 6])
        mv3 = sb("mv3", [128, G, 2])
        ve3 = sb("ve3", [128, G])
        rs3 = sb("rs3", [128, G])
        xn3 = sb("xn3", [128, G, D])
        h2T = sb("h2T", [128, N])

        x3 = sb("x3", [128, G, D])
        x3T = sb("x3T", [128, N])
        hd = sb("hd", [A, G, S])
        wc = sb("wc", [A, G, A])
        ec = sb("ec", [A, G])
        h3 = sb("h3", [A + 1, G, S])
        x4 = sb("x4", [128, G, D])
        st4 = sb("st4", [128, G, 6])
        mv4 = sb("mv4", [128, G, 2])
        ve4 = sb("ve4", [128, G])
        rs4 = sb("rs4", [128, G])
        xn4 = sb("xn4", [128, G, D])
        xg = sb("xg", [128, G, D])
        xo = sb("xo", [128, G, D])
        mask_c = sb("mask_c", [128, G, S], BF16)

        in_small, in_w1, in_w2, in_mask = sem("in_small"), sem("in_w1"), sem("in_w2"), sem("in_mask")
        in_x = [sem(f"in_x{g}") for g in range(NG)]
        out_done = sem("out_done")
        in_bias = [sem(f"in_bias{i}") for i in range(2)]
        once = {n: sem("s_" + n) for n in (
            "ids", "pool_const", "onehot", "se", "seT", "hyp1", "hyp1T", "hyp2", "hyp2T", "sty1", "sty1T", "sty2",
            "gam_raw", "gam_exp", "gam_abs", "gam_ln", "gamT", "ang", "sin", "silu_e", "silu", "ada", "adaT", "consts",
            "esel", "eselT", "wsel", "sty_copied", "onehot_ed")}
        dve_chain = sem("dve_chain")
        pool_chain = sem("pool_chain")

        sig, owned = {}, {}

        def signals(owner, per, names, ahead=1):
            for n in names.split():
                sig[n] = Signal(sem(n), per, ahead)
                owned.setdefault(owner, []).append(sig[n])

        signals("dve", 1, "a_var a_xn a_var1 a_hs a_lg a_lge a_gate a_gateT a_b2x")
        signals("pool", 1, "a_rstd a_rstd1")
        signals("act", 1, "a_hT a_exp")
        signals("pe", 1, "a_xnT a_logit a_gT a_b2")
        signals("pe", E * FC, "a_hid_mm", ahead=2)
        signals("act", E * FC, "a_hid", ahead=2)
        signals("pe", E, "a_y_mm", ahead=2)
        signals("dve", E, "a_y", ahead=2)
        signals("dve", 1, "b_prodT b_mix b_f1 b_var2 b_xn2 b_xT b_qT b_kh b_vh b_var3 b_xn3 b_x3 b_wc b_h3 b_x4 b_var4 b_xn4")
        signals("pool", 1, "b_a0f b_b0f b_xbT b_rstd2 b_rstd3 b_x2b b_rstd4 b_xg b_xo")
        signals("act", 1, "b_f0 b_kT b_x2 b_h2T b_x3T b_hd")
        signals("pe", 1, "b_f0T b_t1 b_df b_xn2T b_q_mm b_k_mm b_v_mm b_x2_mm b_xn3T b_ff_mm b_x3T_mm b_down_mm b_exp_mm b_up_mm")
        signals("pe", FC, "b_ff1_mm")
        signals("act", FC, "b_hid2")
        signals("dve", G, "c_sc c_mx c_cx", ahead=3)
        signals("pool", G, "c_sub", ahead=3)
        signals("act", G, "c_exp c_cxT", ahead=3)
        signals("pe", G, "c_s_mm c_ctx_mm c_cxT_mm", ahead=3)
        signals("pe", G * (H // HQ), "c_pT_mm", ahead=4)
        signals("act", G * (H // HQ), "c_pT", ahead=4)
        signals("dve", VEC_A, "vec_a")
        signals("dve", VEC_B, "vec_b")

        def need(eng, name, g, k=1):
            sig[name].need(eng, g, k)

        def did(ins, name):
            ins.then_inc(sig[name].sem, 1)

        def start(eng, owner):
            for s in owned[owner]:
                eng.sem_inc(s.sem, s.ahead)

        QB = H // HQ

        def grp(ap, g):
            return ap[:, bass.ds(g * G, G)]

        block = ctx.enter_context(nc.Block())

        @block.sync
        def _(sync):
            sync.dma_start(cols[:, :], t["cols"]).then_inc(in_small, 16)
            sync.dma_start(mats[:, :], t["mats"]).then_inc(in_small, 16)
            sync.dma_start(ids[:, :, :].rearrange("p a b -> p (a b)"), t["ids"].partition_broadcast(128)).then_inc(in_small, 16)
            sync.dma_start(dt_row[:, :], t["dt"].partition_broadcast(128)).then_inc(in_small, 16)
            sync.dma_start(rows[:, :, :].rearrange("p a b -> p (a b)"), t["rows"].partition_broadcast(128)).then_inc(in_small, 16)
            sync.dma_start(expert_T[:, :, :], t["expert_T"]).then_inc(in_small, 16)
            for g in range(NG):
                sync.dma_start(xall[:, G * g:G * g + G, :],
                               t["x"][G * g:G * g + G].rearrange("b s d -> s b d")).then_inc(in_x[g], 16)
                if g == 0:
                    sync.dma_start(w1[:, :, :], t["w1"].rearrange("e d f -> d e f")).then_inc(in_w1, 16)
                    sync.dma_start(w2[:, :, :, :].rearrange("p e c d -> p (e c) d"),
                                   t["w2"].rearrange("e (c p) d -> p (e c) d", p=128)).then_inc(in_w2, 16)
            sync.sem_inc(out_done, 16)
            sync.dma_start(mask_u8[:, :, :], t["mask"].rearrange("b o q k -> q (b o) k")).then_inc(in_mask, 16)
            def store(g):
                need(sync, "b_xo", g)
                sync.dma_start(out[G * g:G * g + G].rearrange("b s d -> s b d"), xo[:, :, :]).then_inc(out_done, 16)

            for i in range(B):
                if i % G == 2 and i > G:
                    store(i // G - 1)
                if i >= 2:
                    need(sync, "c_sc", 0, i - 1)
                sync.dma_start(bias[:, i % 2, :, :], t["bias"][i].rearrange("h q k -> q h k")).then_inc(in_bias[i % 2], 16)

            store(NG - 1)
            sync.wait_ge(out_done, 16 * (NG + 1))

        @block.gpsimd
        def _(pool):
            start(pool, "pool")
            pool.memset(minus_half[:, :], -0.5).then_inc(once["pool_const"], 1)
            pool.memset(vh[:, :, :, :], 1.0).then_inc(once["pool_const"], 1)
            pool.memset(h3[:, :, :], 1.0).then_inc(once["pool_const"], 1)
            pool.wait_ge(once["pool_const"], 3)

            def rstd(g, var, ve, rs, out_sig):
                need(pool, var, g)
                did(pool.tensor_tensor(rs[:, :], ve[:, :], minus_half[:, :], ALU.pow), out_sig)

            pool.wait_ge(once["onehot_ed"], 1)
            pool.wait_ge(in_small, 16 * 6)

            def oh(e):
                return onehot_ed[:, e, :].unsqueeze(2).to_broadcast([A, B, A])

            def ew(e):
                return expert_T[:, e, :].unsqueeze(1).to_broadcast([A, B, A])

            pool.tensor_tensor(wsel[:, :, :], ew(0), oh(0), ALU.mult).then_inc(pool_chain, 1)
            n = 1
            for e in range(1, ED):
                pool.wait_ge(pool_chain, n)
                pool.tensor_tensor(wtmp[:, :, :], ew(e), oh(e), ALU.mult).then_inc(pool_chain, 1)
                pool.wait_ge(pool_chain, n + 1)
                pool.tensor_tensor(wsel[:, :, :], wsel[:, :, :], wtmp[:, :, :], ALU.add).then_inc(pool_chain, 1)
                n += 2
            pool.wait_ge(pool_chain, n)
            pool.tensor_tensor(wtmp[:, :, :], mats[0:A, 0:A].unsqueeze(1).to_broadcast([A, B, A]),
                               invalid[:, :].unsqueeze(2).to_broadcast([A, B, A]), ALU.mult).then_inc(pool_chain, 1)
            pool.wait_ge(pool_chain, n + 1)
            pool.tensor_tensor(wsel[:, :, :], wsel[:, :, :], wtmp[:, :, :], ALU.add).then_inc(once["wsel"], 1)

            with pool.Fori(0, NG) as g:
                rstd(g, "a_var", ve0, rs0, "a_rstd")
                rstd(g, "a_var1", ve1, rs1, "a_rstd1")

            with pool.Fori(0, NG) as g:
                need(pool, "b_f0", g)
                need(pool, "b_mix", g, 0)
                did(pool.tensor_tensor(a0f[:, :, :], f0[:, :, :], mat("A0").unsqueeze(1).to_broadcast([128, G, D]), ALU.mult), "b_a0f")
                need(pool, "b_df", g, 0)
                did(pool.tensor_tensor(b0f[:, :, :], f0[:, :, :], mat("B0").unsqueeze(1).to_broadcast([128, G, D]), ALU.mult), "b_b0f")
                rstd(g, "b_var2", ve2, rs2, "b_rstd2")
                need(pool, "b_xT", g)
                need(pool, "b_x2_mm", g, 0)
                did(pool.tensor_tensor(xbT[:, :, :], xT[:, :, :], col("bo").unsqueeze(2).to_broadcast([128, G, S]), ALU.add), "b_xbT")
                for b in range(G):
                    need(pool, "c_mx", g, b + 1)
                    did(pool.tensor_tensor(sc[:, b % 2, :, :], sc[:, b % 2, :, :],
                                           mx[:, b % 2, :].unsqueeze(2).to_broadcast([128, H, S]), ALU.subtract), "c_sub")
                rstd(g, "b_var3", ve3, rs3, "b_rstd3")
                need(pool, "b_x2", g)
                need(pool, "b_x3", g, 0)
                did(pool.tensor_tensor(x2b[:, :, :], x2[:, :, :], rows[:, 1, :].unsqueeze(1).to_broadcast([128, G, D]), ALU.add), "b_x2b")
                rstd(g, "b_var4", ve4, rs4, "b_rstd4")
                need(pool, "b_xn4", g)
                need(pool, "b_xo", g, 0)
                did(pool.tensor_tensor(xg[:, :, :], xn4[:, :, :], rows[:, 2, :].unsqueeze(1).to_broadcast([128, G, D]), ALU.mult), "b_xg")
                need(pool, "b_xg", g)
                pool.wait_ge(out_done, 16 * (g + 1))
                did(pool.tensor_tensor(xo[:, :, :], xg[:, :, :], rows[:, 3, :].unsqueeze(1).to_broadcast([128, G, D]), ALU.add), "b_xo")

        @block.vector
        def _(dve):
            start(dve, "dve")
            n = 0

            def chain(ins):
                nonlocal n
                n += 1
                ins.then_inc(dve_chain, 1)
                dve.wait_ge(dve_chain, n)

            dve.wait_ge(in_small, 16 * 6)
            dve.tensor_copy(ident_bf[:, :], mat("ident"))
            chain(dve.tensor_copy(idf[:, :, :], ids[:, :, :]))
            dve.tensor_scalar(sp[:, 0, :], idf[:, 2, :], 0.0, None, ALU.is_ge)
            chain(dve.tensor_scalar(sp[:, 1, :], idf[:, 2, :], float(ED - 1), None, ALU.is_le))
            dve.tensor_tensor(valid[:, :], sp[:, 0, :], sp[:, 1, :], ALU.mult)
            dve.tensor_scalar(idf[:, 0, :], idf[:, 0, :], 0.0, 31.0, ALU.max, ALU.min)
            chain(dve.tensor_scalar(idf[:, 2, :], idf[:, 2, :], 0.0, float(ED - 1), ALU.max, ALU.min))
            dve.tensor_scalar(onehot[:, 0, :], idf[:, 0, :], col("row"), None, ALU.is_equal)
            dve.tensor_scalar(onehot[:, 1, :], idf[:, 2, :], col("row"), None, ALU.is_equal)
            c0 = COLS["count"][0]
            chain(dve.tensor_tensor(onehot_ed[:, :, :], idf[0:A, 2, :].unsqueeze(1).to_broadcast([A, ED, B]),
                                    cols[0:A, c0:c0 + ED].unsqueeze(2).to_broadcast([A, ED, B]), ALU.is_equal))
            chain(dve.tensor_tensor(onehot_ed[:, :, :], onehot_ed[:, :, :],
                                    valid[0:A, :].unsqueeze(1).to_broadcast([A, ED, B]), ALU.mult))
            dve.tensor_scalar(invalid[:, :], valid[0:A, :], -1.0, 1.0, ALU.mult, ALU.add).then_inc(once["onehot_ed"], 1)
            chain(dve.tensor_tensor(onehot_v[:, :], onehot[0:ED, 1, :], valid[0:ED, :], ALU.mult))
            dve.tensor_scalar(sp[:, 0, :], idf[:, 1, :], 0.01, 4000.0, ALU.mult, ALU.mult).then_inc(once["onehot"], 1)
            dve.wait_ge(once["onehot"], 1)
            chain(dve.tensor_scalar(ang[:, 0, :], sp[:, 0, :], col("freq"), None, ALU.mult))
            chain(dve.tensor_scalar(ang[:, 1, :], ang[:, 0, :], 1.0 / TWO_PI, col("turn"), ALU.mult, ALU.add))
            chain(dve.tensor_scalar(ang[:, 1, :], ang[:, 1, :], ROUND, None, ALU.add))
            chain(dve.tensor_scalar(ang[:, 1, :], ang[:, 1, :], ROUND, None, ALU.subtract))
            chain(dve.scalar_tensor_tensor(ang[:, 2, :], ang[:, 1, :], -PI_HI, ang[:, 0, :], ALU.mult, ALU.add))
            chain(dve.scalar_tensor_tensor(ang[:, 0, :], ang[:, 1, :], -PI_MID, ang[:, 2, :], ALU.mult, ALU.add))
            chain(dve.scalar_tensor_tensor(ang[:, 2, :], ang[:, 1, :], -PI_LO, ang[:, 0, :], ALU.mult, ALU.add))
            chain(dve.tensor_scalar(ang[:, 3, :], col("turn").to_broadcast([128, B]), TWO_PI, None, ALU.mult))
            chain(dve.tensor_tensor(ang[:, 3, :], ang[:, 3, :], ang[:, 2, :], ALU.add))
            dve.tensor_scalar(ang[:, 3, :], ang[:, 3, :], 3.1415925, -3.1415925, ALU.min, ALU.max).then_inc(once["ang"], 1)

            dve.wait_ge(once["se"], 1)
            dve.tensor_copy(seT[:, :], banks[0][0:SE, 0:B]).then_inc(once["seT"], 1)
            dve.wait_ge(once["hyp1"], 1)
            dve.tensor_scalar(hyp1T[:, :], banks[1][:, 0:B], col("hyp_b1"), 0.0, ALU.add, ALU.max).then_inc(once["hyp1T"], 1)
            dve.wait_ge(once["hyp2"], 1)
            dve.tensor_scalar(hyp2T[:, :], banks[2][:, 0:B], col("hyp_b2"), None, ALU.add).then_inc(once["hyp2T"], 1)
            dve.wait_ge(once["sty1"], 1)
            dve.tensor_scalar(sty1T[:, :], banks[3][0:SH // 2, 0:B], col("sty_b1")[0:SH // 2], 0.0, ALU.add, ALU.max).then_inc(once["sty1T"], 1)
            dve.wait_ge(once["sty2"], 1)
            chain(dve.tensor_scalar(gamT[:, :], banks[4][:, 0:B], col("gamma_b"), None, ALU.add))
            dve.tensor_scalar(betT[:, :], banks[4][:, B:2 * B], col("beta_b"), None, ALU.add)
            chain(dve.tensor_scalar(sp[:, 1, :], gamT[:, :], -1.0, None, ALU.mult))
            dve.tensor_tensor(sp[:, 1, :], gamT[:, :], sp[:, 1, :], ALU.max).then_inc(once["gam_abs"], 1)
            chain(dve.tensor_scalar(sp[:, 0, :], gamT[:, :], 0.0, 1e-8, ALU.max, ALU.add))
            dve.wait_ge(once["gam_ln"], 1)
            chain(dve.tensor_tensor(gamT[:, :], sp[:, 0, :], sp[:, 3, :], ALU.add))
            dve.wait_ge(once["silu_e"], 1)
            chain(dve.tensor_scalar(ang[:, 5, :], ang[:, 5, :], 1.0, None, ALU.add))
            chain(dve.reciprocal(ang[:, 5, :], ang[:, 5, :]))
            dve.tensor_tensor(ang[:, 4, :], ang[:, 4, :], ang[:, 5, :], ALU.mult).then_inc(once["silu"], 1)
            dve.wait_ge(once["ada"], 1)
            dve.tensor_scalar(scaleT[:, :], banks[5][:, 0:B], col("scale_b"), 1.0, ALU.add, ALU.add)
            dve.tensor_scalar(shiftT[:, :], banks[5][:, B:2 * B], col("shift_b"), None, ALU.add)
            dve.wait_ge(once["esel"], 1)
            chain(dve.tensor_copy(esel[:, :], banks[6][0:A, 0:B]))
            dve.wait_ge(in_mask, 16)
            dve.sem_inc(once["consts"], 1)

            linked = 0

            def link(ins, name, g):
                nonlocal linked
                linked += 1
                did(ins, name)
                need(dve, name, g, linked)

            def moments(srcs, st, mv, ve, eps, name, g, ready):
                for b, src in enumerate(srcs):
                    last = dve.bn_stats(st[:, b, :], src)
                link(last, name, g)
                dve.nop(nofuse=True)
                for b in range(G):
                    last = dve.bn_aggr(mv[:, b, :], st[:, b, :])
                link(last, name, g)
                did(dve.tensor_scalar(ve[:, :], mv[:, :, 1], eps, None, ALU.add), ready)

            for g in range(NG):
                dve.wait_ge(in_x[g], 16)
            with dve.Fori(0, NG) as g:
                def x_of(b):
                    return xall[:, bass.ds(g * G + b, 1), :].rearrange("p o d -> p (o d)")

                moments([x_of(b) for b in range(G)], st0, mv0, ve0, 1e-5, "vec_a", g, "a_var")
                need(dve, "a_rstd", g)
                need(dve, "a_xnT", g, 0)
                for b in range(G):
                    last = dve.tensor_scalar(xn0[:, b, :], x_of(b), mv0[:, b, 0:1], rs0[:, b:b + 1], ALU.subtract, ALU.mult)
                did(last, "a_xn")
                need(dve, "a_hT", g)
                moments([hT[:, b, :] for b in range(G)], st1, mv1, ve1, 1e-8, "vec_a", g, "a_var1")
                need(dve, "a_rstd1", g)
                link(dve.tensor_tensor(amp[:, :], rs1[:, :], grp(gamT, g), ALU.mult), "vec_a", g)
                link(dve.tensor_tensor(off[:, :], mv1[:, :, 0], amp[:, :], ALU.mult), "vec_a", g)
                link(dve.tensor_tensor(off[:, :], grp(betT, g), off[:, :], ALU.subtract), "vec_a", g)
                need(dve, "a_hid_mm", g, 0)
                for b in range(G):
                    last = dve.tensor_scalar(hs[:, b, :], hT[:, b, :], amp[:, b:b + 1], off[:, b:b + 1], ALU.mult, ALU.add)
                did(last, "a_hs")
                need(dve, "a_logit", g)
                did(dve.tensor_copy(lg[:, :, :], banks[1][:, 0:G * E].rearrange("p (b e) -> p b e", b=G)), "a_lg")
                need(dve, "a_lg", g)
                dve.nop(nofuse=True)
                for b in range(G):
                    last = dve.max(top[:, b, :], lg[:, b, :])
                link(last, "vec_a", g)
                did(dve.tensor_tensor(lge[:, :, :], lg[:, :, :], top[:, :, 0:1].to_broadcast([128, G, E]), ALU.subtract), "a_lge")
                for b in range(G):
                    last = dve.max_index(topi[:, b, :], top[:, b, :], lg[:, b, :])
                link(last, "vec_a", g)
                link(dve.tensor_copy(topf[:, :, :], topi[:, :, :]), "vec_a", g)
                c0 = COLS["count"][0]
                for k in range(2):
                    last = dve.tensor_tensor(sel[:, k, :, :], cols[:, c0:c0 + E].unsqueeze(1).to_broadcast([128, G, E]),
                                             topf[:, :, k:k + 1].to_broadcast([128, G, E]), ALU.is_equal)
                link(last, "vec_a", g)
                link(dve.tensor_tensor(sel[:, 0, :, :], sel[:, 0, :, :], sel[:, 1, :, :], ALU.add), "vec_a", g)
                need(dve, "a_exp", g)
                link(dve.tensor_tensor(sel[:, 1, :, :], sel[:, 0, :, :], lge[:, :, :], ALU.mult), "vec_a", g)
                link(dve.tensor_reduce(gsum[:, :], sel[:, 1, :, :], AX_X, ALU.add), "vec_a", g)
                link(dve.reciprocal(grec[:, :], gsum[:, :]), "vec_a", g)
                did(dve.tensor_tensor(gate[:, :, :], sel[:, 1, :, :], grec[:, :].unsqueeze(2).to_broadcast([128, G, E]), ALU.mult), "a_gate")
                need(dve, "a_gT", g)
                did(dve.tensor_copy(gateT[:, :, :], banks[2][0:E, :].rearrange("e (b s) -> e b s", b=G)), "a_gateT")
                need(dve, "a_b2", g)
                did(dve.tensor_tensor(grp(xall, g), bank4(7), grp(xall, g), ALU.add), "a_b2x")
                need(dve, "a_b2x", g)
                for e in range(E):
                    need(dve, "a_y_mm", g, e + 1)
                    need(dve, "a_y", g, e)
                    for b in range(G):
                        last = dve.scalar_tensor_tensor(x_of(b), bank4(5 + e % 2)[:, b, :], gate[:, b, e:e + 1], x_of(b),
                                                        ALU.mult, ALU.add)
                    did(last, "a_y")
            assert linked == VEC_A, linked
            linked = 0

            with dve.Fori(0, NG) as g:
                need(dve, "b_exp_mm", g, 0)
                dve.tensor_copy(wc[:, :, :], grp(wsel, g))
                dve.tensor_copy(ec[:, :], grp(esel, g))
                dve.tensor_copy(dtc[:, :], grp(dt_row, g))
                dve.tensor_copy(adac[:, 0, :], grp(scaleT, g))
                need(dve, "c_s_mm", g, 0)
                dve.tensor_scalar(mask_c[:, :, :], grp(mask_u8, g), MASKED, None, ALU.mult)
                did(dve.tensor_copy(adac[:, 1, :], grp(shiftT, g)), "b_wc")
                need(dve, "b_f0T", g)
                need(dve, "b_df", g, 0)
                for dst, grid in ((b2fT, "B2T"), (a1fT, "A1T"), (b1fT, "B1T")):
                    last = dve.tensor_tensor(dst[:, :, :], bank4(0), mat(grid).unsqueeze(1).to_broadcast([128, G, S]), ALU.mult)
                did(last, "b_prodT")
                need(dve, "b_t1", g)
                need(dve, "b_a0f", g)
                did(dve.tensor_tensor(mix[:, :, :], bank4(1), a0f[:, :, :], ALU.subtract), "b_mix")
                need(dve, "b_df", g)
                need(dve, "b_wc", g)
                for b in range(G):
                    last = dve.scalar_tensor_tensor(f1[:, b, :], bank4(2)[:, b, :], dtc[:, b:b + 1], f0[:, b, :], ALU.mult, ALU.add)
                link(last, "vec_b", g)
                did(dve.tensor_scalar(f1[:, :, :], f1[:, :, :], 0.0, None, ALU.max), "b_f1")
                need(dve, "b_f1", g)
                moments([f1[:, b, :] for b in range(G)], st2, mv2, ve2, 1e-5, "vec_b", g, "b_var2")
                need(dve, "b_rstd2", g)
                need(dve, "b_xn2T", g, 0)
                for b in range(G):
                    last = dve.tensor_scalar(xn2[:, b, :], f1[:, b, :], mv2[:, b, 0:1], rs2[:, b:b + 1], ALU.subtract, ALU.mult)
                did(last, "b_xn2")
                need(dve, "b_xn2T", g)
                need(dve, "b_v_mm", g, 0)
                need(dve, "b_xbT", g, 0)
                for b in range(G):
                    last = dve.tensor_scalar(xT[:, b, :], bank4(3)[:, b, :], adac[:, 0, b:b + 1], adac[:, 1, b:b + 1], ALU.mult, ALU.add)
                did(last, "b_xT")
                need(dve, "b_q_mm", g)
                did(dve.tensor_scalar(qT[:, :, :], bank4(0), col("bq"), 1.0 / math.sqrt(HD), ALU.add, ALU.mult), "b_qT")
                need(dve, "b_kT", g)
                for h in range(H):
                    last = dve.tensor_scalar(kh[:, h, :, :], kT[:, :, :], col("head", h), None, ALU.mult)
                did(last, "b_kh")
                need(dve, "b_v_mm", g)
                for b in range(G):
                    last = dve.tensor_tensor(vh[:, b, :, 0:HD], bank4(2)[:, b, :].rearrange("p (h d) -> p h d", h=H),
                                             rows[:, 0, :].rearrange("p (h d) -> p h d", h=H), ALU.add)
                did(last, "b_vh")

                def scores(b):
                    need(dve, "c_s_mm", g, b + 1)
                    dve.wait_ge(in_bias[b % 2], (g * (G // 2) + (b // 2 + 1)) * 16)
                    need(dve, "c_pT_mm", g, (b - 1) * QB)
                    for r in range(QB):
                        last = dve.tensor_tensor(sc[:, b % 2, HQ * r:HQ * r + HQ, :], banks[r][:, :].rearrange("p (h k) -> p h k", h=HQ),
                                                 bias[:, b % 2, HQ * r:HQ * r + HQ, :], ALU.add)
                    did(last, "c_sc")
                    need(dve, "c_sc", g, b + 1)
                    need(dve, "c_sub", g, b - 1)
                    did(dve.tensor_reduce(mx[:, b % 2, :], sc[:, b % 2, :, :], AX_X, ALU.max), "c_mx")

                def context(b):
                    need(dve, "c_ctx_mm", g, b + 1)
                    pv = banks[7][:, 0:H * (HD + 1)].rearrange("p (h d) -> p h d", h=H)
                    link(dve.reciprocal(rec[:, :], pv[:, :, HD]), "vec_b", g)
                    need(dve, "c_cxT_mm", g, b)
                    did(dve.tensor_tensor(cx[:, :, :], pv[:, :, 0:HD], rec[:, :].unsqueeze(2).to_broadcast([128, H, HD]), ALU.mult), "c_cx")

                for b in range(G):
                    scores(b)
                    if b:
                        context(b - 1)
                context(G - 1)

                need(dve, "b_x2", g)
                moments([x2[:, b, :] for b in range(G)], st3, mv3, ve3, 1e-5, "vec_b", g, "b_var3")
                need(dve, "b_rstd3", g)
                need(dve, "b_xn3T", g, 0)
                for b in range(G):
                    last = dve.tensor_scalar(xn3[:, b, :], x2[:, b, :], mv3[:, b, 0:1], rs3[:, b:b + 1], ALU.subtract, ALU.mult)
                did(last, "b_xn3")
                need(dve, "b_ff_mm", g)
                need(dve, "b_x2b", g)
                did(dve.tensor_tensor(x3[:, :, :], bank4(6), x2b[:, :, :], ALU.add), "b_x3")
                need(dve, "b_exp_mm", g)
                need(dve, "b_up_mm", g, 0)
                for b in range(G):
                    last = dve.tensor_scalar(h3[0:A, b, :], banks[2][0:A, b * S:(b + 1) * S], ec[:, b:b + 1], None, ALU.add)
                did(last, "b_h3")
                need(dve, "b_up_mm", g)
                did(dve.tensor_tensor(x4[:, :, :], bank4(3), x3[:, :, :], ALU.add), "b_x4")
                need(dve, "b_x4", g)
                moments([x4[:, b, :] for b in range(G)], st4, mv4, ve4, 1e-5, "vec_b", g, "b_var4")
                need(dve, "b_rstd4", g)
                need(dve, "b_xg", g, 0)
                for b in range(G):
                    last = dve.tensor_scalar(xn4[:, b, :], x4[:, b, :], mv4[:, b, 0:1], rs4[:, b:b + 1], ALU.subtract, ALU.mult)
                did(last, "b_xn4")
            assert linked == VEC_B, linked

        @block.scalar
        def _(act):
            start(act, "act")
            act.wait_ge(in_small, 16 * 6)
            act.wait_ge(once["ang"], 1)
            act.activation(ang[:, 4, :], ang[:, 3, :], ACT.Sin).then_inc(once["sin"], 1)
            act.wait_ge(once["gam_abs"], 1)
            act.activation(sp[:, 2, :], sp[:, 1, :], ACT.Exp, scale=-1.0).then_inc(once["gam_exp"], 1)
            act.wait_ge(once["gam_exp"], 1)
            act.activation(sp[:, 3, :], sp[:, 2, :], ACT.Ln, bias=1.0).then_inc(once["gam_ln"], 1)
            act.wait_ge(once["sin"], 1)
            act.activation(ang[:, 5, :], ang[:, 4, :], ACT.Exp, scale=-1.0).then_inc(once["silu_e"], 1)
            with act.Fori(0, NG) as g:
                need(act, "a_xnT", g)
                need(act, "a_hs", g, 0)
                did(act.activation(hT[:, :, :].rearrange("p b s -> p (b s)"), banks[0][:, :], ACT.Identity, bias=col("ln_b"), scale=col("ln_g")), "a_hT")
                need(act, "a_lge", g)
                did(act.activation(lge[:, :, :], lge[:, :, :], ACT.Exp), "a_exp")
                for i in range(E * FC):
                    e, c = divmod(i, FC)
                    need(act, "a_hid_mm", g, i + 1)
                    need(act, "a_y_mm", g, e - 1)
                    did(act.activation(hid[:, e % 2, c, :], banks[3 + i % 2][:, :], ACT.Relu, bias=col("exp_b1", i)), "a_hid")
            with act.Fori(0, NG) as g:
                need(act, "b_f1", g, 0)
                need(act, "b_b0f", g, 0)
                act.wait_ge(sig["a_y"].sem, NG * E + 2)
                did(act.activation(f0[:, :, :], grp(xall, g), ACT.Copy), "b_f0")
                need(act, "b_k_mm", g)
                need(act, "b_kh", g, 0)
                did(act.activation(kT[:, :, :], bank4(1), ACT.Identity, bias=col("bk")), "b_kT")

                def softmax(b):
                    need(act, "c_sub", g, b + 1)
                    did(act.activation(sc[:, b % 2, :, :], sc[:, b % 2, :, :], ACT.Exp), "c_exp")

                def evacuate(b):
                    for r in range(QB):
                        need(act, "c_pT_mm", g, b * QB + r + 1)
                        need(act, "c_ctx_mm", g, b)
                        did(act.activation(pT[:, HQ * r:HQ * r + HQ, :], banks[4 + r % 2][:, :].rearrange("p (h q) -> p h q", h=HQ), ACT.Copy), "c_pT")

                def context_T(b):
                    need(act, "c_cxT_mm", g, b + 1)
                    need(act, "b_x2_mm", g, 0)
                    did(act.activation(cxT[:, b, :], banks[6][:, 0:S], ACT.Copy), "c_cxT")

                for b in range(G):
                    softmax(b)
                    evacuate(b)
                    if b:
                        context_T(b - 1)
                context_T(G - 1)
                need(act, "b_x2_mm", g)
                need(act, "b_x2b", g, 0)
                did(act.activation(x2[:, :, :], bank4(7), ACT.Copy), "b_x2")
                need(act, "b_xn3T", g)
                need(act, "b_ff1_mm", g, 0)
                did(act.activation(h2T[:, :], banks[4][:, :], ACT.Identity, bias=col("beta2"), scale=col("g2")), "b_h2T")
                need(act, "b_ff_mm", g, 0)
                for c in range(FC):
                    need(act, "b_ff1_mm", g, c + 1)
                    did(act.activation(hid2[:, c, :], banks[c][:, :], ACT.Gelu_apprx_sigmoid, bias=col("ff_b1", c)), "b_hid2")
                need(act, "b_x3T_mm", g)
                need(act, "b_down_mm", g, 0)
                did(act.activation(x3T[:, :], banks[0][:, :], ACT.Copy), "b_x3T")
                need(act, "b_down_mm", g)
                need(act, "b_exp_mm", g, 0)
                did(act.activation(hd[:, :, :].rearrange("a b s -> a (b s)"), banks[1][0:A, :], ACT.Gelu, bias=col("down_b")[0:A]), "b_hd")


        @block.tensor
        def _(pe):
            start(pe, "pe")
            pe.wait_ge(in_small, 16 * 6)
            pe.wait_ge(once["onehot"], 1)
            pe.matmul(banks[0][0:SE, 0:B], mat("subj", p=32), onehot[0:32, 0, :], start=True, stop=True).then_inc(once["se"], 1)
            pe.matmul(banks[6][0:A, 0:B], mat("expert_b", p=ED), onehot_v[:, :], start=True, stop=False)
            pe.matmul(banks[6][0:A, 0:B], mat("domain_emb", p=ED), onehot[0:ED, 1, :], start=False, stop=True).then_inc(once["esel"], 1)
            pe.wait_ge(once["seT"], 1)
            pe.matmul(banks[1][:, 0:B], mat("hyp_w1", p=SE), seT[:, :], start=True, stop=True).then_inc(once["hyp1"], 1)
            pe.wait_ge(once["hyp1T"], 1)
            pe.matmul(banks[2][:, 0:B], mat("hyp_w2"), hyp1T[:, :], start=True, stop=True).then_inc(once["hyp2"], 1)
            pe.wait_ge(once["hyp2T"], 1)
            pe.matmul(banks[3][0:SH // 2, 0:B], mat("sty_w1"), hyp2T[:, :], start=True, stop=True).then_inc(once["sty1"], 1)
            pe.wait_ge(once["sty1T"], 1)
            for k in range(2):
                last = pe.matmul(banks[4][:, B * k:B * k + B], mat("sty_w2", k, p=SH // 2), sty1T[:, :], start=True, stop=True)
            last.then_inc(once["sty2"], 1)
            pe.wait_ge(once["silu"], 1)
            for k in range(2):
                last = pe.matmul(banks[5][:, B * k:B * k + B], mat("W_ada", k), ang[:, 4, :], start=True, stop=True)
            last.then_inc(once["ada"], 1)
            pe.wait_ge(once["consts"], 1)
            pe.wait_ge(in_w1, 16)
            pe.wait_ge(in_w2, 16)

            hs_all = hs[:, :, :].rearrange("p b s -> p (b s)")
            with pe.Fori(0, NG) as g:
                need(pe, "a_xn", g)
                need(pe, "a_hT", g, 0)
                for b in range(G):
                    last = pe.transpose(bank4(0)[:, b, :], xn0[:, b, :], mat("ident"))
                did(last, "a_xnT")
                need(pe, "a_hs", g)
                need(pe, "a_lg", g, 0)
                for b in range(G):
                    last = pe.matmul(banks[1][:, b * E:(b + 1) * E], hs[:, b, :], mat("router"), start=True, stop=True)
                did(last, "a_logit")

                def first(i):
                    e, c = divmod(i, FC)
                    need(pe, "a_hid", g, i - 1)
                    did(pe.matmul(banks[3 + i % 2][:, :], w1[:, e, 128 * c:128 * c + 128], hs_all, start=True, stop=True), "a_hid_mm")

                for c in range(FC):
                    first(c)
                need(pe, "a_gate", g)
                need(pe, "a_gateT", g, 0)
                for b in range(G):
                    last = pe.transpose(banks[2][0:E, b * S:(b + 1) * S], gate[:, b, :], mat("ident"))
                did(last, "a_gT")
                need(pe, "a_gateT", g)
                need(pe, "a_b2x", g, 0)
                for b in range(G):
                    last = pe.matmul(bank4(7)[:, b, :], gateT[:, b, :], mat("exp_b2", p=E), start=True, stop=True)
                did(last, "a_b2")
                for e in range(E):
                    if e + 1 < E:
                        for c in range(FC):
                            first(FC * (e + 1) + c)
                    need(pe, "a_hid", g, FC * (e + 1))
                    need(pe, "a_y", g, e - 1)
                    for b in range(G):
                        for c in range(FC):
                            last = pe.matmul(bank4(5 + e % 2)[:, b, :], hid[:, e % 2, c, b * S:(b + 1) * S], w2[:, e, c, :],
                                             start=(c == 0), stop=(c == FC - 1))
                    did(last, "a_y_mm")
            need(pe, "a_y", NG, 0)
            with pe.Fori(0, NG) as g:
                def T(ap, b):
                    return ap[:, b, :]

                need(pe, "b_f0", g)
                need(pe, "b_x3T", g, 0)
                for b in range(G):
                    last = pe.transpose(bank4(0)[:, b, :], f0[:, b, :], mat("ident"))
                did(last, "b_f0T")
                need(pe, "b_prodT", g)
                need(pe, "b_hd", g, 0)
                for b in range(G):
                    last = pe.matmul(bank4(1)[:, b, :], b2fT[:, b, :], mat("gradT"), start=True, stop=True)
                did(last, "b_t1")
                need(pe, "b_b0f", g)
                need(pe, "b_h3", g, 0)
                pe.matmul(banks[2][:, :], mat("hgrad2T"), b0f[:, :, :].rearrange("p b d -> p (b d)"), start=True, stop=False, skip_group_check=True)
                for b in range(G):
                    pe.matmul(bank4(2)[:, b, :], a1fT[:, b, :], mat("ngradT"), start=False, stop=False, skip_group_check=True)
                    pe.matmul(bank4(2)[:, b, :], b1fT[:, b, :], mat("hgrad2T"), start=False, stop=False, skip_group_check=True)
                need(pe, "b_mix", g)
                did(pe.matmul(banks[2][:, :], mat("gradT"), mix[:, :, :].rearrange("p b d -> p (b d)"), start=False, stop=True, skip_group_check=True), "b_df")
                need(pe, "b_xn2", g)
                need(pe, "b_x4", g, 0)
                for b in range(G):
                    last = pe.transpose(bank4(3)[:, b, :], xn2[:, b, :], mat("ident"))
                did(last, "b_xn2T")
                need(pe, "b_xT", g)
                x_flat = xT[:, :, :].rearrange("p b s -> p (b s)")
                did(pe.matmul(banks[0][:, :], mat("Wq"), x_flat, start=True, stop=True), "b_q_mm")
                did(pe.matmul(banks[1][:, :], mat("Wk"), x_flat, start=True, stop=True), "b_k_mm")
                need(pe, "b_f1", g)
                for b in range(G):
                    last = pe.matmul(bank4(2)[:, b, :], xT[:, b, :], mat("Wv"), start=True, stop=True)
                did(last, "b_v_mm")

                def scores(b):
                    if b == 0:
                        need(pe, "b_qT", g)
                        need(pe, "b_kh", g)
                        need(pe, "b_vh", g)
                    need(pe, "c_sc", g, b)
                    for r in range(QB):
                        pe.matmul(banks[r][:, :].rearrange("p (h k) -> p h k", h=HQ), ident_bf[:, :],
                                  mask_c[:, b, :].unsqueeze(1).to_broadcast([128, HQ, S]), start=True, stop=False)
                        last = pe.matmul(banks[r][:, :].rearrange("p (h k) -> p h k", h=HQ), qT[:, b, :], kh[:, HQ * r:HQ * r + HQ, b, :],
                                         start=False, stop=True)
                    did(last, "c_s_mm")

                def values(b):
                    need(pe, "c_exp", g, b + 1)
                    for r in range(QB):
                        need(pe, "c_pT", g, b * QB + r - 1)
                        if b == 0 and r < 2:
                            need(pe, "b_h2T", g, 0)
                        for h in range(HQ):
                            last = pe.transpose(banks[4 + r % 2][:, h * S:(h + 1) * S], sc[:, b % 2, HQ * r + h, :], mat("ident"))
                        did(last, "c_pT_mm")
                    need(pe, "c_pT", g, (b + 1) * QB)
                    need(pe, "c_cx", g, b)
                    if b == 0:
                        need(pe, "b_x2", g, 0)
                    for h in range(H):
                        last = pe.matmul(banks[7][:, h * (HD + 1):(h + 1) * (HD + 1)], pT[:, h, :], vh[:, b, h, :], start=True, stop=True)
                    did(last, "c_ctx_mm")

                def context_T(b):
                    need(pe, "c_cx", g, b + 1)
                    need(pe, "c_cxT", g, b)
                    if b == 0:
                        need(pe, "b_x3", g, 0)
                    did(pe.transpose(banks[6][:, 0:S], cx[:, :, :].rearrange("p h d -> p (h d)"), mat("ident")), "c_cxT_mm")

                scores(0)
                for b in range(G):
                    if b + 1 < G:
                        scores(b + 1)
                    values(b)
                    if b:
                        context_T(b - 1)
                context_T(G - 1)
                need(pe, "c_cxT", g, G)
                need(pe, "b_xbT", g)
                for b in range(G):
                    pe.matmul(bank4(7)[:, b, :], cxT[:, b, :], mat("Wo"), start=True, stop=False)
                    last = pe.matmul(bank4(7)[:, b, :], xbT[:, b, :], mat("ident"), start=False, stop=True)
                did(last, "b_x2_mm")
                need(pe, "b_xn3", g)
                for b in range(G):
                    last = pe.transpose(bank4(4)[:, b, :], xn3[:, b, :], mat("ident"))
                did(last, "b_xn3T")
                need(pe, "b_h2T", g)
                need(pe, "c_sc", g, G)
                for c in range(FC):
                    did(pe.matmul(banks[c][:, :], mat("W1", c), h2T[:, :], start=True, stop=True), "b_ff1_mm")
                need(pe, "b_hid2", g, FC)
                for b in range(G):
                    for c in range(FC):
                        last = pe.matmul(bank4(6)[:, b, :], hid2[:, c, b * S:(b + 1) * S], mat("W2", c), start=(c == 0), stop=(c == FC - 1))
                did(last, "b_ff_mm")
                need(pe, "b_x3", g)
                for b in range(G):
                    last = pe.transpose(bank4(0)[:, b, :], x3[:, b, :], mat("ident"))
                did(last, "b_x3T_mm")
                need(pe, "b_x3T", g)
                did(pe.matmul(banks[1][0:A, :], mat("downT"), x3T[:, :], start=True, stop=True), "b_down_mm")
                need(pe, "b_hd", g)
                need(pe, "b_wc", g)
                pe.nop(nofuse=True)
                for b in range(G):
                    last = pe.matmul(banks[2][0:A, b * S:(b + 1) * S], wc[:, b, :], hd[:, b, :], start=True, stop=True)
                did(last, "b_exp_mm")
                need(pe, "b_h3", g)
                for b in range(G):
                    last = pe.matmul(bank4(3)[:, b, :], h3[:, b, :], mat("upT", p=A + 1), start=True, stop=True)
                did(last, "b_up_mm")



def kernel(**inputs):
    from concourse import bacc
    from concourse.bass_utils import run_bass_kernel_spmd

    x = {k: np.asarray(v) for k, v in inputs.items()}
    grad = np.zeros((128, 128), np.float32)
    grad2 = np.zeros((128, 128), np.float32)
    for i in range(1, 127):
        grad[i, i - 1], grad[i, i + 1] = -0.5, 0.5
        grad2[i, i - 1], grad2[i, i], grad2[i, i + 1] = 1.0, -2.0, 1.0
    grad[0, 0:3] = -1.5, 2.0, -0.5
    grad[127, 125:128] = 0.5, -2.0, 1.5
    grad2[0, 0:4] = 2.0, -5.0, 4.0, -1.0
    grad2[127, 124:128] = -1.0, 4.0, -5.0, 2.0
    half = D // 2
    freq = np.exp(np.arange(half, dtype=np.float32) * np.float32(-math.log(10000.0) / (half - 1)))
    head = (np.arange(128)[:, None] // HD == np.arange(H)[None, :]).astype(np.float32)

    def padded(a):
        a = a.reshape(a.shape[0], -1)
        full = np.zeros((128, a.shape[1]), np.float32)
        full[:a.shape[0]] = a
        return full

    vectors = {
        "ln_g": x["L0_cond_ln_g"], "ln_b": x["L0_cond_ln_b"], "hyp_b1": x["L0_cond_hyp_b1"], "hyp_b2": x["L0_cond_hyp_b2"],
        "sty_b1": x["L0_cond_sty_b1"], "gamma_b": x["L0_cond_sty_b2"][:D], "beta_b": x["L0_cond_sty_b2"][D:],
        "scale_b": x["L2_cond_b_ada"][:D], "shift_b": x["L2_cond_b_ada"][D:], "bq": x["L2_cond_bq"], "bk": x["L2_cond_bk"],
        "bo": x["L2_cond_bo"], "g2": x["L2_cond_g2"], "beta2": x["L2_cond_beta2"], "down_b": x["L3_cond_down_b"],
        "ff_b1": x["L2_cond_b1"].reshape(FC, 128).T, "exp_b1": x["L0_cond_exp_b1"].reshape(E * FC, 128).T,
        "head": head, "freq": np.tile(freq, 2), "turn": np.repeat(np.float32([0.0, 0.25]), half),
        "row": np.arange(128, dtype=np.float32), "count": np.tile(np.arange(ED, dtype=np.float32), (128, 1)),
    }
    matrices = {
        "ident": np.eye(128, dtype=np.float32), "gradT": grad.T, "ngradT": -grad.T, "hgrad2T": 0.5 * grad2.T,
        "A0": x["L1_cond_A_grid"][0], "B0": x["L1_cond_B_grid"][0], "A1T": x["L1_cond_A_grid"][1].T,
        "B1T": x["L1_cond_B_grid"][1].T, "B2T": x["L1_cond_B_grid"][2].T, "subj": x["L0_cond_subj_emb"],
        "hyp_w1": x["L0_cond_hyp_w1"], "hyp_w2": x["L0_cond_hyp_w2"], "sty_w1": x["L0_cond_sty_w1"],
        "sty_w2": x["L0_cond_sty_w2"], "W_ada": x["L2_cond_W_ada"], "router": x["L0_cond_router_w"],
        "Wq": x["L2_cond_Wq"], "Wk": x["L2_cond_Wk"], "Wv": x["L2_cond_Wv"], "Wo": x["L2_cond_Wo"], "W1": x["L2_cond_W1"],
        "W2": x["L2_cond_W2"].reshape(FC, 128, D).transpose(1, 0, 2), "downT": x["L3_cond_down_W"].T,
        "upT": np.concatenate([x["L3_cond_up_W"].T, x["L3_cond_up_b"][None]]), "expert_b": x["L3_cond_expert_b"],
        "domain_emb": x["L3_cond_domain_emb"], "exp_b2": x["L0_cond_exp_b2"],
    }
    arrays = {
        "cols": np.concatenate([padded(vectors[n]) for n in COLS], axis=1),
        "mats": np.concatenate([padded(matrices[n]) for n in MATS], axis=1),
        "ids": np.concatenate([x["itok_B_6_14"], x["itok_B_34_63"], x["itok_B_0_15"]]),
        "dt": x["condB_dt"],
        "rows": np.concatenate([x["L2_cond_bv"], x["L2_cond_b2"], x["L3_cond_ln_gamma"], x["L3_cond_ln_beta"]]),
        "expert_T": x["L3_cond_expert_W"].transpose(2, 0, 1), "x": x["x"], "w1": x["L0_cond_exp_w1"],
        "w2": x["L0_cond_exp_w2"], "mask": x["mask_Bx1xSxS_bk0"], "bias": x["fside_Bx16xSxS_0"],
    }
    nc = bacc.Bacc("TRN2", target_bir_lowering=False, num_devices=1)
    arrays = {"in_" + n: np.ascontiguousarray(a) for n, a in arrays.items()}
    tensors = {n[3:]: nc.dram_tensor(n, a.shape, mybir.dt.from_np(a.dtype), kind="ExternalInput").ap() for n, a in arrays.items()}
    out = nc.dram_tensor("out", (B, S, D), F32, kind="ExternalOutput").ap()
    build(nc, tensors, out)
    return run_bass_kernel_spmd(nc, [arrays], core_ids=[0]).results[0]["out"]
```

```python
import math
from contextlib import ExitStack

import numpy as np
import concourse.bass as bass
from concourse import mybir

ALU = mybir.AluOpType
ACT = mybir.ActivationFunctionType
F32 = mybir.dt.float32
BF16 = mybir.dt.bfloat16
I32 = mybir.dt.int32
U32 = mybir.dt.uint32
U8 = mybir.dt.uint8
AX_X = mybir.AxisListType.X

B, S, D = 32, 128, 128
G = 4
NG = B // G
HID_BANKS = (3, 4, 2, 7)
N = G * S
E, FF = 8, 512
FC = FF // 128
H, HD = 16, 8
HQ = 4
A, ED = 32, 16
SE, SH = 64, 128
MASKED = -1e30
TWO_PI = 2.0 * math.pi
ROUND = 12582912.0
PI_HI = 6.28125
PI_MID = 0.0019340515136718750
PI_LO = TWO_PI - PI_HI - PI_MID

COLS = {}
for _name, _width in (("ln_g", 1), ("ln_b", 1), ("hyp_b1", 1), ("hyp_b2", 1), ("sty_b1", 1), ("gamma_b", 1),
                      ("beta_b", 1), ("scale_b", 1), ("shift_b", 1), ("bq", 1), ("bk", 1), ("bo", 1), ("g2", 1),
                      ("beta2", 1), ("down_b", 1), ("ff_b1", FC), ("exp_b1", E * FC), ("head", H), ("freq", 1),
                      ("turn", 1), ("row", 1), ("count", ED)):
    COLS[_name] = (sum(w for _, w in COLS.values()), _width)
NCOL = sum(w for _, w in COLS.values())

MATS = {}
for _name, _width in (("ident", 128), ("gradT", 128), ("ngradT", 128), ("hgrad2T", 128), ("A0", 128), ("B0", 128),
                      ("A1T", 128), ("B1T", 128), ("B2T", 128), ("subj", SE), ("hyp_w1", SH), ("hyp_w2", SH),
                      ("sty_w1", SH // 2), ("sty_w2", 2 * D), ("W_ada", 2 * D), ("router", E), ("Wq", D), ("Wk", D),
                      ("Wv", D), ("Wo", D), ("W1", FF), ("W2", FC * D), ("downT", A), ("upT", D), ("expert_b", A),
                      ("domain_emb", A), ("exp_b2", D)):
    MATS[_name] = (sum(w for _, w in MATS.values()), _width)
NMAT = sum(w for _, w in MATS.values())


VEC_A = 7


class Signal:

    def __init__(self, sem, per, ahead=1):
        self.sem, self.per, self.ahead = sem, per, ahead

    def need(self, eng, g, k):
        value = g * self.per + (k + self.ahead)
        if not (isinstance(value, int) and value <= self.ahead):
            eng.wait_ge(self.sem, value)


def build(nc, t, out):
    with ExitStack() as ctx:
        def sb(name, shape, dt=F32):
            return ctx.enter_context(nc.sbuf_tensor(name, shape, dt))

        def sem(name):
            return ctx.enter_context(nc.semaphore(name))

        banks = [ctx.enter_context(nc.psum_tensor(f"bank{i}", [128, 512], F32)) for i in range(8)]

        def bank4(i):
            return banks[i][:, :].rearrange("p (b n) -> p b n", b=G)

        cols = sb("cols", [128, NCOL])
        mats = sb("mats", [128, NMAT])
        moe_w = sb("moe_w", [128, 4 * E * FF], BF16)
        parts = moe_w[:, :].rearrange("p (k n) -> p k n", k=4)
        w1_hi, w1_lo = (parts[:, k, :].rearrange("p (e f) -> p e f", e=E) for k in (0, 1))
        w2_hi, w2_lo = (parts[:, k, :].rearrange("p (e c d) -> p e c d", e=E, c=FC) for k in (2, 3))
        kh = moe_w[:, :].bitcast(F32).rearrange("p (h b s) -> p h b s", h=H, b=G)
        xall = sb("xall", [128, B, D])
        rows = sb("rows", [128, 4, D])
        ids = sb("ids", [128, 3, B], I32)
        dt_row = sb("dt_row", [128, B])
        mask_u8 = sb("mask_u8", [128, B, S], U8)
        ident_bf = sb("ident_bf", [128, 128], BF16)
        minus_half = sb("minus_half", [128, G])
        expert_w = sb("expert_w", [ED, A, A])

        def col(name, k=0):
            c = COLS[name][0] + k
            return cols[:, c:c + 1]

        def mat(name, k=None, p=128):
            c, w = MATS[name]
            if k is not None:
                c, w = c + 128 * k, 128
            return mats[0:p, c:c + w]

        idf = sb("idf", [128, 3, B])
        onehot = sb("onehot", [128, 2, B])
        valid = sb("valid", [128, B])
        seT = sb("seT", [SE, B])
        hyp1T = sb("hyp1T", [SH, B])
        hyp2T = sb("hyp2T", [SH, B])
        sty1T = sb("sty1T", [SH // 2, B])
        gamT = sb("gamT", [128, B])
        betT = sb("betT", [128, B])
        sp = sb("sp", [128, 4, B])
        ang = sb("ang", [128, 6, B])
        scaleT = sb("scaleT", [128, B])
        shiftT = sb("shiftT", [128, B])
        onehot_v = sb("onehot_v", [ED, B])
        invalid = sb("invalid", [A, B])
        wsel = sb("wsel", [A, B, A])
        wtmp = sb("wtmp", [A, B, A])
        esel = sb("esel", [A, B])

        st0 = sb("st0", [128, G, 6])
        mv0 = sb("mv0", [128, G, 2])
        ve0 = sb("ve0", [128, G])
        rs0 = sb("rs0", [128, G])
        xn0 = sb("xn0", [128, G, D])
        hT = sb("hT", [128, G, S])
        st1 = sb("st1", [128, G, 6])
        mv1 = sb("mv1", [128, G, 2])
        ve1 = sb("ve1", [128, G])
        rs1 = sb("rs1", [128, G])
        amp = sb("amp", [128, G])
        off = sb("off", [128, G])
        hs = sb("hs", [128, G, S])
        lg = sb("lg", [128, G, E])
        top = sb("top", [128, G, 8])
        topi = sb("topi", [128, G, 8], U32)
        sel = sb("sel", [128, 2, G, E])
        lge = sb("lge", [128, G, E])
        gate = sb("gate", [128, G, E])
        gsum = sb("gsum", [128, G])
        grec = sb("grec", [128, G])
        gateT = sb("gateT", [E, G, S])
        hs_hi = sb("hs_hi", [128, N], BF16)
        hs_lo = sb("hs_lo", [128, N], BF16)
        hid = sb("hid", [128, 2, 2, FC, N], BF16)
        hid2 = hid[:, 0, :, :, :].rearrange("p e c n -> p (e c n)").bitcast(F32).rearrange("p (c n) -> p c n", c=FC)
        pT = hid[:, 1, :, :, :].rearrange("p e c n -> p (e c n)").bitcast(F32).rearrange("p (h q) -> p h q", h=H)
        ring = sb("ring", [128, 4, N])

        f0 = sb("f0", [128, G, D])
        a0f = sb("a0f", [128, G, D])
        b0f = sb("b0f", [128, G, D])
        a1fT = sb("a1fT", [128, G, S])
        b1fT = sb("b1fT", [128, G, S])
        b2fT = sb("b2fT", [128, G, S])
        mix = sb("mix", [128, G, D])
        f1 = sb("f1", [128, G, D])
        dtc = sb("dtc", [128, G])
        adac = sb("adac", [128, 2, G])

        st2 = sb("st2", [128, G, 6])
        mv2 = sb("mv2", [128, G, 2])
        ve2 = sb("ve2", [128, G])
        rs2 = sb("rs2", [128, G])
        xn2 = sb("xn2", [128, G, D])
        xT = sb("xT", [128, G, S])
        xbT = sb("xbT", [128, G, S])
        qT = sb("qT", [128, G, S])
        kT = sb("kT", [128, G, S])
        v0 = sb("v0", [128, G, D])
        vh = sb("vh", [128, G, H, HD + 1])
        bias = sb("bias", [128, 2, H, S])
        sc = sb("sc", [128, 2, H, S])
        w1_in = sc[:, :, :, :].rearrange("p a h s -> p (a h s)")
        w2_in = bias[:, :, :, :].rearrange("p a h s -> p (a h s)")
        mx = sb("mx", [128, 2, H])
        rec = sb("rec", [128, H])
        cx = sb("cx", [128, H, HD])
        cxT = sb("cxT", [128, G, S])
        x2 = sb("x2", [128, G, D])
        x2b = sb("x2b", [128, G, D])
        st3 = sb("st3", [128, G, 6])
        mv3 = sb("mv3", [128, G, 2])
        ve3 = sb("ve3", [128, G])
        rs3 = sb("rs3", [128, G])
        xn3 = sb("xn3", [128, G, D])
        h2T = sb("h2T", [128, N])

        x3 = sb("x3", [128, G, D])
        x3T = sb("x3T", [128, N])
        hd = sb("hd", [A, G, S])
        wc = sb("wc", [A, G, A])
        ec = sb("ec", [A, G])
        h3 = sb("h3", [A + 1, G, S])
        x4 = ring[:, 0, :].rearrange("p (b d) -> p b d", b=G)
        st4 = sb("st4", [128, G, 6])
        mv4 = sb("mv4", [128, G, 2])
        ve4 = sb("ve4", [128, G])
        rs4 = sb("rs4", [128, G])
        xn4 = ring[:, 1, :].rearrange("p (b d) -> p b d", b=G)
        xg = ring[:, 2, :].rearrange("p (b d) -> p b d", b=G)
        xo = ring[:, 3, :].rearrange("p (b d) -> p b d", b=G)
        mask_c = sb("mask_c", [128, G, S], BF16)

        in_small, in_w1, in_w2, in_mask = sem("in_small"), sem("in_w1"), sem("in_w2"), sem("in_mask")
        in_x = [sem(f"in_x{k}") for k in range(2)]
        out_done = sem("out_done")
        in_bias = [sem(f"in_bias{i}") for i in range(2)]
        once = {n: sem("s_" + n) for n in (
            "pool_const", "onehot", "se", "seT", "hyp1", "hyp1T", "hyp2", "hyp2T", "sty1", "sty1T", "sty2",
            "gam_exp", "gam_abs", "gam_ln", "ang", "sin", "silu_e", "silu", "ada", "esel", "invalid", "wtmp", "wsel_mm", "wsel",
            "w1_hi", "w1_lo", "w2_hi", "w2_lo")}
        dve_chain = sem("dve_chain")

        sig, owned = {}, {}

        def signals(owner, per, names, ahead=1):
            for n in names.split():
                sig[n] = Signal(sem(n), per, ahead)
                owned.setdefault(owner, []).append(sig[n])

        signals("dve", 1, "a_var a_xn a_var1 a_hs a_lg a_lge a_gate a_gateT a_b2x")
        signals("pool", 1, "a_rstd a_rstd1")
        signals("act", 1, "a_hT a_exp")
        signals("pe", 1, "a_xnT a_logit a_gT a_b2")
        signals("pe", E * FC, "a_hid_mm", ahead=2)
        signals("act", E * FC, "a_hid", ahead=4)
        signals("dve", E * FC, "a_hi", ahead=2)
        signals("pool", E * FC, "a_lo", ahead=4)
        signals("dve", 1, "a_hs_hi a_hs_lo")
        signals("pe", E, "a_y_mm", ahead=2)
        signals("dve", E, "a_y", ahead=2)
        signals("dve", 1, "b_prodT b_mix b_f1 b_var2 b_xn2 b_xT b_qT b_v b_var3 b_xn3 b_x3 b_dtc b_wc b_mask b_x4 b_var4 b_xn4")
        signals("pool", 1, "b_vh b_a0f b_b0f b_xbT b_rstd2 b_rstd3 b_x2b b_rstd4 b_xg b_xo")
        signals("act", 1, "b_f0 b_kT b_x2 b_h2T b_x3T b_hd b_h3")
        signals("pe", 1, "b_f0T b_t1 b_df b_xn2T b_q_mm b_k_mm b_v_mm b_x2_mm b_xn3T b_ff_mm b_x3T_mm b_down_mm b_exp_mm b_up_mm")
        signals("pe", FC, "b_ff1_mm")
        signals("act", FC, "b_hid2")
        signals("dve", H // HQ, "b_kh")
        signals("dve", G, "c_mx c_cx", ahead=3)
        signals("dve", G * (H // HQ), "c_sc", ahead=4)
        signals("pool", G, "c_sub", ahead=3)
        signals("act", G, "c_exp c_cxT", ahead=3)
        signals("pe", G, "c_ctx_mm c_cxT_mm", ahead=3)
        signals("pe", G * (H // HQ), "c_s_mm", ahead=4)
        signals("pe", G * (H // HQ), "c_pT_mm", ahead=4)
        signals("act", G * (H // HQ), "c_pT", ahead=4)
        signals("dve", VEC_A, "vec_a")
        signals("dve", 1, "a_st0 a_mv0 a_st1 a_mv1 a_amp a_off a_offs")
        signals("dve", 1, "b_f1r b_st2 b_mv2 b_st3 b_mv3 b_st4 b_mv4")
        signals("dve", G, "c_rec", ahead=3)

        def need(eng, name, g, k=1):
            sig[name].need(eng, g, k)

        def did(ins, name):
            ins.then_inc(sig[name].sem, 1)

        def start(eng, owner):
            for s in owned[owner]:
                eng.sem_inc(s.sem, s.ahead)

        def pipeline(eng, passes):
            for i in (-1, 0, 1):
                passes(i, att=i >= 0, prev=i >= 1, tail=False, pre=True)
            with eng.Fori(2, NG - 1) as i:
                passes(i, att=True, prev=True, tail=True, pre=True)
            for i in (NG - 1, NG, NG + 1):
                passes(i, att=i < NG, prev=i <= NG, tail=True, pre=False)

        QB = H // HQ

        def grp(ap, g):
            return ap[:, bass.ds(g * G, G)]

        block = ctx.enter_context(nc.Block())

        @block.sync
        def _(sync):
            sync.dma_start(cols[:, :], t["cols"]).then_inc(in_small, 16)
            sync.dma_start(mats[:, :], t["mats"]).then_inc(in_small, 16)
            sync.dma_start(ids[:, :, :].rearrange("p a b -> p (a b)"), t["ids"].partition_broadcast(128)).then_inc(in_small, 16)
            sync.dma_start(dt_row[:, :], t["dt"].partition_broadcast(128)).then_inc(in_small, 16)
            sync.dma_start(rows[:, :, :].rearrange("p a b -> p (a b)"), t["rows"].partition_broadcast(128)).then_inc(in_small, 16)
            sync.dma_start(expert_w[:, :, :], t["expert_w"]).then_inc(in_small, 16)
            sync.dma_start(xall[:, 0:G, :], t["x"][0:G].rearrange("b s d -> s b d")).then_inc(in_x[0], 16)
            sync.dma_start(w1_in.rearrange("p (e f) -> p e f", e=E), t["w1"].rearrange("e d f -> d e f")).then_inc(in_w1, 16)
            sync.dma_start(w2_in.rearrange("p (e d) -> p e d", d=D), t["w2"].rearrange("e (c p) d -> p (e c) d", p=128)).then_inc(in_w2, 16)
            sync.dma_start(xall[:, G:B, :], t["x"][G:B].rearrange("b s d -> s b d")).then_inc(in_x[1], 16)
            sync.sem_inc(out_done, 16)
            sync.dma_start(mask_u8[:, :, :], t["mask"].rearrange("b o q k -> q (b o) k")).then_inc(in_mask, 16)
            def store(g):
                need(sync, "b_xo", g)
                sync.dma_start(out[G * g:G * g + G].rearrange("b s d -> s b d"), xo[:, :, :]).then_inc(out_done, 16)

            for i in range(B):
                if i % G == 1 and i // G >= 3:
                    store(i // G - 3)
                if i == 0:
                    sync.wait_ge(once["w2_hi"], 1)
                    sync.wait_ge(once["w2_lo"], 1)
                if i >= 2:
                    need(sync, "c_sc", 0, QB * (i - 1))
                sync.dma_start(bias[:, i % 2, :, :], t["bias"][i].rearrange("h q k -> q h k")).then_inc(in_bias[i % 2], 16)

            for g in range(NG - 3, NG):
                store(g)
            sync.wait_ge(out_done, 16 * (NG + 1))

        @block.gpsimd
        def _(pool):
            start(pool, "pool")
            pool.memset(minus_half[:, :], -0.5).then_inc(once["pool_const"], 1)
            pool.memset(vh[:, :, :, :], 1.0).then_inc(once["pool_const"], 1)
            pool.memset(h3[:, :, :], 1.0).then_inc(once["pool_const"], 1)
            pool.wait_ge(once["pool_const"], 3)

            def rstd(g, var, ve, rs, out_sig):
                need(pool, var, g)
                did(pool.tensor_tensor(rs[:, :], ve[:, :], minus_half[:, :], ALU.pow), out_sig)

            pool.wait_ge(once["invalid"], 1)
            pool.tensor_tensor(wtmp[:, :, :], mats[0:A, 0:A].unsqueeze(1).to_broadcast([A, B, A]),
                               invalid[:, :].unsqueeze(2).to_broadcast([A, B, A]), ALU.mult).then_inc(once["wtmp"], 1)
            rstd(0, "a_var", ve0, rs0, "a_rstd")
            pool.wait_ge(once["w2_hi"], 1)
            pool.tensor_tensor(parts[:, 3, :], w2_in, parts[:, 2, :], ALU.subtract).then_inc(once["w2_lo"], 1)
            rstd(0, "a_var1", ve1, rs1, "a_rstd1")

            def low_part(g, i):
                e, c = divmod(i, FC)
                need(pool, "a_hi", g, i + 1)
                need(pool, "a_y_mm", g, e - 1)
                did(pool.tensor_tensor(hid[:, 1, e % 2, c, :], ring[:, i % 4, :], hid[:, 0, e % 2, c, :], ALU.subtract), "a_lo")

            def layer0(g, more):
                for i in range(FC, E * FC):
                    low_part(g, i)
                    if more and i == FC * 3 - 1:
                        rstd(g + 1, "a_var", ve0, rs0, "a_rstd")
                    if more and i == FC * 5 - 1:
                        rstd(g + 1, "a_var1", ve1, rs1, "a_rstd1")
                if more:
                    for i in range(FC):
                        low_part(g + 1, i)

            for i in range(FC):
                low_part(0, i)
            with pool.Fori(0, NG - 1) as g:
                layer0(g, True)
            layer0(NG - 1, False)

            def passes(i, att, prev, tail, pre):
                if pre:
                    need(pool, "b_f0", i + 1)
                    need(pool, "b_mix", i)
                    did(pool.tensor_tensor(a0f[:, :, :], f0[:, :, :], mat("A0").unsqueeze(1).to_broadcast([128, G, D]), ALU.mult), "b_a0f")
                    need(pool, "b_df", i)
                    did(pool.tensor_tensor(b0f[:, :, :], f0[:, :, :], mat("B0").unsqueeze(1).to_broadcast([128, G, D]), ALU.mult), "b_b0f")
                if att:
                    subtract(i, 0)
                    subtract(i, 1)
                if pre:
                    rstd(i + 1, "b_var2", ve2, rs2, "b_rstd2")
                if att:
                    need(pool, "b_v", i)
                    need(pool, "c_ctx_mm", i, 0)
                    for b in range(G):
                        last = pool.tensor_tensor(vh[:, b, :, 0:HD], v0[:, b, :].rearrange("p (h d) -> p h d", h=H),
                                                  rows[:, 0, :].rearrange("p (h d) -> p h d", h=H), ALU.add)
                    did(last, "b_vh")
                if att:
                    need(pool, "b_xT", i)
                    need(pool, "b_x2_mm", i, 0)
                    did(pool.tensor_tensor(xbT[:, :, :], xT[:, :, :], col("bo").unsqueeze(2).to_broadcast([128, G, S]), ALU.add), "b_xbT")
                    subtract(i, 2)
                if prev:
                    rstd(i - 1, "b_var3", ve3, rs3, "b_rstd3")
                if tail:
                    rstd(i - 2, "b_var4", ve4, rs4, "b_rstd4")
                if att:
                    subtract(i, 3)
                if prev:
                    need(pool, "b_x2", i - 1)
                    need(pool, "b_x3", i - 2)
                    did(pool.tensor_tensor(x2b[:, :, :], x2[:, :, :], rows[:, 1, :].unsqueeze(1).to_broadcast([128, G, D]), ALU.add), "b_x2b")
                if tail:
                    need(pool, "b_xn4", i - 2)
                    need(pool, "b_xo", i - 3)
                    did(pool.tensor_tensor(xg[:, :, :], xn4[:, :, :], rows[:, 2, :].unsqueeze(1).to_broadcast([128, G, D]), ALU.mult), "b_xg")
                    need(pool, "b_xg", i - 2)
                    pool.wait_ge(out_done, 16 * (i - 1))
                    did(pool.tensor_tensor(xo[:, :, :], xg[:, :, :], rows[:, 3, :].unsqueeze(1).to_broadcast([128, G, D]), ALU.add), "b_xo")

            def subtract(i, b):
                need(pool, "c_mx", i, b + 1)
                did(pool.tensor_tensor(sc[:, b % 2, :, :], sc[:, b % 2, :, :],
                                       mx[:, b % 2, :].unsqueeze(2).to_broadcast([128, H, S]), ALU.subtract), "c_sub")

            pipeline(pool, passes)

        @block.vector
        def _(dve):
            start(dve, "dve")
            n = 0

            def chain(ins):
                nonlocal n
                n += 1
                ins.then_inc(dve_chain, 1)
                dve.wait_ge(dve_chain, n)

            dve.wait_ge(in_small, 16 * 6)
            dve.tensor_copy(ident_bf[:, :], mat("ident"))
            chain(dve.tensor_copy(idf[:, :, :], ids[:, :, :]))
            dve.tensor_scalar(sp[:, 0, :], idf[:, 2, :], 0.0, None, ALU.is_ge)
            chain(dve.tensor_scalar(sp[:, 1, :], idf[:, 2, :], float(ED - 1), None, ALU.is_le))
            dve.tensor_tensor(valid[:, :], sp[:, 0, :], sp[:, 1, :], ALU.mult)
            dve.tensor_scalar(idf[:, 0, :], idf[:, 0, :], 0.0, 31.0, ALU.max, ALU.min)
            chain(dve.tensor_scalar(idf[:, 2, :], idf[:, 2, :], 0.0, float(ED - 1), ALU.max, ALU.min))
            dve.tensor_scalar(onehot[:, 0, :], idf[:, 0, :], col("row"), None, ALU.is_equal)
            chain(dve.tensor_scalar(onehot[:, 1, :], idf[:, 2, :], col("row"), None, ALU.is_equal))
            dve.tensor_scalar(invalid[:, :], valid[0:A, :], -1.0, 1.0, ALU.mult, ALU.add).then_inc(once["invalid"], 1)
            chain(dve.tensor_tensor(onehot_v[:, :], onehot[0:ED, 1, :], valid[0:ED, :], ALU.mult))
            dve.tensor_scalar(sp[:, 0, :], idf[:, 1, :], 0.01, 4000.0, ALU.mult, ALU.mult).then_inc(once["onehot"], 1)
            dve.wait_ge(once["onehot"], 1)
            chain(dve.tensor_scalar(ang[:, 0, :], sp[:, 0, :], col("freq"), None, ALU.mult))
            chain(dve.tensor_scalar(ang[:, 1, :], ang[:, 0, :], 1.0 / TWO_PI, col("turn"), ALU.mult, ALU.add))
            chain(dve.tensor_scalar(ang[:, 1, :], ang[:, 1, :], ROUND, None, ALU.add))
            chain(dve.tensor_scalar(ang[:, 1, :], ang[:, 1, :], ROUND, None, ALU.subtract))
            chain(dve.scalar_tensor_tensor(ang[:, 2, :], ang[:, 1, :], -PI_HI, ang[:, 0, :], ALU.mult, ALU.add))
            chain(dve.scalar_tensor_tensor(ang[:, 0, :], ang[:, 1, :], -PI_MID, ang[:, 2, :], ALU.mult, ALU.add))
            chain(dve.scalar_tensor_tensor(ang[:, 2, :], ang[:, 1, :], -PI_LO, ang[:, 0, :], ALU.mult, ALU.add))
            chain(dve.tensor_scalar(ang[:, 3, :], col("turn").to_broadcast([128, B]), TWO_PI, None, ALU.mult))
            chain(dve.tensor_tensor(ang[:, 3, :], ang[:, 3, :], ang[:, 2, :], ALU.add))
            dve.tensor_scalar(ang[:, 3, :], ang[:, 3, :], 3.1415925, -3.1415925, ALU.min, ALU.max).then_inc(once["ang"], 1)

            dve.wait_ge(once["se"], 1)
            dve.tensor_copy(seT[:, :], banks[0][0:SE, 0:B]).then_inc(once["seT"], 1)
            dve.wait_ge(once["hyp1"], 1)
            dve.tensor_scalar(hyp1T[:, :], banks[1][:, 0:B], col("hyp_b1"), 0.0, ALU.add, ALU.max).then_inc(once["hyp1T"], 1)
            dve.wait_ge(once["hyp2"], 1)
            dve.tensor_scalar(hyp2T[:, :], banks[2][:, 0:B], col("hyp_b2"), None, ALU.add).then_inc(once["hyp2T"], 1)
            dve.wait_ge(once["sty1"], 1)
            dve.tensor_scalar(sty1T[:, :], banks[3][0:SH // 2, 0:B], col("sty_b1")[0:SH // 2], 0.0, ALU.add, ALU.max).then_inc(once["sty1T"], 1)
            dve.wait_ge(once["sty2"], 1)
            chain(dve.tensor_scalar(gamT[:, :], banks[4][:, 0:B], col("gamma_b"), None, ALU.add))
            dve.tensor_scalar(betT[:, :], banks[4][:, B:2 * B], col("beta_b"), None, ALU.add)
            chain(dve.tensor_scalar(sp[:, 1, :], gamT[:, :], -1.0, None, ALU.mult))
            dve.tensor_tensor(sp[:, 1, :], gamT[:, :], sp[:, 1, :], ALU.max).then_inc(once["gam_abs"], 1)
            chain(dve.tensor_scalar(sp[:, 0, :], gamT[:, :], 0.0, 1e-8, ALU.max, ALU.add))
            dve.wait_ge(once["gam_ln"], 1)
            chain(dve.tensor_tensor(gamT[:, :], sp[:, 0, :], sp[:, 3, :], ALU.add))
            dve.wait_ge(once["silu_e"], 1)
            chain(dve.tensor_scalar(ang[:, 5, :], ang[:, 5, :], 1.0, None, ALU.add))
            chain(dve.reciprocal(ang[:, 5, :], ang[:, 5, :]))
            dve.tensor_tensor(ang[:, 4, :], ang[:, 4, :], ang[:, 5, :], ALU.mult).then_inc(once["silu"], 1)
            dve.wait_ge(once["ada"], 1)
            dve.tensor_scalar(scaleT[:, :], banks[5][:, 0:B], col("scale_b"), 1.0, ALU.add, ALU.add)
            dve.tensor_scalar(shiftT[:, :], banks[5][:, B:2 * B], col("shift_b"), None, ALU.add)
            dve.wait_ge(once["esel"], 1)
            dve.tensor_copy(esel[:, :], banks[3][0:A, B:2 * B])
            dve.wait_ge(once["wsel_mm"], 1)
            dve.wait_ge(once["wtmp"], 1)
            for k in range(2):
                half = slice(k * (A // 2), (k + 1) * (A // 2))
                last = dve.tensor_tensor(wsel[:, :, half], banks[6 + k][0:A, :].rearrange("p (o b) -> p b o", b=B), wtmp[:, :, half], ALU.add)
            chain(last)
            dve.sem_inc(once["wsel"], 1)

            linked = 0

            def link(ins, name, g):
                nonlocal linked
                linked += 1
                did(ins, name)
                need(dve, name, g, linked)

            def moments(srcs, st, mv, ve, eps, g, signal_stats, signal_means, ready):
                for b, src in enumerate(srcs):
                    last = dve.bn_stats(st[:, b, :], src)
                did(last, signal_stats)
                need(dve, signal_stats, g)
                dve.nop(nofuse=True)
                for b in range(G):
                    last = dve.bn_aggr(mv[:, b, :], st[:, b, :])
                did(last, signal_means)
                need(dve, signal_means, g)
                did(dve.tensor_scalar(ve[:, :], mv[:, :, 1], eps, None, ALU.add), ready)

            def x_of(g, b):
                return xall[:, bass.ds(g * G + b, 1), :].rearrange("p o d -> p (o d)")

            def feature_moments(g):
                moments([x_of(g, b) for b in range(G)], st0, mv0, ve0, 1e-5, g, "a_st0", "a_mv0", "a_var")

            def norm_features(g):
                need(dve, "a_xnT", g, 0)
                need(dve, "a_rstd", g)
                for b in range(G):
                    last = dve.tensor_scalar(xn0[:, b, :], x_of(g, b), mv0[:, b, 0:1], rs0[:, b:b + 1], ALU.subtract, ALU.mult)
                did(last, "a_xn")

            def position_moments(g):
                need(dve, "a_hT", g)
                moments([hT[:, b, :] for b in range(G)], st1, mv1, ve1, 1e-8, g, "a_st1", "a_mv1", "a_var1")

            def norm_positions(g):
                need(dve, "a_rstd1", g)
                did(dve.tensor_tensor(amp[:, :], rs1[:, :], grp(gamT, g), ALU.mult), "a_amp")
                need(dve, "a_amp", g)
                did(dve.tensor_tensor(off[:, :], mv1[:, :, 0], amp[:, :], ALU.mult), "a_off")

            def style(g):
                need(dve, "a_off", g)
                did(dve.tensor_tensor(off[:, :], grp(betT, g), off[:, :], ALU.subtract), "a_offs")
                need(dve, "a_offs", g)
                need(dve, "a_hid_mm", g, 0)
                for b in range(G):
                    last = dve.tensor_scalar(hs[:, b, :], hT[:, b, :], amp[:, b:b + 1], off[:, b:b + 1], ALU.mult, ALU.add)
                did(last, "a_hs")
                need(dve, "a_hs", g)
                did(dve.tensor_copy(hs_hi[:, :], hs[:, :, :].rearrange("p b s -> p (b s)")), "a_hs_hi")
                need(dve, "a_hs_hi", g)
                did(dve.tensor_tensor(hs_lo[:, :], hs[:, :, :].rearrange("p b s -> p (b s)"), hs_hi[:, :], ALU.subtract), "a_hs_lo")

            def high_parts(g, e):
                for c in range(FC):
                    i = FC * e + c
                    need(dve, "a_hid", g, i + 1)
                    if c == 0:
                        need(dve, "a_y_mm", g, e - 1)
                    did(dve.tensor_copy(hid[:, 0, e % 2, c, :], ring[:, i % 4, :]), "a_hi")

            def gates(g):
                need(dve, "a_logit", g)
                did(dve.tensor_copy(lg[:, :, :], banks[1][:, 0:G * E].rearrange("p (b e) -> p b e", b=G)), "a_lg")
                need(dve, "a_lg", g)
                dve.nop(nofuse=True)
                for b in range(G):
                    last = dve.max(top[:, b, :], lg[:, b, :])
                link(last, "vec_a", g)
                did(dve.tensor_tensor(lge[:, :, :], lg[:, :, :], top[:, :, 0:1].to_broadcast([128, G, E]), ALU.subtract), "a_lge")
                for b in range(G):
                    last = dve.max_index(topi[:, b, :], top[:, b, :], lg[:, b, :])
                link(last, "vec_a", g)
                high_parts(g, 1)
                c0 = COLS["count"][0]
                for k in range(2):
                    last = dve.tensor_tensor(sel[:, k, :, :], cols[:, c0:c0 + E].unsqueeze(1).to_broadcast([128, G, E]),
                                             topi[:, :, k:k + 1].to_broadcast([128, G, E]), ALU.is_equal)
                link(last, "vec_a", g)
                link(dve.tensor_tensor(sel[:, 0, :, :], sel[:, 0, :, :], sel[:, 1, :, :], ALU.add), "vec_a", g)
                need(dve, "a_exp", g)
                link(dve.tensor_tensor(sel[:, 1, :, :], sel[:, 0, :, :], lge[:, :, :], ALU.mult), "vec_a", g)
                link(dve.tensor_reduce(gsum[:, :], sel[:, 1, :, :], AX_X, ALU.add), "vec_a", g)
                link(dve.reciprocal(grec[:, :], gsum[:, :]), "vec_a", g)
                did(dve.tensor_tensor(gate[:, :, :], sel[:, 1, :, :], grec[:, :].unsqueeze(2).to_broadcast([128, G, E]), ALU.mult), "a_gate")

            def layer0(g, more):
                nonlocal linked
                linked = 0
                gates(g)
                need(dve, "a_gate", g)
                for e in range(E):
                    if 1 <= e < E - 1:
                        high_parts(g, e + 1)
                    if more and e == E - 2:
                        style(g + 1)
                    if more and e == E - 1:
                        high_parts(g + 1, 0)
                    if e == 1:
                        need(dve, "a_gT", g)
                        did(dve.tensor_copy(gateT[:, :, :], banks[1][0:E, :].rearrange("e (b s) -> e b s", b=G)), "a_gateT")
                    if e == 2:
                        need(dve, "a_b2", g)
                        need(dve, "a_y", g, e)
                        did(dve.tensor_tensor(grp(xall, g), bank4(1), grp(xall, g), ALU.add), "a_b2x")
                        need(dve, "a_b2x", g)
                    need(dve, "a_y_mm", g, e + 1)
                    if e:
                        need(dve, "a_y", g, e)
                    for b in range(G):
                        last = dve.scalar_tensor_tensor(x_of(g, b), bank4(5 + e % 2)[:, b, :], gate[:, b, e:e + 1], x_of(g, b),
                                                        ALU.mult, ALU.add)
                    did(last, "a_y")
                    if more and e == 1:
                        feature_moments(g + 1)
                    if more and e == 2:
                        norm_features(g + 1)
                    if more and e == 3:
                        position_moments(g + 1)
                    if more and e == 4:
                        norm_positions(g + 1)

            dve.wait_ge(in_x[0], 16)
            feature_moments(0)
            norm_features(0)
            dve.wait_ge(once["w1_hi"], 1)
            dve.tensor_tensor(parts[:, 1, :], w1_in, parts[:, 0, :], ALU.subtract).then_inc(once["w1_lo"], 1)
            position_moments(0)
            norm_positions(0)
            style(0)
            high_parts(0, 0)
            dve.wait_ge(in_x[1], 16)
            dve.wait_ge(in_mask, 16)
            with dve.Fori(0, NG - 1) as g:
                layer0(g, True)
            layer0(NG - 1, False)
            assert linked == VEC_A, linked

            def scores(i, b):
                dve.wait_ge(in_bias[b % 2], (i * (G // 2) + (b // 2 + 1)) * 16)
                need(dve, "c_pT_mm", i, (b - 1) * QB)
                for r in range(QB):
                    need(dve, "c_s_mm", i, QB * b + r + 1)
                    did(dve.tensor_tensor(sc[:, b % 2, HQ * r:HQ * r + HQ, :], banks[r][:, :].rearrange("p (h k) -> p h k", h=HQ),
                                          bias[:, b % 2, HQ * r:HQ * r + HQ, :], ALU.add), "c_sc")
                need(dve, "c_sc", i, QB * (b + 1))
                need(dve, "c_sub", i, b - 1)
                did(dve.tensor_reduce(mx[:, b % 2, :], sc[:, b % 2, :, :], AX_X, ALU.max), "c_mx")

            def context(i, b):
                need(dve, "c_ctx_mm", i, b + 1)
                pv = banks[6][:, 0:H * (HD + 1)].rearrange("p (h d) -> p h d", h=H)
                did(dve.reciprocal(rec[:, :], pv[:, :, HD]), "c_rec")
                need(dve, "c_rec", i, b + 1)
                need(dve, "c_cxT_mm", i, b)
                did(dve.tensor_tensor(cx[:, :, :], pv[:, :, 0:HD], rec[:, :].unsqueeze(2).to_broadcast([128, H, HD]), ALU.mult), "c_cx")

            def passes(i, att, prev, tail, pre):
                if pre:
                    dve.tensor_copy(dtc[:, :], grp(dt_row, i + 1))
                    dve.tensor_copy(adac[:, 0, :], grp(scaleT, i + 1))
                    did(dve.tensor_copy(adac[:, 1, :], grp(shiftT, i + 1)), "b_dtc")
                if tail:
                    dve.tensor_copy(wc[:, :, :], grp(wsel, i - 2))
                    did(dve.tensor_copy(ec[:, :], grp(esel, i - 2)), "b_wc")
                if att:
                    scores(i, 0)
                if pre:
                    need(dve, "b_f0T", i + 1)
                    for dst, grid in ((b2fT, "B2T"), (a1fT, "A1T"), (b1fT, "B1T")):
                        last = dve.tensor_tensor(dst[:, :, :], bank4(7), mat(grid).unsqueeze(1).to_broadcast([128, G, S]), ALU.mult)
                    did(last, "b_prodT")
                if tail:
                    need(dve, "b_ff_mm", i - 2)
                    need(dve, "b_x2b", i - 2)
                    did(dve.tensor_tensor(x3[:, :, :], bank4(5), x2b[:, :, :], ALU.add), "b_x3")
                if prev:
                    context(i - 1, 2)
                if pre:
                    need(dve, "b_t1", i + 1)
                    need(dve, "b_a0f", i + 1)
                    did(dve.tensor_tensor(mix[:, :, :], bank4(7), a0f[:, :, :], ALU.subtract), "b_mix")
                if att:
                    scores(i, 1)
                if pre:
                    need(dve, "b_df", i + 1)
                    need(dve, "b_dtc", i + 1)
                    for b in range(G):
                        last = dve.scalar_tensor_tensor(f1[:, b, :], bank4(7)[:, b, :], dtc[:, b:b + 1], f0[:, b, :], ALU.mult, ALU.add)
                    did(last, "b_f1r")
                    need(dve, "b_f1r", i + 1)
                    did(dve.tensor_scalar(f1[:, :, :], f1[:, :, :], 0.0, None, ALU.max), "b_f1")
                    need(dve, "b_f1", i + 1)
                    moments([f1[:, b, :] for b in range(G)], st2, mv2, ve2, 1e-5, i + 1, "b_st2", "b_mv2", "b_var2")
                if prev:
                    context(i - 1, 3)
                if pre:
                    need(dve, "b_rstd2", i + 1)
                    for b in range(G):
                        last = dve.tensor_scalar(xn2[:, b, :], f1[:, b, :], mv2[:, b, 0:1], rs2[:, b:b + 1], ALU.subtract, ALU.mult)
                    did(last, "b_xn2")
                if att:
                    scores(i, 2)
                if prev:
                    need(dve, "b_x2", i - 1)
                    moments([x2[:, b, :] for b in range(G)], st3, mv3, ve3, 1e-5, i - 1, "b_st3", "b_mv3", "b_var3")
                if tail:
                    need(dve, "b_up_mm", i - 2)
                    did(dve.tensor_tensor(x4[:, :, :], bank4(5), x3[:, :, :], ALU.add), "b_x4")
                if att:
                    context(i, 0)
                if pre:
                    need(dve, "b_xn2T", i + 1)
                    need(dve, "b_xbT", i)
                    for b in range(G):
                        last = dve.tensor_scalar(xT[:, b, :], bank4(7)[:, b, :], adac[:, 0, b:b + 1], adac[:, 1, b:b + 1], ALU.mult, ALU.add)
                    did(last, "b_xT")
                if tail:
                    need(dve, "b_x4", i - 2)
                    moments([x4[:, b, :] for b in range(G)], st4, mv4, ve4, 1e-5, i - 2, "b_st4", "b_mv4", "b_var4")
                if prev:
                    need(dve, "b_rstd3", i - 1)
                    for b in range(G):
                        last = dve.tensor_scalar(xn3[:, b, :], x2[:, b, :], mv3[:, b, 0:1], rs3[:, b:b + 1], ALU.subtract, ALU.mult)
                    did(last, "b_xn3")
                if att:
                    scores(i, 3)
                if tail:
                    need(dve, "b_rstd4", i - 2)
                    need(dve, "b_xg", i - 3)
                    for b in range(G):
                        last = dve.tensor_scalar(xn4[:, b, :], x4[:, b, :], mv4[:, b, 0:1], rs4[:, b:b + 1], ALU.subtract, ALU.mult)
                    did(last, "b_xn4")
                if pre:
                    need(dve, "b_q_mm", i + 1)
                    need(dve, "c_s_mm", i + 1, 0)
                    did(dve.tensor_scalar(qT[:, :, :], bank4(4), col("bq"), 1.0 / math.sqrt(HD), ALU.add, ALU.mult), "b_qT")
                    did(dve.tensor_scalar(mask_c[:, :, :], grp(mask_u8, i + 1), MASKED, None, ALU.mult), "b_mask")
                    need(dve, "b_kT", i + 1)
                for r in range(QB):
                    if att and r == QB - 1:
                        context(i, 1)
                    if pre:
                        for h in range(HQ * r, HQ * r + HQ):
                            last = dve.tensor_scalar(kh[:, h, :, :], kT[:, :, :], col("head", h), None, ALU.mult)
                        did(last, "b_kh")
                if pre:
                    need(dve, "b_v_mm", i + 1)
                    need(dve, "b_vh", i)
                    did(dve.tensor_copy(v0[:, :, :], bank4(7)), "b_v")

            pipeline(dve, passes)

        @block.scalar
        def _(act):
            start(act, "act")
            act.wait_ge(in_small, 16 * 6)
            act.wait_ge(in_w1, 16)
            act.activation(parts[:, 0, :], w1_in, ACT.Copy).then_inc(once["w1_hi"], 1)
            act.wait_ge(in_w2, 16)
            act.activation(parts[:, 2, :], w2_in, ACT.Copy).then_inc(once["w2_hi"], 1)
            act.wait_ge(once["ang"], 1)
            act.activation(ang[:, 4, :], ang[:, 3, :], ACT.Sin).then_inc(once["sin"], 1)
            act.wait_ge(once["gam_abs"], 1)
            act.activation(sp[:, 2, :], sp[:, 1, :], ACT.Exp, scale=-1.0).then_inc(once["gam_exp"], 1)
            act.wait_ge(once["gam_exp"], 1)
            act.activation(sp[:, 3, :], sp[:, 2, :], ACT.Ln, bias=1.0).then_inc(once["gam_ln"], 1)
            act.wait_ge(once["sin"], 1)
            act.activation(ang[:, 5, :], ang[:, 4, :], ACT.Exp, scale=-1.0).then_inc(once["silu_e"], 1)
            def transposed(g):
                need(act, "a_xnT", g)
                need(act, "a_hs", g, 0)
                did(act.activation(hT[:, :, :].rearrange("p b s -> p (b s)"), banks[0][:, :], ACT.Identity, bias=col("ln_b"), scale=col("ln_g")), "a_hT")

            def hidden(g, i):
                need(act, "a_hid_mm", g, i + 1)
                need(act, "a_lo", g, i - 3)
                did(act.activation(ring[:, i % 4, :], banks[HID_BANKS[i % 4]][:, :], ACT.Relu, bias=col("exp_b1", i)), "a_hid")

            def layer0(g, more):
                for i in range(FC, E * FC):
                    if i == FC + 1:
                        need(act, "a_lge", g)
                        did(act.activation(lge[:, :, :], lge[:, :, :], ACT.Exp), "a_exp")
                    hidden(g, i)
                    if more and i == FC * 5 - 1:
                        transposed(g + 1)
                if more:
                    for i in range(FC):
                        hidden(g + 1, i)

            transposed(0)
            for i in range(FC):
                hidden(0, i)
            with act.Fori(0, NG - 1) as g:
                layer0(g, True)
            layer0(NG - 1, False)

            need(act, "a_y", NG, 0)

            def evacuate(i, b):
                for r in range(QB):
                    need(act, "c_pT_mm", i, b * QB + r + 1)
                    if r == 0:
                        need(act, "c_ctx_mm", i, b)
                    did(act.activation(pT[:, HQ * r:HQ * r + HQ, :], banks[4 + r % 2][:, :].rearrange("p (h q) -> p h q", h=HQ), ACT.Copy), "c_pT")

            def context_T(i, b):
                need(act, "c_cxT_mm", i, b + 1)
                if b == 0:
                    need(act, "b_x2_mm", i, 0)
                did(act.activation(cxT[:, b, :], banks[6][:, 0:S], ACT.Copy), "c_cxT")

            def softmax(i, b):
                need(act, "c_sub", i, b + 1)
                did(act.activation(sc[:, b % 2, :, :], sc[:, b % 2, :, :], ACT.Exp), "c_exp")

            def passes(i, att, prev, tail, pre):
                if pre:
                    need(act, "b_f1", i)
                    need(act, "b_b0f", i)
                    did(act.activation(f0[:, :, :], grp(xall, i + 1), ACT.Copy), "b_f0")
                if prev:
                    evacuate(i - 1, 2)
                    softmax(i - 1, 3)
                if tail:
                    need(act, "b_x3T_mm", i - 2)
                    did(act.activation(x3T[:, :], banks[5][:, :], ACT.Copy), "b_x3T")
                if prev:
                    context_T(i - 1, 2)
                if prev:
                    evacuate(i - 1, 3)
                if att:
                    softmax(i, 0)
                if tail:
                    need(act, "b_down_mm", i - 2)
                    did(act.activation(hd[:, :, :].rearrange("a b s -> a (b s)"), banks[5][0:A, :], ACT.Gelu, bias=col("down_b")[0:A]), "b_hd")
                    need(act, "b_exp_mm", i - 2)
                    for b in range(G):
                        last = act.activation(h3[0:A, b, :], banks[5][0:A, b * S:(b + 1) * S], ACT.Identity, bias=ec[:, b:b + 1])
                    did(last, "b_h3")
                if prev:
                    context_T(i - 1, 3)
                if att:
                    evacuate(i, 0)
                if prev:
                    need(act, "b_x2_mm", i - 1)
                    need(act, "b_x2b", i - 2)
                    did(act.activation(x2[:, :, :], bank4(7), ACT.Copy), "b_x2")
                if att:
                    softmax(i, 1)
                    context_T(i, 0)
                if att:
                    evacuate(i, 1)
                if prev:
                    need(act, "b_xn3T", i - 1)
                    did(act.activation(h2T[:, :], banks[5][:, :], ACT.Identity, bias=col("beta2"), scale=col("g2")), "b_h2T")
                if pre:
                    need(act, "b_k_mm", i + 1)
                    need(act, "b_kh", i, QB)
                    did(act.activation(kT[:, :, :], bank4(7), ACT.Identity, bias=col("bk")), "b_kT")
                if att:
                    softmax(i, 2)
                if prev:
                    for c in range(FC):
                        need(act, "b_ff1_mm", i - 1, c + 1)
                        did(act.activation(hid2[:, c, :], banks[4 + c % 2][:, :], ACT.Gelu_apprx_sigmoid, bias=col("ff_b1", c)), "b_hid2")
                if att:
                    context_T(i, 1)

            pipeline(act, passes)

        @block.tensor
        def _(pe):
            start(pe, "pe")
            pe.wait_ge(in_small, 16 * 6)
            pe.wait_ge(once["onehot"], 1)
            pe.matmul(banks[0][0:SE, 0:B], mat("subj", p=32), onehot[0:32, 0, :], start=True, stop=True).then_inc(once["se"], 1)
            pe.matmul(banks[3][0:A, B:2 * B], mat("expert_b", p=ED), onehot_v[:, :], start=True, stop=False)
            pe.matmul(banks[3][0:A, B:2 * B], mat("domain_emb", p=ED), onehot[0:ED, 1, :], start=False, stop=True).then_inc(once["esel"], 1)
            for o in range(A):
                last = pe.matmul(banks[6 + o // (A // 2)][0:A, o % (A // 2) * B:(o % (A // 2) + 1) * B], expert_w[:, o, :], onehot_v[:, :],
                                 start=True, stop=True)
            last.then_inc(once["wsel_mm"], 1)
            pe.wait_ge(once["seT"], 1)
            pe.matmul(banks[1][:, 0:B], mat("hyp_w1", p=SE), seT[:, :], start=True, stop=True).then_inc(once["hyp1"], 1)
            pe.wait_ge(once["hyp1T"], 1)
            pe.matmul(banks[2][:, 0:B], mat("hyp_w2"), hyp1T[:, :], start=True, stop=True).then_inc(once["hyp2"], 1)
            pe.wait_ge(once["hyp2T"], 1)
            pe.matmul(banks[3][0:SH // 2, 0:B], mat("sty_w1"), hyp2T[:, :], start=True, stop=True).then_inc(once["sty1"], 1)
            pe.wait_ge(once["sty1T"], 1)
            for k in range(2):
                last = pe.matmul(banks[4][:, B * k:B * k + B], mat("sty_w2", k, p=SH // 2), sty1T[:, :], start=True, stop=True)
            last.then_inc(once["sty2"], 1)
            pe.wait_ge(once["silu"], 1)
            for k in range(2):
                last = pe.matmul(banks[5][:, B * k:B * k + B], mat("W_ada", k), ang[:, 4, :], start=True, stop=True)
            last.then_inc(once["ada"], 1)
            def transposes(g):
                need(pe, "a_xn", g)
                need(pe, "a_hT", g, 0)
                for b in range(G):
                    last = pe.transpose(bank4(0)[:, b, :], xn0[:, b, :], mat("ident"))
                did(last, "a_xnT")

            def logits(g):
                need(pe, "a_hs", g)
                need(pe, "a_b2x", g, 0)
                for b in range(G):
                    last = pe.matmul(banks[1][:, b * E:(b + 1) * E], hs[:, b, :], mat("router"), start=True, stop=True)
                did(last, "a_logit")

            def first(g, i):
                e, c = divmod(i, FC)
                if i == 0:
                    need(pe, "a_hs_lo", g)
                need(pe, "a_hid", g, i - 3)
                bank, at = banks[HID_BANKS[i % 4]], slice(128 * c, 128 * c + 128)
                pe.matmul(bank[:, :], w1_hi[:, e, at], hs_hi[:, :], start=True, stop=False)
                pe.matmul(bank[:, :], w1_hi[:, e, at], hs_lo[:, :], start=False, stop=False)
                did(pe.matmul(bank[:, :], w1_lo[:, e, at], hs_hi[:, :], start=False, stop=True), "a_hid_mm")

            def second(g, e):
                need(pe, "a_lo", g, FC * (e + 1))
                need(pe, "a_y", g, e - 1)
                for b in range(G):
                    for c in range(FC):
                        part = [hid[:, k, e % 2, c, b * S:(b + 1) * S] for k in range(2)]
                        pe.matmul(bank4(5 + e % 2)[:, b, :], part[0], w2_hi[:, e, c, :], start=(c == 0), stop=False)
                        pe.matmul(bank4(5 + e % 2)[:, b, :], part[0], w2_lo[:, e, c, :], start=False, stop=False)
                        last = pe.matmul(bank4(5 + e % 2)[:, b, :], part[1], w2_hi[:, e, c, :], start=False, stop=(c == FC - 1))
                did(last, "a_y_mm")

            def layer0(g, more):
                for e in range(E):
                    if e + 1 < E:
                        for c in range(FC):
                            first(g, FC * (e + 1) + c)
                    elif more:
                        logits(g + 1)
                        for c in range(FC):
                            first(g + 1, c)
                    if e == 1:
                        need(pe, "a_gate", g)
                        for b in range(G):
                            last = pe.transpose(banks[1][0:E, b * S:(b + 1) * S], gate[:, b, :], mat("ident"))
                        did(last, "a_gT")
                    if e == 2:
                        need(pe, "a_gateT", g)
                        for b in range(G):
                            last = pe.matmul(bank4(1)[:, b, :], gateT[:, b, :], mat("exp_b2", p=E), start=True, stop=True)
                        did(last, "a_b2")
                    second(g, e)
                    if more and e == 3:
                        transposes(g + 1)

            pe.wait_ge(once["wsel"], 1)
            transposes(0)
            for part in ("w1_hi", "w1_lo", "w2_hi", "w2_lo"):
                pe.wait_ge(once[part], 1)
            logits(0)
            for i in range(FC):
                first(0, i)
            with pe.Fori(0, NG - 1) as g:
                layer0(g, True)
            layer0(NG - 1, False)
            need(pe, "a_y", NG, 0)

            def scores(i, b, r):
                if b == 0 and r == 0:
                    need(pe, "b_qT", i)
                    need(pe, "b_mask", i)
                if b == 0:
                    need(pe, "b_kh", i, r + 1)
                need(pe, "c_sc", i, (b - 1) * QB + r + 1)
                quad = banks[r][:, :].rearrange("p (h k) -> p h k", h=HQ)
                pe.matmul(quad, ident_bf[:, :], mask_c[:, b, :].unsqueeze(1).to_broadcast([128, HQ, S]), start=True, stop=False)
                did(pe.matmul(quad, qT[:, b, :], kh[:, HQ * r:HQ * r + HQ, b, :], start=False, stop=True), "c_s_mm")

            def probs_T(i, b, r):
                if r == 0:
                    need(pe, "c_exp", i, b + 1)
                need(pe, "c_pT", i, b * QB + r - 1)
                for h in range(HQ):
                    last = pe.transpose(banks[4 + r % 2][:, h * S:(h + 1) * S], sc[:, b % 2, HQ * r + h, :], mat("ident"))
                did(last, "c_pT_mm")

            def values(i, b):
                need(pe, "c_pT", i, (b + 1) * QB)
                need(pe, "c_cxT", i, b)
                if b == 0:
                    need(pe, "b_vh", i)
                for h in range(H):
                    last = pe.matmul(banks[6][:, h * (HD + 1):(h + 1) * (HD + 1)], pT[:, h, :], vh[:, b, h, :], start=True, stop=True)
                did(last, "c_ctx_mm")

            def context_T(i, b):
                need(pe, "c_cx", i, b + 1)
                did(pe.transpose(banks[6][:, 0:S], cx[:, :, :].rearrange("p h d -> p (h d)"), mat("ident")), "c_cxT_mm")

            def turned(bank, src, name):
                for b in range(G):
                    last = pe.transpose(bank4(bank)[:, b, :], src[:, b, :], mat("ident"))
                did(last, name)

            x_flat = xT[:, :, :].rearrange("p b s -> p (b s)")

            def passes(i, att, prev, tail, pre):
                for r in range(QB):
                    if prev:
                        if tail and r < 2:
                            need(pe, "b_hid2", i - 2, FC - 1 + r)
                        if att and r == 0:
                            need(pe, "b_qT", i)
                        probs_T(i - 1, 2, r)
                    if att:
                        scores(i, 0, r)
                if pre:
                    need(pe, "b_v", i)
                    need(pe, "b_f0", i + 1)
                    turned(7, f0, "b_f0T")
                if tail:
                    need(pe, "b_hid2", i - 2, FC)
                    if prev:
                        need(pe, "c_pT", i - 1, 3 * QB)
                    for b in range(G):
                        for c in range(FC):
                            last = pe.matmul(bank4(5)[:, b, :], hid2[:, c, b * S:(b + 1) * S], mat("W2", c), start=(c == 0), stop=(c == FC - 1))
                    did(last, "b_ff_mm")
                if prev:
                    values(i - 1, 2)
                if tail:
                    need(pe, "b_x3", i - 2)
                    turned(5, x3, "b_x3T_mm")
                if pre:
                    need(pe, "b_prodT", i + 1)
                    for b in range(G):
                        last = pe.matmul(bank4(7)[:, b, :], b2fT[:, b, :], mat("gradT"), start=True, stop=True)
                    did(last, "b_t1")
                if prev:
                    context_T(i - 1, 2)
                for r in range(QB):
                    if prev:
                        if tail and r == 1:
                            need(pe, "b_x3T", i - 2)
                        probs_T(i - 1, 3, r)
                    if att:
                        scores(i, 1, r)
                if pre:
                    need(pe, "b_b0f", i + 1)
                    need(pe, "b_mix", i + 1)
                    pe.matmul(banks[7][:, :], mat("hgrad2T"), b0f[:, :, :].rearrange("p b d -> p (b d)"), start=True, stop=False, skip_group_check=True)
                    for b in range(G):
                        pe.matmul(bank4(7)[:, b, :], a1fT[:, b, :], mat("ngradT"), start=False, stop=False, skip_group_check=True)
                        pe.matmul(bank4(7)[:, b, :], b1fT[:, b, :], mat("hgrad2T"), start=False, stop=False, skip_group_check=True)
                    did(pe.matmul(banks[7][:, :], mat("gradT"), mix[:, :, :].rearrange("p b d -> p (b d)"), start=False, stop=True, skip_group_check=True), "b_df")
                if tail:
                    need(pe, "b_x3T", i - 2)
                    if prev:
                        need(pe, "c_pT", i - 1, 4 * QB)
                    did(pe.matmul(banks[5][0:A, :], mat("downT"), x3T[:, :], start=True, stop=True), "b_down_mm")
                if prev:
                    values(i - 1, 3)
                if tail:
                    need(pe, "b_hd", i - 2)
                    need(pe, "b_wc", i - 2)
                    pe.nop(nofuse=True)
                    for b in range(G):
                        last = pe.matmul(banks[5][0:A, b * S:(b + 1) * S], wc[:, b, :], hd[:, b, :], start=True, stop=True)
                    did(last, "b_exp_mm")
                if prev:
                    context_T(i - 1, 3)
                if att:
                    for r in range(QB):
                        if tail and r == 1:
                            need(pe, "b_h3", i - 2)
                        probs_T(i, 0, r)
                        scores(i, 2, r)
                if prev:
                    need(pe, "c_cxT", i - 1, G)
                    need(pe, "b_xbT", i - 1)
                    if pre:
                        need(pe, "b_f1r", i + 1)
                    elif att:
                        need(pe, "b_v", i)
                    else:
                        need(pe, "b_x2", i - 2)
                    for b in range(G):
                        pe.matmul(bank4(7)[:, b, :], cxT[:, b, :], mat("Wo"), start=True, stop=False)
                        last = pe.matmul(bank4(7)[:, b, :], xbT[:, b, :], mat("ident"), start=False, stop=True)
                    did(last, "b_x2_mm")
                if tail:
                    need(pe, "b_h3", i - 2)
                    if att:
                        need(pe, "c_pT", i, QB)
                    for b in range(G):
                        last = pe.matmul(bank4(5)[:, b, :], h3[:, b, :], mat("upT", p=A + 1), start=True, stop=True)
                    did(last, "b_up_mm")
                if att:
                    values(i, 0)
                if pre:
                    need(pe, "b_xn2", i + 1)
                    if prev:
                        need(pe, "b_x2", i - 1)
                    else:
                        need(pe, "b_f1r", i + 1)
                    turned(7, xn2, "b_xn2T")
                if att:
                    context_T(i, 0)
                if att:
                    for r in range(QB):
                        if tail and r == 1:
                            need(pe, "b_x4", i - 2)
                        probs_T(i, 1, r)
                        scores(i, 3, r)
                if prev:
                    need(pe, "b_xn3", i - 1)
                    if att:
                        need(pe, "c_pT", i, 2 * QB)
                    elif tail:
                        need(pe, "b_x4", i - 2)
                    turned(5, xn3, "b_xn3T")
                if pre:
                    need(pe, "b_xT", i + 1)
                    did(pe.matmul(banks[7][:, :], mat("Wk"), x_flat, start=True, stop=True), "b_k_mm")
                    if att:
                        need(pe, "c_pT", i, 2 * QB)
                    did(pe.matmul(banks[4][:, :], mat("Wq"), x_flat, start=True, stop=True), "b_q_mm")
                if att:
                    values(i, 1)
                if prev:
                    need(pe, "b_h2T", i - 1)
                    if pre:
                        need(pe, "b_qT", i + 1)
                for c in range(FC):
                    if prev:
                        need(pe, "b_hid2", i - 1, c - 1)
                        did(pe.matmul(banks[4 + c % 2][:, :], mat("W1", c), h2T[:, :], start=True, stop=True), "b_ff1_mm")
                    if pre and c == 1:
                        need(pe, "b_kT", i + 1)
                        for b in range(G):
                            last = pe.matmul(bank4(7)[:, b, :], xT[:, b, :], mat("Wv"), start=True, stop=True)
                        did(last, "b_v_mm")
                if att:
                    context_T(i, 1)

            pipeline(pe, passes)


def kernel(**inputs):
    from concourse import bacc
    from concourse.bass_utils import run_bass_kernel_spmd

    x = {k: np.asarray(v) for k, v in inputs.items()}
    grad = np.zeros((128, 128), np.float32)
    grad2 = np.zeros((128, 128), np.float32)
    for i in range(1, 127):
        grad[i, i - 1], grad[i, i + 1] = -0.5, 0.5
        grad2[i, i - 1], grad2[i, i], grad2[i, i + 1] = 1.0, -2.0, 1.0
    grad[0, 0:3] = -1.5, 2.0, -0.5
    grad[127, 125:128] = 0.5, -2.0, 1.5
    grad2[0, 0:4] = 2.0, -5.0, 4.0, -1.0
    grad2[127, 124:128] = -1.0, 4.0, -5.0, 2.0
    half = D // 2
    freq = np.exp(np.arange(half, dtype=np.float32) * np.float32(-math.log(10000.0) / (half - 1)))
    head = (np.arange(128)[:, None] // HD == np.arange(H)[None, :]).astype(np.float32)

    def padded(a):
        a = a.reshape(a.shape[0], -1)
        full = np.zeros((128, a.shape[1]), np.float32)
        full[:a.shape[0]] = a
        return full

    vectors = {
        "ln_g": x["L0_cond_ln_g"], "ln_b": x["L0_cond_ln_b"], "hyp_b1": x["L0_cond_hyp_b1"], "hyp_b2": x["L0_cond_hyp_b2"],
        "sty_b1": x["L0_cond_sty_b1"], "gamma_b": x["L0_cond_sty_b2"][:D], "beta_b": x["L0_cond_sty_b2"][D:],
        "scale_b": x["L2_cond_b_ada"][:D], "shift_b": x["L2_cond_b_ada"][D:], "bq": x["L2_cond_bq"], "bk": x["L2_cond_bk"],
        "bo": x["L2_cond_bo"], "g2": x["L2_cond_g2"], "beta2": x["L2_cond_beta2"], "down_b": x["L3_cond_down_b"],
        "ff_b1": x["L2_cond_b1"].reshape(FC, 128).T, "exp_b1": x["L0_cond_exp_b1"].reshape(E * FC, 128).T,
        "head": head, "freq": np.tile(freq, 2), "turn": np.repeat(np.float32([0.0, 0.25]), half),
        "row": np.arange(128, dtype=np.float32), "count": np.tile(np.arange(ED, dtype=np.float32), (128, 1)),
    }
    matrices = {
        "ident": np.eye(128, dtype=np.float32), "gradT": grad.T, "ngradT": -grad.T, "hgrad2T": 0.5 * grad2.T,
        "A0": x["L1_cond_A_grid"][0], "B0": x["L1_cond_B_grid"][0], "A1T": x["L1_cond_A_grid"][1].T,
        "B1T": x["L1_cond_B_grid"][1].T, "B2T": x["L1_cond_B_grid"][2].T, "subj": x["L0_cond_subj_emb"],
        "hyp_w1": x["L0_cond_hyp_w1"], "hyp_w2": x["L0_cond_hyp_w2"], "sty_w1": x["L0_cond_sty_w1"],
        "sty_w2": x["L0_cond_sty_w2"], "W_ada": x["L2_cond_W_ada"], "router": x["L0_cond_router_w"],
        "Wq": x["L2_cond_Wq"], "Wk": x["L2_cond_Wk"], "Wv": x["L2_cond_Wv"], "Wo": x["L2_cond_Wo"], "W1": x["L2_cond_W1"],
        "W2": x["L2_cond_W2"].reshape(FC, 128, D).transpose(1, 0, 2), "downT": x["L3_cond_down_W"].T,
        "upT": np.concatenate([x["L3_cond_up_W"].T, x["L3_cond_up_b"][None]]), "expert_b": x["L3_cond_expert_b"],
        "domain_emb": x["L3_cond_domain_emb"], "exp_b2": x["L0_cond_exp_b2"],
    }
    arrays = {
        "cols": np.concatenate([padded(vectors[n]) for n in COLS], axis=1),
        "mats": np.concatenate([padded(matrices[n]) for n in MATS], axis=1),
        "ids": np.concatenate([x["itok_B_6_14"], x["itok_B_34_63"], x["itok_B_0_15"]]),
        "dt": x["condB_dt"],
        "rows": np.concatenate([x["L2_cond_bv"], x["L2_cond_b2"], x["L3_cond_ln_gamma"], x["L3_cond_ln_beta"]]),
        "expert_w": x["L3_cond_expert_W"], "x": x["x"], "w1": x["L0_cond_exp_w1"],
        "w2": x["L0_cond_exp_w2"], "mask": x["mask_Bx1xSxS_bk0"], "bias": x["fside_Bx16xSxS_0"],
    }
    nc = bacc.Bacc("TRN2", target_bir_lowering=False, num_devices=1)
    arrays = {"in_" + n: np.ascontiguousarray(a) for n, a in arrays.items()}
    tensors = {n[3:]: nc.dram_tensor(n, a.shape, mybir.dt.from_np(a.dtype), kind="ExternalInput").ap() for n, a in arrays.items()}
    out = nc.dram_tensor("out", (B, S, D), F32, kind="ExternalOutput").ap()
    build(nc, tensors, out)
    return run_bass_kernel_spmd(nc, [arrays], core_ids=[0]).results[0]["out"]
```

```python
import math
from contextlib import ExitStack

import numpy as np
import concourse.bass as bass
from concourse import mybir

ALU = mybir.AluOpType
ACT = mybir.ActivationFunctionType
F32 = mybir.dt.float32
BF16 = mybir.dt.bfloat16
I32 = mybir.dt.int32
U32 = mybir.dt.uint32
U8 = mybir.dt.uint8
AX_X = mybir.AxisListType.X

B, S, D = 32, 128, 128
G = 4
NG = B // G
N = G * S
E, FF = 8, 512
FC = FF // 128
H, HD = 16, 8
HQ = 4
A, ED = 32, 16
SE, SH = 64, 128
MASKED = -1e30
TWO_PI = 2.0 * math.pi
ROUND = 12582912.0
PI_HI = 6.28125
PI_MID = 0.0019340515136718750
PI_LO = TWO_PI - PI_HI - PI_MID

COLS = {}
for _name, _width in (("ln_g", 1), ("ln_b", 1), ("hyp_b1", 1), ("hyp_b2", 1), ("sty_b1", 1), ("gamma_b", 1),
                      ("beta_b", 1), ("scale_b", 1), ("shift_b", 1), ("bq", 1), ("bk", 1), ("bo", 1), ("g2", 1),
                      ("beta2", 1), ("down_b", 1), ("ff_b1", FC), ("exp_b1", E * FC), ("head", H), ("freq", 1),
                      ("turn", 1), ("row", 1), ("count", ED)):
    COLS[_name] = (sum(w for _, w in COLS.values()), _width)
NCOL = sum(w for _, w in COLS.values())

MATS = {}
for _name, _width in (("ident", 128), ("gradT", 128), ("ngradT", 128), ("hgrad2T", 128), ("A0", 128), ("B0", 128),
                      ("A1T", 128), ("B1T", 128), ("B2T", 128), ("subj", SE), ("hyp_w1", SH), ("hyp_w2", SH),
                      ("sty_w1", SH // 2), ("sty_w2", 2 * D), ("W_ada", 2 * D), ("router", E), ("Wq", D), ("Wk", D),
                      ("Wv", D), ("Wo", D), ("W1", FF), ("W2", FC * D), ("downT", A), ("upT", D), ("expert_b", A),
                      ("domain_emb", A), ("exp_b2", D)):
    MATS[_name] = (sum(w for _, w in MATS.values()), _width)
NMAT = sum(w for _, w in MATS.values())


VEC_A = 7


class Signal:

    def __init__(self, sem, per, ahead=1):
        self.sem, self.per, self.ahead = sem, per, ahead

    def need(self, eng, g, k):
        value = g * self.per + (k + self.ahead)
        if not (isinstance(value, int) and value <= self.ahead):
            eng.wait_ge(self.sem, value)


def build(nc, t, out):
    with ExitStack() as ctx:
        def sb(name, shape, dt=F32):
            return ctx.enter_context(nc.sbuf_tensor(name, shape, dt))

        def sem(name):
            return ctx.enter_context(nc.semaphore(name))

        banks = [ctx.enter_context(nc.psum_tensor(f"bank{i}", [128, 512], F32)) for i in range(8)]

        def bank4(i):
            return banks[i][:, :].rearrange("p (b n) -> p b n", b=G)

        cols = sb("cols", [128, NCOL])
        mats = sb("mats", [128, NMAT])
        moe_w = sb("moe_w", [128, 4 * E * FF], BF16)
        parts = moe_w[:, :].rearrange("p (k n) -> p k n", k=4)
        w1_hi, w1_lo = (parts[:, k, :].rearrange("p (e f) -> p e f", e=E) for k in (0, 1))
        w2_hi, w2_lo = (parts[:, k, :].rearrange("p (e c d) -> p e c d", e=E, c=FC) for k in (2, 3))
        kh = moe_w[:, :].bitcast(F32).rearrange("p (h b s) -> p h b s", h=H, b=G)
        xall = sb("xall", [128, B, D])
        rows = sb("rows", [128, 4, D])
        ids = sb("ids", [128, 3, B], I32)
        dt_row = sb("dt_row", [128, B])
        mask_u8 = sb("mask_u8", [128, B, S], U8)
        minus_half = sb("minus_half", [128, G])
        expert_w = sb("expert_w", [ED, A, A])

        def col(name, k=0):
            c = COLS[name][0] + k
            return cols[:, c:c + 1]

        def mat(name, k=None, p=128):
            c, w = MATS[name]
            if k is not None:
                c, w = c + 128 * k, 128
            return mats[0:p, c:c + w]

        idf = sb("idf", [128, 3, B])
        onehot = sb("onehot", [128, 2, B])
        valid = sb("valid", [128, B])
        seT = sb("seT", [SE, B])
        hyp1T = sb("hyp1T", [SH, B])
        hyp2T = sb("hyp2T", [SH, B])
        sty1T = sb("sty1T", [SH // 2, B])
        gamT = sb("gamT", [128, B])
        betT = sb("betT", [128, B])
        sp = sb("sp", [128, 4, B])
        ang = sb("ang", [128, 6, B])
        scaleT = sb("scaleT", [128, B])
        shiftT = sb("shiftT", [128, B])
        onehot_v = sb("onehot_v", [ED, B])
        invalid = sb("invalid", [A, B])
        wsel = sb("wsel", [A, B, A])
        wtmp = sb("wtmp", [A, B, A])
        esel = sb("esel", [A, B])
        bq_scaled = sb("bq_scaled", [128, 1])

        st0 = sb("st0", [128, G, 6])
        mv0 = sb("mv0", [128, G, 2])
        ve0 = sb("ve0", [128, G])
        rs0 = sb("rs0", [128, G])
        xn0 = sb("xn0", [128, G, D])
        hT = sb("hT", [128, G, S])
        st1 = sb("st1", [128, G, 6])
        mv1 = sb("mv1", [128, G, 2])
        ve1 = sb("ve1", [128, G])
        rs1 = sb("rs1", [128, G])
        amp = sb("amp", [128, G])
        off = sb("off", [128, G])
        hs = sb("hs", [128, G, S])
        lg = sb("lg", [128, G, E])
        top = sb("top", [128, G, 8])
        topi = sb("topi", [128, G, 8], U32)
        sel = sb("sel", [128, 2, G, E])
        lge = sb("lge", [128, G, E])
        gate = sb("gate", [128, G, E])
        gsum = sb("gsum", [128, G])
        grec = sb("grec", [128, G])
        gateT = sb("gateT", [E, G, S])
        hs_hi = sb("hs_hi", [128, N], BF16)
        hs_lo = sb("hs_lo", [128, N], BF16)
        hid = sb("hid", [128, 2, 2, FC, N], BF16)
        hid2 = hid[:, 0, :, :, :].rearrange("p e c n -> p (e c n)").bitcast(F32).rearrange("p (c n) -> p c n", c=FC)
        pT = hid[:, 1, :, :, :].rearrange("p e c n -> p (e c n)").bitcast(F32).rearrange("p (h q) -> p h q", h=H)
        ring = sb("ring", [128, 4, N])

        f0 = sb("f0", [128, G, D])
        a0f = sb("a0f", [128, G, D])
        b0f = sb("b0f", [128, G, D])
        a1fT = sb("a1fT", [128, G, S])
        b1fT = sb("b1fT", [128, G, S])
        b2fT = sb("b2fT", [128, G, S])
        mix = sb("mix", [128, G, D])
        f1 = sb("f1", [128, G, D])
        dtc = sb("dtc", [128, G])
        adac = sb("adac", [128, 2, G])

        st2 = sb("st2", [128, G, 6])
        mv2 = sb("mv2", [128, G, 2])
        ve2 = sb("ve2", [128, G])
        rs2 = sb("rs2", [128, G])
        xn2 = sb("xn2", [128, G, D])
        xT = sb("xT", [128, G, S])
        xbT = sb("xbT", [128, G, S])
        qT = sb("qT", [128, G, S])
        kT = sb("kT", [128, G, S])
        v0 = sb("v0", [128, G, D])
        vh = sb("vh", [128, G, H, HD + 1])
        bias = sb("bias", [128, 2, H, S])
        sc = sb("sc", [128, 2, H, S])
        w1_in = sc[:, :, :, :].rearrange("p a h s -> p (a h s)")
        w2_in = bias[:, :, :, :].rearrange("p a h s -> p (a h s)")
        mx = sb("mx", [128, 2, H])
        rec = sb("rec", [128, H])
        cx = sb("cx", [128, H, HD])
        cxT = sb("cxT", [128, G, S])
        x2 = sb("x2", [128, G, D])
        x2b = sb("x2b", [128, G, D])
        st3 = sb("st3", [128, G, 6])
        mv3 = sb("mv3", [128, G, 2])
        ve3 = sb("ve3", [128, G])
        rs3 = sb("rs3", [128, G])
        xn3 = sb("xn3", [128, G, D])
        h2T = sb("h2T", [128, N])

        x3 = sb("x3", [128, G, D])
        x3T = sb("x3T", [128, N])
        hd = sb("hd", [A, G, S])
        wc = sb("wc", [A, G, A])
        ec = sb("ec", [A, G])
        h3 = sb("h3", [A + 1, G, S])
        x4 = ring[:, 0, :].rearrange("p (b d) -> p b d", b=G)
        st4 = sb("st4", [128, G, 6])
        mv4 = sb("mv4", [128, G, 2])
        ve4 = sb("ve4", [128, G])
        rs4 = sb("rs4", [128, G])
        xn4 = ring[:, 1, :].rearrange("p (b d) -> p b d", b=G)
        xg = ring[:, 2, :].rearrange("p (b d) -> p b d", b=G)
        xo = ring[:, 3, :].rearrange("p (b d) -> p b d", b=G)
        mask_c = sb("mask_c", [128, G, S])
        spare = sb("spare", [128, 1])

        in_small, in_w1, in_w2, in_mask = sem("in_small"), sem("in_w1"), sem("in_w2"), sem("in_mask")
        in_x = [sem(f"in_x{k}") for k in range(2)]
        out_done = sem("out_done")
        in_bias = [sem(f"in_bias{i}") for i in range(2)]
        once = {n: sem("s_" + n) for n in (
            "pool_const", "onehot", "se", "seT", "hyp1", "hyp1T", "hyp2", "hyp2T", "sty1", "sty1T", "sty2",
            "gam_exp", "gam_abs", "gam_ln", "ang", "sin", "silu_e", "silu", "ada", "esel", "invalid", "wtmp", "wsel_mm", "wsel",
            "w1_hi", "w1_lo", "w2_hi", "w2_lo")}
        dve_chain = sem("dve_chain")

        sig, owned = {}, {}

        def signals(owner, per, names, ahead=1):
            for n in names.split():
                sig[n] = Signal(sem(n), per, ahead)
                owned.setdefault(owner, []).append(sig[n])

        signals("dve", 1, "a_var a_xn a_var1 a_hs a_lg a_lge a_gate a_gateT a_b2x")
        signals("pool", 1, "a_rstd a_rstd1")
        signals("act", 1, "a_hT a_exp")
        signals("pe", 1, "a_xnT a_logit a_gT a_b2")
        signals("pe", E * FC, "a_hid_mm", ahead=2)
        signals("act", E * FC, "a_hid", ahead=4)
        signals("dve", E * FC, "a_hi", ahead=2)
        signals("pool", E * FC, "a_lo", ahead=4)
        signals("dve", 1, "a_hs_hi a_hs_lo")
        signals("pe", E, "a_y_mm", ahead=2)
        signals("dve", E, "a_y", ahead=2)
        signals("dve", 1, "b_prodT b_mix b_f1 b_var2 b_xn2 b_xT b_var3 b_xn3 b_x3 b_dtc b_wc b_mask b_x4 b_var4 b_xn4")
        signals("pool", 1, "b_vh b_a0f b_b0f b_xbT b_rstd2 b_rstd3 b_x2b b_rstd4 b_xg b_xo")
        signals("act", 1, "b_f0 b_qT b_v b_kT b_x2 b_h2T b_x3T b_hd b_h3")
        signals("pe", 1, "b_f0T b_t1 b_df b_xn2T b_q_mm b_k_mm b_v_mm b_x2_mm b_xn3T b_ff_mm b_x3T_mm b_down_mm b_exp_mm b_up_mm")
        signals("pe", FC, "b_ff1_mm")
        signals("act", FC, "b_hid2")
        signals("dve", H // HQ, "b_kh")
        signals("dve", G, "c_mx c_cx", ahead=3)
        signals("dve", G * (H // HQ), "c_sc", ahead=4)
        signals("pool", G, "c_sub c_bias", ahead=3)
        signals("act", G, "c_exp c_cxT", ahead=3)
        signals("pe", G, "c_ctx_mm c_cxT_mm", ahead=3)
        signals("pe", G * (H // HQ), "c_s_mm", ahead=4)
        signals("pe", G * (H // HQ), "c_pT_mm", ahead=8)
        signals("act", G * (H // HQ), "c_pT", ahead=4)
        signals("dve", VEC_A, "vec_a")
        signals("dve", 1, "a_st0 a_mv0 a_st1 a_mv1 a_amp a_off a_offs")
        signals("dve", 1, "b_f1r b_st2 b_mv2 b_st3 b_mv3 b_st4 b_mv4")
        signals("dve", G, "c_rec", ahead=3)

        def need(eng, name, g, k=1):
            sig[name].need(eng, g, k)

        def did(ins, name):
            ins.then_inc(sig[name].sem, 1)

        def start(eng, owner):
            for s in owned[owner]:
                eng.sem_inc(s.sem, s.ahead)

        def pipeline(eng, passes):
            for i in (0, 1):
                passes(i, att=True, prev=i == 1, tail=False, pre=True)
            with eng.Fori(2, NG - 1) as i:
                passes(i, att=True, prev=True, tail=True, pre=True)
            for i in (NG - 1, NG, NG + 1):
                passes(i, att=i < NG, prev=i <= NG, tail=True, pre=False)

        QB = H // HQ

        def grp(ap, g):
            return ap[:, bass.ds(g * G, G)]

        def hid_bank(g, i):
            return (3, 4, 2, 0 if isinstance(g, int) and g == NG - 1 else 7)[i % 4]

        block = ctx.enter_context(nc.Block())

        @block.sync
        def _(sync):
            sync.dma_start(cols[:, :], t["cols"]).then_inc(in_small, 16)
            sync.dma_start(mats[:, :], t["mats"]).then_inc(in_small, 16)
            sync.dma_start(ids[:, :, :].rearrange("p a b -> p (a b)"), t["ids"].partition_broadcast(128)).then_inc(in_small, 16)
            sync.dma_start(dt_row[:, :], t["dt"].partition_broadcast(128)).then_inc(in_small, 16)
            sync.dma_start(rows[:, :, :].rearrange("p a b -> p (a b)"), t["rows"].partition_broadcast(128)).then_inc(in_small, 16)
            sync.dma_start(expert_w[:, :, :], t["expert_w"]).then_inc(in_small, 16)
            sync.dma_start(xall[:, 0:G, :], t["x"][0:G].rearrange("b s d -> s b d")).then_inc(in_x[0], 16)
            sync.dma_start(w1_in.rearrange("p (e f) -> p e f", e=E), t["w1"].rearrange("e d f -> d e f")).then_inc(in_w1, 16)
            sync.dma_start(w2_in.rearrange("p (e d) -> p e d", d=D), t["w2"].rearrange("e (c p) d -> p (e c) d", p=128)).then_inc(in_w2, 16)
            sync.dma_start(xall[:, G:B, :], t["x"][G:B].rearrange("b s d -> s b d")).then_inc(in_x[1], 16)
            sync.sem_inc(out_done, 16)
            sync.dma_start(mask_u8[:, :, :], t["mask"].rearrange("b o q k -> q (b o) k")).then_inc(in_mask, 16)
            def store(g):
                need(sync, "b_xo", g)
                sync.dma_start(out[G * g:G * g + G].rearrange("b s d -> s b d"), xo[:, :, :]).then_inc(out_done, 16)

            for i in range(B):
                if i % G == 1 and i // G >= 3:
                    store(i // G - 3)
                if i == 0:
                    sync.wait_ge(once["w2_hi"], 1)
                    sync.wait_ge(once["w2_lo"], 1)
                if i >= 2:
                    need(sync, "c_sc", 0, QB * (i - 1))
                sync.dma_start(bias[:, i % 2, :, :], t["bias"][i].rearrange("h q k -> q h k")).then_inc(in_bias[i % 2], 16)

            for g in range(NG - 3, NG):
                store(g)
            sync.wait_ge(out_done, 16 * (NG + 1))

        @block.gpsimd
        def _(pool):
            start(pool, "pool")
            pool.memset(minus_half[:, :], -0.5).then_inc(once["pool_const"], 1)
            pool.memset(vh[:, :, :, :], 1.0).then_inc(once["pool_const"], 1)
            pool.memset(h3[:, :, :], 1.0).then_inc(once["pool_const"], 1)
            pool.wait_ge(once["pool_const"], 3)

            def rstd(g, var, ve, rs, out_sig):
                need(pool, var, g)
                did(pool.tensor_tensor(rs[:, :], ve[:, :], minus_half[:, :], ALU.pow), out_sig)

            pool.wait_ge(once["invalid"], 1)
            pool.tensor_tensor(wtmp[:, :, :], mats[0:A, 0:A].unsqueeze(1).to_broadcast([A, B, A]),
                               invalid[:, :].unsqueeze(2).to_broadcast([A, B, A]), ALU.mult).then_inc(once["wtmp"], 1)
            rstd(0, "a_var", ve0, rs0, "a_rstd")
            rstd(0, "a_var1", ve1, rs1, "a_rstd1")
            pool.wait_ge(once["w2_hi"], 1)
            pool.tensor_tensor(parts[:, 3, :], w2_in, parts[:, 2, :], ALU.subtract).then_inc(once["w2_lo"], 1)

            def low_part(g, i):
                e, c = divmod(i, FC)
                need(pool, "a_hi", g, i + 1)
                need(pool, "a_y_mm", g, e - 1)
                did(pool.tensor_tensor(hid[:, 1, e % 2, c, :], ring[:, i % 4, :], hid[:, 0, e % 2, c, :], ALU.subtract), "a_lo")

            def layer0(g, more):
                for i in range(FC, E * FC):
                    low_part(g, i)
                    if more and i == FC * 3 - 1:
                        rstd(g + 1, "a_var", ve0, rs0, "a_rstd")
                    if more and i == FC * 5 - 1:
                        rstd(g + 1, "a_var1", ve1, rs1, "a_rstd1")
                    if not more and i == FC * 2 - 1:
                        grid_products(0)
                    if not more and i == FC * 6 - 1:
                        rstd(0, "b_var2", ve2, rs2, "b_rstd2")
                if more:
                    for i in range(FC):
                        low_part(g + 1, i)

            for i in range(FC):
                low_part(0, i)
            with pool.Fori(0, NG - 1) as g:
                layer0(g, True)
            def grid_products(g):
                need(pool, "b_f0", g)
                need(pool, "b_mix", g - 1)
                did(pool.tensor_tensor(a0f[:, :, :], f0[:, :, :], mat("A0").unsqueeze(1).to_broadcast([128, G, D]), ALU.mult), "b_a0f")
                need(pool, "b_df", g - 1)
                did(pool.tensor_tensor(b0f[:, :, :], f0[:, :, :], mat("B0").unsqueeze(1).to_broadcast([128, G, D]), ALU.mult), "b_b0f")

            def passes(i, att, prev, tail, pre):
                if att:
                    mask_bias(i, 1)
                if pre:
                    grid_products(i + 1)
                if att:
                    subtract(i, 0)
                    mask_bias(i, 2)
                    subtract(i, 1)
                if att:
                    need(pool, "b_v", i)
                    need(pool, "c_ctx_mm", i, 0)
                    for b in range(G):
                        last = pool.tensor_tensor(vh[:, b, :, 0:HD], v0[:, b, :].rearrange("p (h d) -> p h d", h=H),
                                                  rows[:, 0, :].rearrange("p (h d) -> p h d", h=H), ALU.add)
                    did(last, "b_vh")
                if pre:
                    rstd(i + 1, "b_var2", ve2, rs2, "b_rstd2")
                if att:
                    mask_bias(i, 3)
                    need(pool, "b_xT", i)
                    need(pool, "b_x2_mm", i, 0)
                    did(pool.tensor_tensor(xbT[:, :, :], xT[:, :, :], col("bo").unsqueeze(2).to_broadcast([128, G, S]), ALU.add), "b_xbT")
                    subtract(i, 2)
                if prev:
                    rstd(i - 1, "b_var3", ve3, rs3, "b_rstd3")
                if tail:
                    rstd(i - 2, "b_var4", ve4, rs4, "b_rstd4")
                if pre:
                    mask_bias(i + 1, 0)
                if att:
                    subtract(i, 3)
                if prev:
                    need(pool, "b_x2", i - 1)
                    need(pool, "b_x3", i - 2)
                    did(pool.tensor_tensor(x2b[:, :, :], x2[:, :, :], rows[:, 1, :].unsqueeze(1).to_broadcast([128, G, D]), ALU.add), "b_x2b")
                if tail:
                    need(pool, "b_xn4", i - 2)
                    need(pool, "b_xo", i - 3)
                    did(pool.tensor_tensor(xg[:, :, :], xn4[:, :, :], rows[:, 2, :].unsqueeze(1).to_broadcast([128, G, D]), ALU.mult), "b_xg")
                    need(pool, "b_xg", i - 2)
                    pool.wait_ge(out_done, 16 * (i - 1))
                    did(pool.tensor_tensor(xo[:, :, :], xg[:, :, :], rows[:, 3, :].unsqueeze(1).to_broadcast([128, G, D]), ALU.add), "b_xo")

            def mask_bias(i, b):
                pool.wait_ge(in_bias[b % 2], (i * (G // 2) + (b // 2 + 1)) * 16)
                need(pool, "b_mask", i)
                did(pool.tensor_tensor(bias[:, b % 2, :, :], bias[:, b % 2, :, :],
                                       mask_c[:, b, :].unsqueeze(1).to_broadcast([128, H, S]), ALU.add), "c_bias")

            def subtract(i, b):
                need(pool, "c_mx", i, b + 1)
                did(pool.tensor_tensor(sc[:, b % 2, :, :], sc[:, b % 2, :, :],
                                       mx[:, b % 2, :].unsqueeze(2).to_broadcast([128, H, S]), ALU.subtract), "c_sub")

            layer0(NG - 1, False)
            mask_bias(0, 0)
            pipeline(pool, passes)

        @block.vector
        def _(dve):
            start(dve, "dve")
            n = 0

            def chain(ins):
                nonlocal n
                n += 1
                ins.then_inc(dve_chain, 1)
                dve.wait_ge(dve_chain, n)

            dve.wait_ge(in_small, 16 * 6)
            chain(dve.tensor_copy(idf[:, :, :], ids[:, :, :]))
            dve.tensor_scalar(sp[:, 0, :], idf[:, 2, :], 0.0, None, ALU.is_ge)
            chain(dve.tensor_scalar(sp[:, 1, :], idf[:, 2, :], float(ED - 1), None, ALU.is_le))
            dve.tensor_tensor(valid[:, :], sp[:, 0, :], sp[:, 1, :], ALU.mult)
            dve.tensor_scalar(idf[:, 0, :], idf[:, 0, :], 0.0, 31.0, ALU.max, ALU.min)
            chain(dve.tensor_scalar(idf[:, 2, :], idf[:, 2, :], 0.0, float(ED - 1), ALU.max, ALU.min))
            dve.tensor_scalar(onehot[:, 0, :], idf[:, 0, :], col("row"), None, ALU.is_equal)
            chain(dve.tensor_scalar(onehot[:, 1, :], idf[:, 2, :], col("row"), None, ALU.is_equal))
            dve.tensor_scalar(invalid[:, :], valid[0:A, :], -1.0, 1.0, ALU.mult, ALU.add).then_inc(once["invalid"], 1)
            chain(dve.tensor_tensor(onehot_v[:, :], onehot[0:ED, 1, :], valid[0:ED, :], ALU.mult))
            dve.tensor_scalar(sp[:, 0, :], idf[:, 1, :], 0.01, 4000.0, ALU.mult, ALU.mult).then_inc(once["onehot"], 1)
            dve.wait_ge(once["onehot"], 1)
            chain(dve.tensor_scalar(ang[:, 0, :], sp[:, 0, :], col("freq"), None, ALU.mult))
            chain(dve.tensor_scalar(ang[:, 1, :], ang[:, 0, :], 1.0 / TWO_PI, col("turn"), ALU.mult, ALU.add))
            chain(dve.tensor_scalar(ang[:, 1, :], ang[:, 1, :], ROUND, None, ALU.add))
            chain(dve.tensor_scalar(ang[:, 1, :], ang[:, 1, :], ROUND, None, ALU.subtract))
            chain(dve.scalar_tensor_tensor(ang[:, 2, :], ang[:, 1, :], -PI_HI, ang[:, 0, :], ALU.mult, ALU.add))
            chain(dve.scalar_tensor_tensor(ang[:, 0, :], ang[:, 1, :], -PI_MID, ang[:, 2, :], ALU.mult, ALU.add))
            chain(dve.scalar_tensor_tensor(ang[:, 2, :], ang[:, 1, :], -PI_LO, ang[:, 0, :], ALU.mult, ALU.add))
            chain(dve.tensor_scalar(ang[:, 3, :], col("turn").to_broadcast([128, B]), TWO_PI, None, ALU.mult))
            chain(dve.tensor_tensor(ang[:, 3, :], ang[:, 3, :], ang[:, 2, :], ALU.add))
            dve.tensor_scalar(ang[:, 3, :], ang[:, 3, :], 3.1415925, -3.1415925, ALU.min, ALU.max).then_inc(once["ang"], 1)

            linked = 0

            def link(ins, name, g):
                nonlocal linked
                linked += 1
                did(ins, name)
                need(dve, name, g, linked)

            def moments(srcs, st, mv, ve, eps, g, signal_stats, signal_means, ready):
                for b, src in enumerate(srcs):
                    last = dve.bn_stats(st[:, b, :], src)
                did(last, signal_stats)
                need(dve, signal_stats, g)
                dve.nop(nofuse=True)
                for b in range(G):
                    last = dve.bn_aggr(mv[:, b, :], st[:, b, :])
                did(last, signal_means)
                need(dve, signal_means, g)
                did(dve.tensor_scalar(ve[:, :], mv[:, :, 1], eps, None, ALU.add), ready)

            def x_of(g, b):
                return xall[:, bass.ds(g * G + b, 1), :].rearrange("p o d -> p (o d)")

            def feature_moments(g):
                moments([x_of(g, b) for b in range(G)], st0, mv0, ve0, 1e-5, g, "a_st0", "a_mv0", "a_var")

            def norm_features(g):
                need(dve, "a_xnT", g, 0)
                need(dve, "a_rstd", g)
                for b in range(G):
                    last = dve.tensor_scalar(xn0[:, b, :], x_of(g, b), mv0[:, b, 0:1], rs0[:, b:b + 1], ALU.subtract, ALU.mult)
                did(last, "a_xn")

            def position_moments(g):
                need(dve, "a_hT", g)
                moments([hT[:, b, :] for b in range(G)], st1, mv1, ve1, 1e-8, g, "a_st1", "a_mv1", "a_var1")

            def norm_positions(g):
                need(dve, "a_rstd1", g)
                did(dve.tensor_tensor(amp[:, :], rs1[:, :], grp(gamT, g), ALU.mult), "a_amp")
                need(dve, "a_amp", g)
                did(dve.tensor_tensor(off[:, :], mv1[:, :, 0], amp[:, :], ALU.mult), "a_off")

            def style(g):
                need(dve, "a_off", g)
                did(dve.tensor_tensor(off[:, :], grp(betT, g), off[:, :], ALU.subtract), "a_offs")
                need(dve, "a_offs", g)
                need(dve, "a_hid_mm", g, 0)
                for b in range(G):
                    last = dve.tensor_scalar(hs[:, b, :], hT[:, b, :], amp[:, b:b + 1], off[:, b:b + 1], ALU.mult, ALU.add)
                did(last, "a_hs")
                need(dve, "a_hs", g)
                did(dve.tensor_copy(hs_hi[:, :], hs[:, :, :].rearrange("p b s -> p (b s)")), "a_hs_hi")
                need(dve, "a_hs_hi", g)
                did(dve.tensor_tensor(hs_lo[:, :], hs[:, :, :].rearrange("p b s -> p (b s)"), hs_hi[:, :], ALU.subtract), "a_hs_lo")

            def high_parts(g, e):
                for c in range(FC):
                    i = FC * e + c
                    need(dve, "a_hid", g, i + 1)
                    if c == 0:
                        need(dve, "a_y_mm", g, e - 1)
                    did(dve.tensor_copy(hid[:, 0, e % 2, c, :], ring[:, i % 4, :]), "a_hi")

            def gates(g):
                need(dve, "a_logit", g)
                did(dve.tensor_copy(lg[:, :, :], banks[1][:, 0:G * E].rearrange("p (b e) -> p b e", b=G)), "a_lg")
                need(dve, "a_lg", g)
                dve.nop(nofuse=True)
                for b in range(G):
                    last = dve.max(top[:, b, :], lg[:, b, :])
                link(last, "vec_a", g)
                did(dve.tensor_tensor(lge[:, :, :], lg[:, :, :], top[:, :, 0:1].to_broadcast([128, G, E]), ALU.subtract), "a_lge")
                for b in range(G):
                    last = dve.max_index(topi[:, b, :], top[:, b, :], lg[:, b, :])
                link(last, "vec_a", g)
                high_parts(g, 1)
                c0 = COLS["count"][0]
                for k in range(2):
                    last = dve.tensor_tensor(sel[:, k, :, :], cols[:, c0:c0 + E].unsqueeze(1).to_broadcast([128, G, E]),
                                             topi[:, :, k:k + 1].to_broadcast([128, G, E]), ALU.is_equal)
                link(last, "vec_a", g)
                link(dve.tensor_tensor(sel[:, 0, :, :], sel[:, 0, :, :], sel[:, 1, :, :], ALU.add), "vec_a", g)
                need(dve, "a_exp", g)
                link(dve.tensor_tensor(sel[:, 1, :, :], sel[:, 0, :, :], lge[:, :, :], ALU.mult), "vec_a", g)
                link(dve.tensor_reduce(gsum[:, :], sel[:, 1, :, :], AX_X, ALU.add), "vec_a", g)
                link(dve.reciprocal(grec[:, :], gsum[:, :]), "vec_a", g)
                did(dve.tensor_tensor(gate[:, :, :], sel[:, 1, :, :], grec[:, :].unsqueeze(2).to_broadcast([128, G, E]), ALU.mult), "a_gate")

            def layer0(g, more):
                nonlocal linked
                linked = 0
                gates(g)
                need(dve, "a_gate", g)
                for e in range(E):
                    if 1 <= e < E - 1:
                        high_parts(g, e + 1)
                    if more and e == E - 2:
                        style(g + 1)
                    if more and e == E - 1:
                        high_parts(g + 1, 0)
                    if e == 1:
                        need(dve, "a_gT", g)
                        did(dve.tensor_copy(gateT[:, :, :], banks[1][0:E, :].rearrange("e (b s) -> e b s", b=G)), "a_gateT")
                    if e == 2:
                        need(dve, "a_b2", g)
                        need(dve, "a_y", g, e)
                        did(dve.tensor_tensor(grp(xall, g), bank4(1), grp(xall, g), ALU.add), "a_b2x")
                        need(dve, "a_b2x", g)
                    need(dve, "a_y_mm", g, e + 1)
                    if e:
                        need(dve, "a_y", g, e)
                    for b in range(G):
                        last = dve.scalar_tensor_tensor(x_of(g, b), bank4(5 + e % 2)[:, b, :], gate[:, b, e:e + 1], x_of(g, b),
                                                        ALU.mult, ALU.add)
                    did(last, "a_y")
                    if not more:
                        if e == 1:
                            columns(0)
                            grid_products(0)
                        if e == 2:
                            mixed(0)
                        if e == 4:
                            stepped(0)
                            stepped_moments(0)
                        if e == 5:
                            normed(0)
                        if e == 6:
                            conditioned(0)
                    if more and e == 1:
                        feature_moments(g + 1)
                    if more and e == 2:
                        norm_features(g + 1)
                    if more and e == 3:
                        position_moments(g + 1)
                    if more and e == 4:
                        norm_positions(g + 1)

            dve.wait_ge(once["se"], 1)
            dve.tensor_copy(seT[:, :], banks[0][0:SE, 0:B]).then_inc(once["seT"], 1)
            dve.wait_ge(in_x[0], 16)
            feature_moments(0)
            dve.wait_ge(once["hyp1"], 1)
            dve.tensor_scalar(hyp1T[:, :], banks[1][:, 0:B], col("hyp_b1"), 0.0, ALU.add, ALU.max).then_inc(once["hyp1T"], 1)
            norm_features(0)
            dve.wait_ge(once["hyp2"], 1)
            dve.tensor_scalar(hyp2T[:, :], banks[2][:, 0:B], col("hyp_b2"), None, ALU.add).then_inc(once["hyp2T"], 1)
            dve.wait_ge(once["sty1"], 1)
            dve.tensor_scalar(sty1T[:, :], banks[3][0:SH // 2, 0:B], col("sty_b1")[0:SH // 2], 0.0, ALU.add, ALU.max).then_inc(once["sty1T"], 1)
            dve.wait_ge(once["sty2"], 1)
            chain(dve.tensor_scalar(gamT[:, :], banks[4][:, 0:B], col("gamma_b"), None, ALU.add))
            dve.tensor_scalar(betT[:, :], banks[4][:, B:2 * B], col("beta_b"), None, ALU.add)
            chain(dve.tensor_scalar(sp[:, 1, :], gamT[:, :], -1.0, None, ALU.mult))
            dve.tensor_tensor(sp[:, 1, :], gamT[:, :], sp[:, 1, :], ALU.max).then_inc(once["gam_abs"], 1)
            chain(dve.tensor_scalar(sp[:, 0, :], gamT[:, :], 0.0, 1e-8, ALU.max, ALU.add))
            dve.wait_ge(once["silu_e"], 1)
            chain(dve.tensor_scalar(ang[:, 5, :], ang[:, 5, :], 1.0, None, ALU.add))
            chain(dve.reciprocal(ang[:, 5, :], ang[:, 5, :]))
            dve.tensor_tensor(ang[:, 4, :], ang[:, 4, :], ang[:, 5, :], ALU.mult).then_inc(once["silu"], 1)
            dve.tensor_scalar(bq_scaled[:, :], col("bq"), 1.0 / math.sqrt(HD), None, ALU.mult)
            position_moments(0)
            dve.wait_ge(once["ada"], 1)
            dve.tensor_scalar(scaleT[:, :], banks[5][:, 0:B], col("scale_b"), 1.0, ALU.add, ALU.add)
            dve.tensor_scalar(shiftT[:, :], banks[5][:, B:2 * B], col("shift_b"), None, ALU.add)
            dve.wait_ge(once["esel"], 1)
            dve.tensor_copy(esel[:, :], banks[3][0:A, B:2 * B])
            dve.wait_ge(once["wsel_mm"], 1)
            dve.wait_ge(once["wtmp"], 1)
            for k in range(2):
                half = slice(k * (A // 2), (k + 1) * (A // 2))
                last = dve.tensor_tensor(wsel[:, :, half], banks[6 + k][0:A, :].rearrange("p (o b) -> p b o", b=B), wtmp[:, :, half], ALU.add)
            chain(last)
            dve.sem_inc(once["wsel"], 1)
            dve.wait_ge(once["gam_ln"], 1)
            chain(dve.tensor_tensor(gamT[:, :], sp[:, 0, :], sp[:, 3, :], ALU.add))
            norm_positions(0)
            style(0)
            dve.wait_ge(once["w1_hi"], 1)
            dve.tensor_tensor(parts[:, 1, :], w1_in, parts[:, 0, :], ALU.subtract).then_inc(once["w1_lo"], 1)
            high_parts(0, 0)
            dve.wait_ge(in_x[1], 16)
            dve.wait_ge(in_mask, 16)
            with dve.Fori(0, NG - 1) as g:
                layer0(g, True)

            def scores(i, b):
                biased(i, b)
                maximum(i, b)

            def biased(i, b):
                need(dve, "c_bias", i, b + 1)
                for r in range(QB):
                    need(dve, "c_pT_mm", i, (b - 2) * QB + r + 1)
                    need(dve, "c_s_mm", i, QB * b + r + 1)
                    did(dve.tensor_tensor(sc[:, b % 2, HQ * r:HQ * r + HQ, :], banks[r][:, :].rearrange("p (h k) -> p h k", h=HQ),
                                          bias[:, b % 2, HQ * r:HQ * r + HQ, :], ALU.add), "c_sc")

            def maximum(i, b):
                need(dve, "c_sc", i, QB * (b + 1))
                need(dve, "c_sub", i, b - 1)
                did(dve.tensor_reduce(mx[:, b % 2, :], sc[:, b % 2, :, :], AX_X, ALU.max), "c_mx")

            def mask(i):
                need(dve, "c_bias", i, 0)
                did(dve.tensor_scalar(mask_c[:, :, :], grp(mask_u8, i), MASKED, None, ALU.mult), "b_mask")

            def context(i, b):
                need(dve, "c_ctx_mm", i, b + 1)
                pv = banks[6][:, 0:H * (HD + 1)].rearrange("p (h d) -> p h d", h=H)
                did(dve.reciprocal(rec[:, :], pv[:, :, HD]), "c_rec")
                need(dve, "c_rec", i, b + 1)
                need(dve, "c_cxT_mm", i, b)
                did(dve.tensor_tensor(cx[:, :, :], pv[:, :, 0:HD], rec[:, :].unsqueeze(2).to_broadcast([128, H, HD]), ALU.mult), "c_cx")

            def keys(r):
                for h in range(HQ * r, HQ * r + HQ):
                    last = dve.tensor_scalar(kh[:, h, :, :], kT[:, :, :], col("head", h), None, ALU.mult)
                did(last, "b_kh")

            def columns(g):
                dve.tensor_copy(dtc[:, :], grp(dt_row, g))
                dve.tensor_copy(adac[:, 0, :], grp(scaleT, g))
                did(dve.tensor_copy(adac[:, 1, :], grp(shiftT, g)), "b_dtc")

            def grid_products(g):
                need(dve, "b_f0T", g)
                for dst, grid in ((b2fT, "B2T"), (a1fT, "A1T"), (b1fT, "B1T")):
                    last = dve.tensor_tensor(dst[:, :, :], bank4(7), mat(grid).unsqueeze(1).to_broadcast([128, G, S]), ALU.mult)
                did(last, "b_prodT")

            def mixed(g):
                need(dve, "b_t1", g)
                need(dve, "b_a0f", g)
                did(dve.tensor_tensor(mix[:, :, :], bank4(7), a0f[:, :, :], ALU.subtract), "b_mix")

            def stepped(g):
                need(dve, "b_df", g)
                need(dve, "b_dtc", g)
                for b in range(G):
                    last = dve.scalar_tensor_tensor(f1[:, b, :], bank4(7)[:, b, :], dtc[:, b:b + 1], f0[:, b, :], ALU.mult, ALU.add)
                did(last, "b_f1r")
                need(dve, "b_f1r", g)
                did(dve.tensor_scalar(f1[:, :, :], f1[:, :, :], 0.0, None, ALU.max), "b_f1")

            def stepped_moments(g):
                need(dve, "b_f1", g)
                moments([f1[:, b, :] for b in range(G)], st2, mv2, ve2, 1e-5, g, "b_st2", "b_mv2", "b_var2")

            def normed(g):
                need(dve, "b_rstd2", g)
                for b in range(G):
                    last = dve.tensor_scalar(xn2[:, b, :], f1[:, b, :], mv2[:, b, 0:1], rs2[:, b:b + 1], ALU.subtract, ALU.mult)
                did(last, "b_xn2")

            def conditioned(g):
                need(dve, "b_xn2T", g)
                need(dve, "b_xbT", g - 1)
                for b in range(G):
                    last = dve.tensor_scalar(xT[:, b, :], bank4(7)[:, b, :], adac[:, 0, b:b + 1], adac[:, 1, b:b + 1], ALU.mult, ALU.add)
                did(last, "b_xT")

            def feed_forward_moments(g):
                need(dve, "b_x2", g)
                moments([x2[:, b, :] for b in range(G)], st3, mv3, ve3, 1e-5, g, "b_st3", "b_mv3", "b_var3")

            def feed_forward_norm(g):
                need(dve, "b_rstd3", g)
                for b in range(G):
                    last = dve.tensor_scalar(xn3[:, b, :], x2[:, b, :], mv3[:, b, 0:1], rs3[:, b:b + 1], ALU.subtract, ALU.mult)
                did(last, "b_xn3")

            def passes(i, att, prev, tail, pre):
                if pre:
                    columns(i + 1)
                if tail:
                    dve.tensor_copy(wc[:, :, :], grp(wsel, i - 2))
                    did(dve.tensor_copy(ec[:, :], grp(esel, i - 2)), "b_wc")
                if att:
                    biased(i, 0)
                    if tail or not prev:
                        maximum(i, 0)
                if pre:
                    grid_products(i + 1)
                if att and prev and not tail:
                    maximum(i, 0)
                if tail:
                    need(dve, "b_ff_mm", i - 2)
                    need(dve, "b_x2b", i - 2)
                    did(dve.tensor_tensor(x3[:, :, :], bank4(5), x2b[:, :, :], ALU.add), "b_x3")
                if prev:
                    context(i - 1, 2)
                if pre:
                    mixed(i + 1)
                if att:
                    scores(i, 1)
                if pre:
                    stepped(i + 1)
                if prev:
                    context(i - 1, 3)
                if pre:
                    stepped_moments(i + 1)
                if pre:
                    normed(i + 1)
                if att:
                    scores(i, 2)
                if pre:
                    mask(i + 1)
                if att:
                    context(i, 0)
                if prev and not att:
                    feed_forward_moments(i - 1)
                if tail:
                    need(dve, "b_up_mm", i - 2)
                    did(dve.tensor_tensor(x4[:, :, :], bank4(5), x3[:, :, :], ALU.add), "b_x4")
                if prev and att:
                    feed_forward_moments(i - 1)
                elif prev:
                    feed_forward_norm(i - 1)
                if pre:
                    conditioned(i + 1)
                if tail:
                    need(dve, "b_x4", i - 2)
                    moments([x4[:, b, :] for b in range(G)], st4, mv4, ve4, 1e-5, i - 2, "b_st4", "b_mv4", "b_var4")
                if prev and att:
                    feed_forward_norm(i - 1)
                if att:
                    scores(i, 3)
                if tail:
                    need(dve, "b_rstd4", i - 2)
                    need(dve, "b_xg", i - 3)
                    for b in range(G):
                        last = dve.tensor_scalar(xn4[:, b, :], x4[:, b, :], mv4[:, b, 0:1], rs4[:, b:b + 1], ALU.subtract, ALU.mult)
                    did(last, "b_xn4")
                if pre:
                    need(dve, "c_s_mm", i + 1, 0)
                    need(dve, "b_kT", i + 1)
                for r in range(QB):
                    if att and r == (2 if prev else 1):
                        context(i, 1)
                    if pre:
                        keys(r)

            layer0(NG - 1, False)
            assert linked == VEC_A, linked
            mask(0)
            need(dve, "b_kT", 0)
            for r in range(QB):
                keys(r)
            pipeline(dve, passes)

        @block.scalar
        def _(act):
            start(act, "act")
            act.wait_ge(in_small, 16 * 6)
            act.wait_ge(once["ang"], 1)
            act.activation(ang[:, 4, :], ang[:, 3, :], ACT.Sin).then_inc(once["sin"], 1)
            act.wait_ge(once["sin"], 1)
            act.activation(ang[:, 5, :], ang[:, 4, :], ACT.Exp, scale=-1.0).then_inc(once["silu_e"], 1)

            def transposed(g):
                need(act, "a_xnT", g)
                need(act, "a_hs", g, 0)
                did(act.activation(hT[:, :, :].rearrange("p b s -> p (b s)"), banks[0][:, :], ACT.Identity, bias=col("ln_b"), scale=col("ln_g")), "a_hT")

            def hidden(g, i):
                need(act, "a_hid_mm", g, i + 1)
                need(act, "a_lo", g, i - 3)
                did(act.activation(ring[:, i % 4, :], banks[hid_bank(g, i)][:, :], ACT.Relu, bias=col("exp_b1", i)), "a_hid")

            def layer0(g, more):
                for i in range(FC, E * FC):
                    if i == FC + 1:
                        need(act, "a_lge", g)
                        did(act.activation(lge[:, :, :], lge[:, :, :], ACT.Exp), "a_exp")
                    hidden(g, i)
                    if not more and i == FC:
                        need(act, "a_y", 0, E)
                        copied(0)
                    if more and i == FC * 5 - 1:
                        transposed(g + 1)
                if more:
                    for i in range(FC):
                        hidden(g + 1, i)

            act.wait_ge(once["gam_abs"], 1)
            act.activation(sp[:, 2, :], sp[:, 1, :], ACT.Exp, scale=-1.0).then_inc(once["gam_exp"], 1)
            act.wait_ge(once["gam_exp"], 1)
            act.activation(sp[:, 3, :], sp[:, 2, :], ACT.Ln, bias=1.0).then_inc(once["gam_ln"], 1)
            transposed(0)
            act.wait_ge(in_w1, 16)
            act.activation(parts[:, 0, :], w1_in, ACT.Copy).then_inc(once["w1_hi"], 1)
            act.wait_ge(in_w2, 16)
            act.activation(parts[:, 2, :], w2_in, ACT.Copy).then_inc(once["w2_hi"], 1)
            for i in range(FC):
                hidden(0, i)
            with act.Fori(0, NG - 1) as g:
                layer0(g, True)
            def evacuate(i, b, then=None):
                for r in range(QB):
                    need(act, "c_pT_mm", i, b * QB + r + 1)
                    if r == 0:
                        need(act, "c_ctx_mm", i, b)
                    did(act.activation(pT[:, HQ * r:HQ * r + HQ, :], banks[4 + r % 2][:, :].rearrange("p (h q) -> p h q", h=HQ), ACT.Copy), "c_pT")
                    if r == 1 and then:
                        softmax(*then)

            def context_T(i, b):
                need(act, "c_cxT_mm", i, b + 1)
                if b == 0:
                    need(act, "b_x2_mm", i, 0)
                did(act.activation(cxT[:, b, :], banks[6][:, 0:S], ACT.Copy), "c_cxT")

            def softmax(i, b):
                need(act, "c_sub", i, b + 1)
                did(act.activation(sc[:, b % 2, :, :], sc[:, b % 2, :, :], ACT.Exp), "c_exp")

            def copied(g):
                need(act, "b_f1", g - 1)
                need(act, "b_b0f", g - 1)
                did(act.activation(f0[:, :, :], grp(xall, g), ACT.Copy), "b_f0")

            def projected(g):
                need(act, "b_k_mm", g)
                need(act, "b_kh", g - 1, QB)
                did(act.activation(kT[:, :, :], bank4(7), ACT.Identity, bias=col("bk")), "b_kT")
                need(act, "b_q_mm", g)
                need(act, "c_s_mm", g, 0)
                did(act.activation(qT[:, :, :], bank4(4), ACT.Identity, bias=bq_scaled[:, :], scale=1.0 / math.sqrt(HD)), "b_qT")

            def table_of(function):
                act.activation(spare[:, :], col("ln_g"), function)

            def value(g):
                need(act, "b_v_mm", g)
                need(act, "b_vh", g - 1)
                did(act.activation(v0[:, :, :], bank4(7), ACT.Copy), "b_v")

            def passes(i, att, prev, tail, pre):
                if pre:
                    copied(i + 1)
                if prev:
                    evacuate(i - 1, 2, then=(i - 1, 3))
                if tail:
                    need(act, "b_x3T_mm", i - 2)
                    did(act.activation(x3T[:, :], banks[5][:, :], ACT.Copy), "b_x3T")
                if prev:
                    context_T(i - 1, 2)
                if prev:
                    evacuate(i - 1, 3, then=(i, 0) if att else None)
                elif att:
                    softmax(i, 0)
                if tail:
                    need(act, "b_down_mm", i - 2)
                    did(act.activation(hd[:, :, :].rearrange("a b s -> a (b s)"), banks[5][0:A, :], ACT.Gelu, bias=col("down_b")[0:A]), "b_hd")
                    need(act, "b_exp_mm", i - 2)
                    for b in range(G):
                        last = act.activation(h3[0:A, b, :], banks[5][0:A, b * S:(b + 1) * S], ACT.Identity, bias=ec[:, b:b + 1])
                    did(last, "b_h3")
                if prev:
                    context_T(i - 1, 3)
                if att:
                    evacuate(i, 0, then=(i, 1))
                if prev:
                    need(act, "b_x2_mm", i - 1)
                    need(act, "b_x2b", i - 2)
                    did(act.activation(x2[:, :, :], bank4(7), ACT.Copy), "b_x2")
                    if not att:
                        table_of(ACT.Gelu_apprx_sigmoid)
                if att:
                    context_T(i, 0)
                if att:
                    evacuate(i, 1, then=(i, 2))
                if prev:
                    need(act, "b_xn3T", i - 1)
                    did(act.activation(h2T[:, :], banks[5][:, :], ACT.Identity, bias=col("beta2"), scale=col("g2")), "b_h2T")
                if pre:
                    projected(i + 1)
                for c in range(FC):
                    if pre and c == 2:
                        value(i + 1)
                    if prev:
                        need(act, "b_ff1_mm", i - 1, c + 1)
                        did(act.activation(hid2[:, c, :], banks[4 + c % 2][:, :], ACT.Gelu_apprx_sigmoid, bias=col("ff_b1", c)), "b_hid2")
                if prev and not att:
                    table_of(ACT.Gelu)
                if att:
                    context_T(i, 1)

            layer0(NG - 1, False)
            need(act, "a_y", NG, 0)
            projected(0)
            value(0)
            pipeline(act, passes)

        @block.tensor
        def _(pe):
            start(pe, "pe")
            pe.wait_ge(in_small, 16 * 6)
            pe.wait_ge(once["onehot"], 1)
            pe.matmul(banks[0][0:SE, 0:B], mat("subj", p=32), onehot[0:32, 0, :], start=True, stop=True).then_inc(once["se"], 1)
            pe.wait_ge(once["seT"], 1)
            pe.matmul(banks[1][:, 0:B], mat("hyp_w1", p=SE), seT[:, :], start=True, stop=True).then_inc(once["hyp1"], 1)
            pe.wait_ge(once["hyp1T"], 1)
            pe.matmul(banks[2][:, 0:B], mat("hyp_w2"), hyp1T[:, :], start=True, stop=True).then_inc(once["hyp2"], 1)
            pe.wait_ge(once["hyp2T"], 1)
            pe.matmul(banks[3][0:SH // 2, 0:B], mat("sty_w1"), hyp2T[:, :], start=True, stop=True).then_inc(once["sty1"], 1)
            pe.wait_ge(once["sty1T"], 1)
            for k in range(2):
                last = pe.matmul(banks[4][:, B * k:B * k + B], mat("sty_w2", k, p=SH // 2), sty1T[:, :], start=True, stop=True)
            last.then_inc(once["sty2"], 1)

            def transposes(g):
                need(pe, "a_xn", g)
                need(pe, "a_hT", g, 0)
                for b in range(G):
                    last = pe.transpose(bank4(0)[:, b, :], xn0[:, b, :], mat("ident"))
                did(last, "a_xnT")

            def logits(g):
                need(pe, "a_hs", g)
                need(pe, "a_b2x", g, 0)
                for b in range(G):
                    last = pe.matmul(banks[1][:, b * E:(b + 1) * E], hs[:, b, :], mat("router"), start=True, stop=True)
                did(last, "a_logit")

            def first(g, i):
                e, c = divmod(i, FC)
                if i == 0:
                    need(pe, "a_hs_lo", g)
                need(pe, "a_hid", g, i - 3)
                bank, at = banks[hid_bank(g, i)], slice(128 * c, 128 * c + 128)
                pe.matmul(bank[:, :], w1_hi[:, e, at], hs_hi[:, :], start=True, stop=False)
                pe.matmul(bank[:, :], w1_hi[:, e, at], hs_lo[:, :], start=False, stop=False)
                did(pe.matmul(bank[:, :], w1_lo[:, e, at], hs_hi[:, :], start=False, stop=True), "a_hid_mm")

            def second(g, e):
                need(pe, "a_lo", g, FC * (e + 1))
                need(pe, "a_y", g, e - 1)
                for b in range(G):
                    for c in range(FC):
                        part = [hid[:, k, e % 2, c, b * S:(b + 1) * S] for k in range(2)]
                        pe.matmul(bank4(5 + e % 2)[:, b, :], part[0], w2_hi[:, e, c, :], start=(c == 0), stop=False)
                        pe.matmul(bank4(5 + e % 2)[:, b, :], part[0], w2_lo[:, e, c, :], start=False, stop=False)
                        last = pe.matmul(bank4(5 + e % 2)[:, b, :], part[1], w2_hi[:, e, c, :], start=False, stop=(c == FC - 1))
                did(last, "a_y_mm")

            def layer0(g, more):
                for e in range(E):
                    if e + 1 < E:
                        for c in range(FC):
                            first(g, FC * (e + 1) + c)
                    elif more:
                        logits(g + 1)
                        for c in range(FC):
                            first(g + 1, c)
                    if e == 1:
                        need(pe, "a_gate", g)
                        for b in range(G):
                            last = pe.transpose(banks[1][0:E, b * S:(b + 1) * S], gate[:, b, :], mat("ident"))
                        did(last, "a_gT")
                    if e == 2:
                        need(pe, "a_gateT", g)
                        for b in range(G):
                            last = pe.matmul(bank4(1)[:, b, :], gateT[:, b, :], mat("exp_b2", p=E), start=True, stop=True)
                        did(last, "a_b2")
                    second(g, e)
                    if not more:
                        if e == 1:
                            need(pe, "a_hid", g, FC)
                            turned_x(0)
                        if e == 2:
                            differentiated(0)
                        if e == 3:
                            right_side(0)
                        if e == 6:
                            need(pe, "b_f1r", 0)
                            need(pe, "b_xn2", 0)
                            turned(7, xn2, "b_xn2T")
                        if e == 7:
                            key(0)
                    if more and e == 3:
                        transposes(g + 1)

            transposes(0)
            pe.matmul(banks[3][0:A, B:2 * B], mat("expert_b", p=ED), onehot_v[:, :], start=True, stop=False)
            pe.matmul(banks[3][0:A, B:2 * B], mat("domain_emb", p=ED), onehot[0:ED, 1, :], start=False, stop=True).then_inc(once["esel"], 1)
            for o in range(A):
                last = pe.matmul(banks[6 + o // (A // 2)][0:A, o % (A // 2) * B:(o % (A // 2) + 1) * B], expert_w[:, o, :], onehot_v[:, :],
                                 start=True, stop=True)
            last.then_inc(once["wsel_mm"], 1)
            pe.wait_ge(once["silu"], 1)
            for k in range(2):
                last = pe.matmul(banks[5][:, B * k:B * k + B], mat("W_ada", k), ang[:, 4, :], start=True, stop=True)
            last.then_inc(once["ada"], 1)
            pe.wait_ge(once["wsel"], 1)
            logits(0)
            pe.wait_ge(once["w1_hi"], 1)
            pe.wait_ge(once["w1_lo"], 1)
            for i in range(FC):
                first(0, i)
            pe.wait_ge(once["w2_hi"], 1)
            pe.wait_ge(once["w2_lo"], 1)
            with pe.Fori(0, NG - 1) as g:
                layer0(g, True)

            def scores(i, b, r):
                if b == 0 and r == 0:
                    need(pe, "b_qT", i)
                if b == 0:
                    need(pe, "b_kh", i, r + 1)
                need(pe, "c_sc", i, (b - 1) * QB + r + 1)
                quad = banks[r][:, :].rearrange("p (h k) -> p h k", h=HQ)
                did(pe.matmul(quad, qT[:, b, :], kh[:, HQ * r:HQ * r + HQ, b, :], start=True, stop=True), "c_s_mm")

            def probs_T(i, b, r):
                if r == 0:
                    need(pe, "c_exp", i, b + 1)
                need(pe, "c_pT", i, b * QB + r - 1)
                for h in range(HQ):
                    last = pe.transpose(banks[4 + r % 2][:, h * S:(h + 1) * S], sc[:, b % 2, HQ * r + h, :], mat("ident"))
                did(last, "c_pT_mm")

            def values(i, b, r):
                need(pe, "c_pT", i, b * QB + r + 1)
                if r == 0:
                    need(pe, "c_cxT", i, b)
                if b == 0 and r == 0:
                    need(pe, "b_vh", i)
                for h in range(HQ * r, HQ * r + HQ):
                    last = pe.matmul(banks[6][:, h * (HD + 1):(h + 1) * (HD + 1)], pT[:, h, :], vh[:, b, h, :], start=True, stop=True)
                if r == QB - 1:
                    did(last, "c_ctx_mm")

            def context_T(i, b):
                need(pe, "c_cx", i, b + 1)
                did(pe.transpose(banks[6][:, 0:S], cx[:, :, :].rearrange("p h d -> p (h d)"), mat("ident")), "c_cxT_mm")

            def turned(bank, src, name):
                for b in range(G):
                    last = pe.transpose(bank4(bank)[:, b, :], src[:, b, :], mat("ident"))
                did(last, name)

            x_flat = xT[:, :, :].rearrange("p b s -> p (b s)")

            def turned_x(g):
                need(pe, "b_v", g - 1)
                need(pe, "b_f0", g)
                turned(7, f0, "b_f0T")

            def differentiated(g):
                need(pe, "b_prodT", g)
                for b in range(G):
                    last = pe.matmul(bank4(7)[:, b, :], b2fT[:, b, :], mat("gradT"), start=True, stop=True)
                did(last, "b_t1")

            def right_side(g):
                need(pe, "b_b0f", g)
                need(pe, "b_mix", g)
                pe.matmul(banks[7][:, :], mat("hgrad2T"), b0f[:, :, :].rearrange("p b d -> p (b d)"), start=True, stop=False, skip_group_check=True)
                for b in range(G):
                    pe.matmul(bank4(7)[:, b, :], a1fT[:, b, :], mat("ngradT"), start=False, stop=False, skip_group_check=True)
                    pe.matmul(bank4(7)[:, b, :], b1fT[:, b, :], mat("hgrad2T"), start=False, stop=False, skip_group_check=True)
                did(pe.matmul(banks[7][:, :], mat("gradT"), mix[:, :, :].rearrange("p b d -> p (b d)"), start=False, stop=True, skip_group_check=True), "b_df")

            def key(g):
                need(pe, "b_xT", g)
                did(pe.matmul(banks[7][:, :], mat("Wk"), x_flat, start=True, stop=True), "b_k_mm")

            def query(g):
                did(pe.matmul(banks[4][:, :], mat("Wq"), x_flat, start=True, stop=True), "b_q_mm")

            def value(g):
                need(pe, "b_kT", g)
                for b in range(G):
                    last = pe.matmul(bank4(7)[:, b, :], xT[:, b, :], mat("Wv"), start=True, stop=True)
                did(last, "b_v_mm")

            def passes(i, att, prev, tail, pre):
                for r in range(QB):
                    if prev:
                        if tail and r < 2:
                            need(pe, "b_hid2", i - 2, FC - 1 + r)
                        if att and r == 0:
                            need(pe, "b_qT", i)
                        probs_T(i - 1, 2, r)
                    if att:
                        scores(i, 0, r)
                    if prev and r:
                        values(i - 1, 2, r - 1)
                if pre:
                    turned_x(i + 1)
                if tail:
                    need(pe, "b_hid2", i - 2, FC)
                    if prev:
                        need(pe, "c_pT", i - 1, 3 * QB)
                    for b in range(G):
                        for c in range(FC):
                            last = pe.matmul(bank4(5)[:, b, :], hid2[:, c, b * S:(b + 1) * S], mat("W2", c), start=(c == 0), stop=(c == FC - 1))
                    did(last, "b_ff_mm")
                if prev:
                    values(i - 1, 2, QB - 1)
                    if pre:
                        differentiated(i + 1)
                if tail:
                    need(pe, "b_x3", i - 2)
                    turned(5, x3, "b_x3T_mm")
                if prev:
                    context_T(i - 1, 2)
                for r in range(QB):
                    if prev:
                        if tail and r == 1:
                            need(pe, "b_x3T", i - 2)
                        probs_T(i - 1, 3, r)
                    if att:
                        scores(i, 1, r)
                    if prev and r:
                        values(i - 1, 3, r - 1)
                if pre:
                    if not prev:
                        differentiated(i + 1)
                    right_side(i + 1)
                if tail:
                    need(pe, "b_x3T", i - 2)
                    if prev:
                        need(pe, "c_pT", i - 1, 4 * QB)
                    did(pe.matmul(banks[5][0:A, :], mat("downT"), x3T[:, :], start=True, stop=True), "b_down_mm")
                if prev:
                    values(i - 1, 3, QB - 1)
                if tail:
                    need(pe, "b_hd", i - 2)
                    need(pe, "b_wc", i - 2)
                    pe.nop(nofuse=True)
                    for b in range(G):
                        last = pe.matmul(banks[5][0:A, b * S:(b + 1) * S], wc[:, b, :], hd[:, b, :], start=True, stop=True)
                    did(last, "b_exp_mm")
                if prev:
                    context_T(i - 1, 3)
                if att:
                    for r in range(QB):
                        if tail and r == 1:
                            need(pe, "b_h3", i - 2)
                        probs_T(i, 0, r)
                        scores(i, 2, r)
                        if r:
                            values(i, 0, r - 1)
                if prev:
                    need(pe, "c_cxT", i - 1, G)
                    need(pe, "b_xbT", i - 1)
                    if pre:
                        need(pe, "b_f1r", i + 1)
                    elif att:
                        need(pe, "b_v", i)
                    else:
                        need(pe, "b_x2", i - 2)
                    for b in range(G):
                        pe.matmul(bank4(7)[:, b, :], cxT[:, b, :], mat("Wo"), start=True, stop=False)
                        last = pe.matmul(bank4(7)[:, b, :], xbT[:, b, :], mat("ident"), start=False, stop=True)
                    did(last, "b_x2_mm")
                if tail:
                    need(pe, "b_h3", i - 2)
                    if att:
                        need(pe, "c_pT", i, QB)
                    for b in range(G):
                        last = pe.matmul(bank4(5)[:, b, :], h3[:, b, :], mat("upT", p=A + 1), start=True, stop=True)
                    did(last, "b_up_mm")
                if att:
                    values(i, 0, QB - 1)
                if pre:
                    need(pe, "b_xn2", i + 1)
                    if prev:
                        need(pe, "b_x2", i - 1)
                    else:
                        need(pe, "b_f1r", i + 1)
                    turned(7, xn2, "b_xn2T")
                if att and prev:
                    context_T(i, 0)
                if att:
                    for r in range(QB):
                        if tail and r == 1:
                            need(pe, "b_x4", i - 2)
                        probs_T(i, 1, r)
                        scores(i, 3, r)
                        if not prev and r == 0:
                            context_T(i, 0)
                        if r:
                            values(i, 1, r - 1)
                if prev:
                    need(pe, "b_xn3", i - 1)
                    if att:
                        need(pe, "c_pT", i, 2 * QB)
                    elif tail:
                        need(pe, "b_x4", i - 2)
                    turned(5, xn3, "b_xn3T")
                if pre:
                    key(i + 1)
                    if att:
                        need(pe, "c_pT", i, 2 * QB)
                    query(i + 1)
                if att:
                    values(i, 1, QB - 1)
                if prev:
                    need(pe, "b_h2T", i - 1)
                    if pre:
                        need(pe, "b_qT", i + 1)
                for c in range(FC):
                    if prev:
                        need(pe, "b_hid2", i - 1, c - 1)
                        did(pe.matmul(banks[4 + c % 2][:, :], mat("W1", c), h2T[:, :], start=True, stop=True), "b_ff1_mm")
                    if pre and c == 1:
                        value(i + 1)
                if att:
                    context_T(i, 1)

            layer0(NG - 1, False)
            need(pe, "a_y", NG, 0)
            query(0)
            value(0)
            pipeline(pe, passes)


def kernel(**inputs):
    from concourse import bacc
    from concourse.bass_utils import run_bass_kernel_spmd

    x = {k: np.asarray(v) for k, v in inputs.items()}
    grad = np.zeros((128, 128), np.float32)
    grad2 = np.zeros((128, 128), np.float32)
    for i in range(1, 127):
        grad[i, i - 1], grad[i, i + 1] = -0.5, 0.5
        grad2[i, i - 1], grad2[i, i], grad2[i, i + 1] = 1.0, -2.0, 1.0
    grad[0, 0:3] = -1.5, 2.0, -0.5
    grad[127, 125:128] = 0.5, -2.0, 1.5
    grad2[0, 0:4] = 2.0, -5.0, 4.0, -1.0
    grad2[127, 124:128] = -1.0, 4.0, -5.0, 2.0
    half = D // 2
    freq = np.exp(np.arange(half, dtype=np.float32) * np.float32(-math.log(10000.0) / (half - 1)))
    head = (np.arange(128)[:, None] // HD == np.arange(H)[None, :]).astype(np.float32)

    def padded(a):
        a = a.reshape(a.shape[0], -1)
        full = np.zeros((128, a.shape[1]), np.float32)
        full[:a.shape[0]] = a
        return full

    vectors = {
        "ln_g": x["L0_cond_ln_g"], "ln_b": x["L0_cond_ln_b"], "hyp_b1": x["L0_cond_hyp_b1"], "hyp_b2": x["L0_cond_hyp_b2"],
        "sty_b1": x["L0_cond_sty_b1"], "gamma_b": x["L0_cond_sty_b2"][:D], "beta_b": x["L0_cond_sty_b2"][D:],
        "scale_b": x["L2_cond_b_ada"][:D], "shift_b": x["L2_cond_b_ada"][D:], "bq": x["L2_cond_bq"], "bk": x["L2_cond_bk"],
        "bo": x["L2_cond_bo"], "g2": x["L2_cond_g2"], "beta2": x["L2_cond_beta2"], "down_b": x["L3_cond_down_b"],
        "ff_b1": x["L2_cond_b1"].reshape(FC, 128).T, "exp_b1": x["L0_cond_exp_b1"].reshape(E * FC, 128).T,
        "head": head, "freq": np.tile(freq, 2), "turn": np.repeat(np.float32([0.0, 0.25]), half),
        "row": np.arange(128, dtype=np.float32), "count": np.tile(np.arange(ED, dtype=np.float32), (128, 1)),
    }
    matrices = {
        "ident": np.eye(128, dtype=np.float32), "gradT": grad.T, "ngradT": -grad.T, "hgrad2T": 0.5 * grad2.T,
        "A0": x["L1_cond_A_grid"][0], "B0": x["L1_cond_B_grid"][0], "A1T": x["L1_cond_A_grid"][1].T,
        "B1T": x["L1_cond_B_grid"][1].T, "B2T": x["L1_cond_B_grid"][2].T, "subj": x["L0_cond_subj_emb"],
        "hyp_w1": x["L0_cond_hyp_w1"], "hyp_w2": x["L0_cond_hyp_w2"], "sty_w1": x["L0_cond_sty_w1"],
        "sty_w2": x["L0_cond_sty_w2"], "W_ada": x["L2_cond_W_ada"], "router": x["L0_cond_router_w"],
        "Wq": x["L2_cond_Wq"], "Wk": x["L2_cond_Wk"], "Wv": x["L2_cond_Wv"], "Wo": x["L2_cond_Wo"], "W1": x["L2_cond_W1"],
        "W2": x["L2_cond_W2"].reshape(FC, 128, D).transpose(1, 0, 2), "downT": x["L3_cond_down_W"].T,
        "upT": np.concatenate([x["L3_cond_up_W"].T, x["L3_cond_up_b"][None]]), "expert_b": x["L3_cond_expert_b"],
        "domain_emb": x["L3_cond_domain_emb"], "exp_b2": x["L0_cond_exp_b2"],
    }
    arrays = {
        "cols": np.concatenate([padded(vectors[n]) for n in COLS], axis=1),
        "mats": np.concatenate([padded(matrices[n]) for n in MATS], axis=1),
        "ids": np.concatenate([x["itok_B_6_14"], x["itok_B_34_63"], x["itok_B_0_15"]]),
        "dt": x["condB_dt"],
        "rows": np.concatenate([x["L2_cond_bv"], x["L2_cond_b2"], x["L3_cond_ln_gamma"], x["L3_cond_ln_beta"]]),
        "expert_w": x["L3_cond_expert_W"], "x": x["x"], "w1": x["L0_cond_exp_w1"],
        "w2": x["L0_cond_exp_w2"], "mask": x["mask_Bx1xSxS_bk0"], "bias": x["fside_Bx16xSxS_0"],
    }
    nc = bacc.Bacc("TRN2", target_bir_lowering=False, num_devices=1)
    arrays = {"in_" + n: np.ascontiguousarray(a) for n, a in arrays.items()}
    tensors = {n[3:]: nc.dram_tensor(n, a.shape, mybir.dt.from_np(a.dtype), kind="ExternalInput").ap() for n, a in arrays.items()}
    out = nc.dram_tensor("out", (B, S, D), F32, kind="ExternalOutput").ap()
    build(nc, tensors, out)
    return run_bass_kernel_spmd(nc, [arrays], core_ids=[0]).results[0]["out"]
```
